# Optimizing a Trainium2 kernel written in Bass

```python
import numpy as np
import jax
import jax.numpy as jnp

def _softmax(x, axis=-1):
    return jax.nn.softmax(x, axis=axis)

def _gelu(x):
    return jax.nn.gelu(x, approximate=True)

def _silu(x):
    return jax.nn.silu(x)

def _sigmoid(x):
    return jax.nn.sigmoid(x)

def _layernorm(x, axis=-1, eps=1e-05):
    m = jnp.mean(x, axis=axis, keepdims=True)
    v = jnp.var(x, axis=axis, keepdims=True)
    return (x - m) / jnp.sqrt(v + eps)

def _scatter_add(tgt, idx, src, axis=0):
    return tgt.at[idx].add(src)

def _segment_sum(src, seg, n):
    return jax.ops.segment_sum(src, seg, n)
kernel_name = 'mk_gnn_preln_d4_gnn_r16_8eb32e'

def setup_inputs(seed: int=0):
    np.random.seed(seed)
    _w = jnp.asarray

    def _rec_inputs():
        import jax
        import jax.numpy as jnp
        _gk = jax.random.key(seed)
        x = -8.776e-05 + 1 * jax.random.normal(jax.random.fold_in(_gk, 1), (3125, 256), jnp.float32)
        _s = jax.random.randint(jax.random.fold_in(_gk, 2), (50000,), 0, 3125, jnp.int32)
        _d = jax.random.randint(jax.random.fold_in(_gk, 3), (50000,), 0, 3125, jnp.int32)
        _loop = jnp.arange(3125, dtype=jnp.int32)
        src = jnp.concatenate([_s, _d, _loop])
        dst = jnp.concatenate([_d, _s, _loop])
        _o = jnp.argsort(dst, stable=True)
        src = src[_o]
        dst = dst[_o]
        edge_type_64 = jax.random.randint(jax.random.fold_in(_gk, 13), (103125,), 0, 64, jnp.int32)
        edge_type_8 = jax.random.randint(jax.random.fold_in(_gk, 14), (103125,), 0, 8, jnp.int32)
        node_type_4 = jax.random.randint(jax.random.fold_in(_gk, 15), (3125,), 0, 4, jnp.int32)
        return (x, src, dst, edge_type_64, edge_type_8, node_type_4)
    x, src, dst, edge_type_64, edge_type_8, node_type_4 = _rec_inputs()

    def _L0_gnn_setup():
        import jax, jax.numpy as jnp
        import numpy as np
        N_NODES = 1250
        N_EDGES = 20000
        IN_DIM = 256
        OUT_DIM = 256
        N_HEADS = 4
        D_K = OUT_DIM // N_HEADS
        N_NTYPES = 4
        N_RELS = 8
        SQRT_DK = float(np.sqrt(D_K))

        def _typed_matmul(x, W, node_type):
            all_t = jnp.einsum('ni,tio->tno', x, W)
            return all_t[node_type, jnp.arange(x.shape[0])]
        key = jax.random.key(seed)
        ks = jax.random.split(key, 12)
        xav = lambda k, shape, fan: jax.random.normal(k, shape, jnp.float32) * (1.0 / np.sqrt(fan))
        return {'h': jax.random.normal(ks[0], (N_NODES, IN_DIM), jnp.float32), 'k_linears': xav(ks[1], (N_NTYPES, IN_DIM, OUT_DIM), IN_DIM), 'q_linears': xav(ks[2], (N_NTYPES, IN_DIM, OUT_DIM), IN_DIM), 'v_linears': xav(ks[3], (N_NTYPES, IN_DIM, OUT_DIM), IN_DIM), 'a_linears': xav(ks[4], (N_NTYPES, OUT_DIM, OUT_DIM), OUT_DIM), 'relation_att': xav(ks[5], (N_RELS, N_HEADS, D_K, D_K), D_K), 'relation_msg': xav(ks[6], (N_RELS, N_HEADS, D_K, D_K), D_K), 'relation_pri': jnp.ones((N_RELS, N_HEADS), jnp.float32), 'skip': jnp.ones((N_NTYPES,), jnp.float32), 'node_type': jax.random.randint(ks[7], (N_NODES,), 0, N_NTYPES), 'etype': jnp.sort(jax.random.randint(ks[8], (N_EDGES,), 0, N_RELS)), 'row_idx': jax.random.randint(ks[9], (N_EDGES,), 0, N_NODES), 'col_idx': jax.random.randint(ks[10], (N_EDGES,), 0, N_NODES)}
    _L0_gnn_all = _L0_gnn_setup()
    _L0_gnn_in = {k: v for k, v in _L0_gnn_all.items() if k in ('k_linears', 'q_linears', 'v_linears', 'a_linears', 'relation_att', 'relation_msg', 'relation_pri', 'skip')}
    del _L0_gnn_all

    def _L1_gnn_setup():
        import jax, jax.numpy as jnp
        import numpy as np
        N, IN_CH, HEADS, OUT_CH, E = (3125, 256, 4, 64, 50000)
        key = jax.random.key(seed)
        k1, k2, k3, k4, k5 = jax.random.split(key, 5)
        x = jax.random.normal(k1, (N, IN_CH), dtype=jnp.float32)
        edge_index = jax.random.randint(k2, (2, E), 0, N, dtype=jnp.int64)
        bw = float(np.sqrt(6.0 / (IN_CH + HEADS * OUT_CH)))
        ba = float(np.sqrt(6.0 / (HEADS + OUT_CH)))
        weight = jax.random.uniform(k3, (IN_CH, HEADS * OUT_CH), jnp.float32, -bw, bw)
        attn_l = jax.random.uniform(k4, (HEADS, OUT_CH), jnp.float32, -ba, ba)
        attn_r = jax.random.uniform(k5, (HEADS, OUT_CH), jnp.float32, -ba, ba)
        return {'x': x, 'edge_index': edge_index, 'weight': weight, 'attn_l': attn_l, 'attn_r': attn_r}
    _L1_gnn_all = _L1_gnn_setup()
    _L1_gnn_in = {k: v for k, v in _L1_gnn_all.items() if k in ('weight', 'attn_l', 'attn_r')}
    del _L1_gnn_all

    def _L2_gnn_setup():
        import jax, jax.numpy as jnp
        import numpy as np
        N_NODES = 1024
        N_EDGES = 16384
        D_IN = 256
        D = 256
        H = 512
        E = 64
        TOP_K = 2
        CAP = 1024
        BN_EPS = 1e-05

        def _moe_ff(x, Wg, bg, w1, b1, w2, b2):
            N = x.shape[0]
            logits = x @ Wg + bg
            vals, idx = jax.lax.top_k(logits, TOP_K)
            gates = jax.nn.softmax(vals, axis=-1)
            e_flat = idx.reshape(-1)
            g_flat = gates.reshape(-1)
            tok = jnp.arange(N * TOP_K) // TOP_K
            order = jnp.argsort(e_flat)
            e_s, tok_s, g_s = (e_flat[order], tok[order], g_flat[order])
            counts = jnp.bincount(e_flat, length=E)
            offs = jnp.concatenate([jnp.zeros((1,), counts.dtype), jnp.cumsum(counts)[:-1]])
            rank = jnp.arange(N * TOP_K) - offs[e_s]
            valid = rank < CAP
            slot = jnp.where(valid, e_s * CAP + rank, E * CAP)
            buf = jnp.zeros((E * CAP + 1, D), x.dtype).at[slot].set(x[tok_s])
            h = buf[:E * CAP].reshape(E, CAP, D)
            h1 = jax.nn.gelu(jnp.einsum('ecd,edh->ech', h, w1) + b1[:, None, :], approximate=False)
            h2 = jnp.einsum('ech,ehd->ecd', h1, w2) + b2[:, None, :]
            out_buf = h2.reshape(E * CAP, D)
            y_s = jnp.where(valid[:, None], out_buf[jnp.minimum(slot, E * CAP - 1)], 0.0)
            return jnp.zeros((N, D), x.dtype).at[tok_s].add(g_s[:, None] * y_s)

        def _forward(feats, W_gc, b_gc, W_res, b_res, Wg, bg, w1, b1, w2, b2, gamma, beta, src, dst):
            n = feats.shape[0]
            ones = jnp.ones((src.shape[0],), feats.dtype)
            deg_out = jnp.clip(jax.ops.segment_sum(ones, src, num_segments=n), 1.0)
            deg_in = jnp.clip(jax.ops.segment_sum(ones, dst, num_segments=n), 1.0)
            h = feats * jax.lax.rsqrt(deg_out)[:, None]
            m = jax.ops.segment_sum(h[src], dst, num_segments=n) * jax.lax.rsqrt(deg_in)[:, None]
            gc = m @ W_gc + b_gc
            x = gc + (feats @ W_res + b_res)
            core = _moe_ff(x, Wg, bg, w1, b1, w2, b2)
            y = x + core
            mean = jnp.mean(y, axis=0)
            var = jnp.mean((y - mean) ** 2, axis=0)
            return (y - mean) * jax.lax.rsqrt(var + BN_EPS) * gamma + beta
        key = jax.random.key(seed)
        ks = jax.random.split(key, 16)
        s = lambda d: 1.0 / np.sqrt(d)
        inp = {'feats': jax.random.normal(ks[0], (N_NODES, D_IN), jnp.float32), 'W_gc': jax.random.normal(ks[1], (D_IN, D), jnp.float32) * s(D_IN), 'b_gc': jnp.zeros((D,), jnp.float32), 'W_res': jax.random.normal(ks[2], (D_IN, D), jnp.float32) * s(D_IN), 'b_res': jnp.zeros((D,), jnp.float32), 'Wg': jax.random.normal(ks[3], (D, E), jnp.float32) * s(D), 'bg': jnp.zeros((E,), jnp.float32), 'w1': jax.random.normal(ks[4], (E, D, H), jnp.float32) * s(D), 'b1': jnp.zeros((E, H), jnp.float32), 'w2': jax.random.normal(ks[5], (E, H, D), jnp.float32) * s(H), 'b2': jnp.zeros((E, D), jnp.float32), 'gamma': jnp.ones((D,), jnp.float32), 'beta': jnp.zeros((D,), jnp.float32), 'src': jax.random.randint(ks[6], (N_EDGES,), 0, N_NODES), 'dst': jax.random.randint(ks[7], (N_EDGES,), 0, N_NODES)}
        return inp
    _L2_gnn_all = _L2_gnn_setup()
    _L2_gnn_in = {k: v for k, v in _L2_gnn_all.items() if k in ('W_gc', 'b_gc', 'W_res', 'b_res', 'Wg', 'bg', 'w1', 'b1', 'w2', 'b2', 'gamma', 'beta')}
    del _L2_gnn_all

    def _L3_gnn_setup():
        import jax, jax.numpy as jnp
        import numpy as np
        N_NODES = 3125
        N_EDGES = 31250
        IN_DIM = 256
        HID = 64
        HEADS = 4
        N_REL = 64
        key = jax.random.key(seed)
        ks = jax.random.split(key, 16)
        s = 0.02
        return {'node_features': jax.random.normal(ks[0], (N_NODES, IN_DIM), jnp.float32), 'edge_index': jax.random.randint(ks[1], (2, N_EDGES), 0, N_NODES, jnp.int32), 'edge_relations': jax.random.randint(ks[2], (N_EDGES,), 0, N_REL, jnp.int32), 'query_emb': jax.random.normal(ks[3], (IN_DIM,), jnp.float32), 'Wq': jax.random.normal(ks[4], (IN_DIM, HID * HEADS), jnp.float32) * s, 'bq': jnp.zeros((HID * HEADS,), jnp.float32), 'Wk': jax.random.normal(ks[5], (IN_DIM, HID * HEADS), jnp.float32) * s, 'bk': jnp.zeros((HID * HEADS,), jnp.float32), 'Wv': jax.random.normal(ks[6], (IN_DIM, HID * HEADS), jnp.float32) * s, 'bv': jnp.zeros((HID * HEADS,), jnp.float32), 'rel_w': jax.random.normal(ks[7], (N_REL, HID), jnp.float32) * s, 'Wo': jax.random.normal(ks[8], (HID * HEADS, IN_DIM), jnp.float32) * s, 'bo': jnp.zeros((IN_DIM,), jnp.float32), 'gamma': jnp.ones((IN_DIM,), jnp.float32), 'beta': jnp.zeros((IN_DIM,), jnp.float32)}
    _L3_gnn_all = _L3_gnn_setup()
    _L3_gnn_in = {k: v for k, v in _L3_gnn_all.items() if k in ('query_emb', 'Wq', 'bq', 'Wk', 'bk', 'Wv', 'bv', 'rel_w', 'Wo', 'bo', 'gamma', 'beta')}
    del _L3_gnn_all
    return {'x': x, 'src': src, 'dst': dst, 'edge_type_64': edge_type_64, 'edge_type_8': edge_type_8, 'node_type_4': node_type_4, 'L0_gnn_k_linears': _L0_gnn_in['k_linears'], 'L0_gnn_q_linears': _L0_gnn_in['q_linears'], 'L0_gnn_v_linears': _L0_gnn_in['v_linears'], 'L0_gnn_a_linears': _L0_gnn_in['a_linears'], 'L0_gnn_relation_att': _L0_gnn_in['relation_att'], 'L0_gnn_relation_msg': _L0_gnn_in['relation_msg'], 'L0_gnn_relation_pri': _L0_gnn_in['relation_pri'], 'L0_gnn_skip': _L0_gnn_in['skip'], 'L1_gnn_weight': _L1_gnn_in['weight'], 'L1_gnn_attn_l': _L1_gnn_in['attn_l'], 'L1_gnn_attn_r': _L1_gnn_in['attn_r'], 'L2_gnn_W_gc': _L2_gnn_in['W_gc'], 'L2_gnn_b_gc': _L2_gnn_in['b_gc'], 'L2_gnn_W_res': _L2_gnn_in['W_res'], 'L2_gnn_b_res': _L2_gnn_in['b_res'], 'L2_gnn_Wg': _L2_gnn_in['Wg'], 'L2_gnn_bg': _L2_gnn_in['bg'], 'L2_gnn_w1': _L2_gnn_in['w1'], 'L2_gnn_b1': _L2_gnn_in['b1'], 'L2_gnn_w2': _L2_gnn_in['w2'], 'L2_gnn_b2': _L2_gnn_in['b2'], 'L2_gnn_gamma': _L2_gnn_in['gamma'], 'L2_gnn_beta': _L2_gnn_in['beta'], 'L3_gnn_query_emb': _L3_gnn_in['query_emb'], 'L3_gnn_Wq': _L3_gnn_in['Wq'], 'L3_gnn_bq': _L3_gnn_in['bq'], 'L3_gnn_Wk': _L3_gnn_in['Wk'], 'L3_gnn_bk': _L3_gnn_in['bk'], 'L3_gnn_Wv': _L3_gnn_in['Wv'], 'L3_gnn_bv': _L3_gnn_in['bv'], 'L3_gnn_rel_w': _L3_gnn_in['rel_w'], 'L3_gnn_Wo': _L3_gnn_in['Wo'], 'L3_gnn_bo': _L3_gnn_in['bo'], 'L3_gnn_gamma': _L3_gnn_in['gamma'], 'L3_gnn_beta': _L3_gnn_in['beta']}

def reference(x, src, dst, edge_type_64, edge_type_8, node_type_4, L0_gnn_k_linears, L0_gnn_q_linears, L0_gnn_v_linears, L0_gnn_a_linears, L0_gnn_relation_att, L0_gnn_relation_msg, L0_gnn_relation_pri, L0_gnn_skip, L1_gnn_weight, L1_gnn_attn_l, L1_gnn_attn_r, L2_gnn_W_gc, L2_gnn_b_gc, L2_gnn_W_res, L2_gnn_b_res, L2_gnn_Wg, L2_gnn_bg, L2_gnn_w1, L2_gnn_b1, L2_gnn_w2, L2_gnn_b2, L2_gnn_gamma, L2_gnn_beta, L3_gnn_query_emb, L3_gnn_Wq, L3_gnn_bq, L3_gnn_Wk, L3_gnn_bk, L3_gnn_Wv, L3_gnn_bv, L3_gnn_rel_w, L3_gnn_Wo, L3_gnn_bo, L3_gnn_gamma, L3_gnn_beta):
    import jax
    import jax.numpy as jnp

    def _L0_gnn_ref(h, k_linears, q_linears, v_linears, a_linears, relation_att, relation_msg, relation_pri, skip, node_type, etype, row_idx, col_idx):
        import jax, jax.numpy as jnp
        import numpy as np
        N_NODES = 1250
        N_EDGES = 20000
        IN_DIM = 256
        OUT_DIM = 256
        N_HEADS = 4
        D_K = OUT_DIM // N_HEADS
        N_NTYPES = 4
        N_RELS = 8
        SQRT_DK = float(np.sqrt(D_K))

        def _typed_matmul(x, W, node_type):
            all_t = jnp.einsum('ni,tio->tno', x, W)
            return all_t[node_type, jnp.arange(x.shape[0])]
        n = h.shape[0]
        k = _typed_matmul(h, k_linears, node_type).reshape(n, N_HEADS, D_K)
        q = _typed_matmul(h, q_linears, node_type).reshape(n, N_HEADS, D_K)
        v = _typed_matmul(h, v_linears, node_type).reshape(n, N_HEADS, D_K)
        q_att = jnp.einsum('nhd,rhde->rnhe', q, relation_att)
        v_msg = jnp.einsum('nhd,rhde->rnhe', v, relation_msg)
        aw_q_edge = q_att[etype, col_idx]
        msg_edge = v_msg[etype, row_idx]
        attn_score = jnp.sum(aw_q_edge * k[row_idx], axis=-1)
        score = attn_score * (relation_pri[etype] / SQRT_DK)
        m = jax.ops.segment_max(score, col_idx, num_segments=n)
        ex = jnp.exp(score - m[col_idx])
        denom = jax.ops.segment_sum(ex, col_idx, num_segments=n)
        alpha = ex / denom[col_idx]
        agg = jax.ops.segment_sum(alpha[..., None] * msg_edge, col_idx, num_segments=n)
        agg = agg.reshape(n, OUT_DIM)
        out = _typed_matmul(agg, a_linears, node_type)
        out = jax.nn.sigmoid(skip)[node_type][:, None] * out
        return out

    def _L1_gnn_ref(x, edge_index, weight, attn_l, attn_r):
        import jax, jax.numpy as jnp
        import numpy as np
        N, IN_CH, HEADS, OUT_CH, E = (3125, 256, 4, 64, 50000)
        heads, out_ch = attn_l.shape
        n = x.shape[0]
        xt = jnp.matmul(x, weight).reshape(-1, heads, out_ch)
        row, col = (edge_index[0], edge_index[1])
        alpha_l = jnp.einsum('ehd,hd->eh', xt[row], attn_l)
        alpha_r = jnp.einsum('ehd,hd->eh', xt[col], attn_r)
        alpha = jax.nn.softmax(jax.nn.leaky_relu(alpha_l + alpha_r, 0.01), axis=1)
        tmp = jnp.einsum('nh,nhd->nd', alpha[:n], xt[col[:n]])
        out = jnp.broadcast_to(tmp[:, None, :], (n, heads, out_ch))
        return out.reshape(n, heads * out_ch)

    def _L2_gnn_ref(feats, W_gc, b_gc, W_res, b_res, Wg, bg, w1, b1, w2, b2, gamma, beta, src, dst):
        import jax, jax.numpy as jnp
        import numpy as np
        N_NODES = 1024
        N_EDGES = 16384
        D_IN = 256
        D = 256
        H = 512
        E = 64
        TOP_K = 2
        CAP = 1024
        BN_EPS = 1e-05

        def _moe_ff(x, Wg, bg, w1, b1, w2, b2):
            N = x.shape[0]
            logits = x @ Wg + bg
            vals, idx = jax.lax.top_k(logits, TOP_K)
            gates = jax.nn.softmax(vals, axis=-1)
            e_flat = idx.reshape(-1)
            g_flat = gates.reshape(-1)
            tok = jnp.arange(N * TOP_K) // TOP_K
            order = jnp.argsort(e_flat)
            e_s, tok_s, g_s = (e_flat[order], tok[order], g_flat[order])
            counts = jnp.bincount(e_flat, length=E)
            offs = jnp.concatenate([jnp.zeros((1,), counts.dtype), jnp.cumsum(counts)[:-1]])
            rank = jnp.arange(N * TOP_K) - offs[e_s]
            valid = rank < CAP
            slot = jnp.where(valid, e_s * CAP + rank, E * CAP)
            buf = jnp.zeros((E * CAP + 1, D), x.dtype).at[slot].set(x[tok_s])
            h = buf[:E * CAP].reshape(E, CAP, D)
            h1 = jax.nn.gelu(jnp.einsum('ecd,edh->ech', h, w1) + b1[:, None, :], approximate=False)
            h2 = jnp.einsum('ech,ehd->ecd', h1, w2) + b2[:, None, :]
            out_buf = h2.reshape(E * CAP, D)
            y_s = jnp.where(valid[:, None], out_buf[jnp.minimum(slot, E * CAP - 1)], 0.0)
            return jnp.zeros((N, D), x.dtype).at[tok_s].add(g_s[:, None] * y_s)

        def _forward(feats, W_gc, b_gc, W_res, b_res, Wg, bg, w1, b1, w2, b2, gamma, beta, src, dst):
            n = feats.shape[0]
            ones = jnp.ones((src.shape[0],), feats.dtype)
            deg_out = jnp.clip(jax.ops.segment_sum(ones, src, num_segments=n), 1.0)
            deg_in = jnp.clip(jax.ops.segment_sum(ones, dst, num_segments=n), 1.0)
            h = feats * jax.lax.rsqrt(deg_out)[:, None]
            m = jax.ops.segment_sum(h[src], dst, num_segments=n) * jax.lax.rsqrt(deg_in)[:, None]
            gc = m @ W_gc + b_gc
            x = gc + (feats @ W_res + b_res)
            core = _moe_ff(x, Wg, bg, w1, b1, w2, b2)
            y = x + core
            mean = jnp.mean(y, axis=0)
            var = jnp.mean((y - mean) ** 2, axis=0)
            return (y - mean) * jax.lax.rsqrt(var + BN_EPS) * gamma + beta
        return _forward(feats, W_gc, b_gc, W_res, b_res, Wg, bg, w1, b1, w2, b2, gamma, beta, src, dst)

    def _L3_gnn_ref(node_features, edge_index, edge_relations, query_emb, Wq, bq, Wk, bk, Wv, bv, rel_w, Wo, bo, gamma, beta):
        import jax, jax.numpy as jnp
        import numpy as np
        N_NODES = 3125
        N_EDGES = 31250
        IN_DIM = 256
        HID = 64
        HEADS = 4
        N_REL = 64
        N = node_features.shape[0]
        D = rel_w.shape[1]
        H = Wq.shape[1] // D
        enh = node_features + 0.1 * query_emb[None, :]
        Q = (enh @ Wq + bq).reshape(N, H, D)
        K = (enh @ Wk + bk).reshape(N, H, D)
        V = (enh @ Wv + bv).reshape(N, H, D)
        src, dst = (edge_index[0], edge_index[1])
        rel = rel_w[edge_relations]
        mod_k = K[src] + 0.2 * rel[:, None, :]
        scores = jnp.einsum('ehd,ehd->eh', Q[dst], mod_k) / D ** 0.5
        seg_max = jax.ops.segment_max(scores, dst, num_segments=N)
        ex = jnp.exp(scores - seg_max[dst])
        denom = jax.ops.segment_sum(ex, dst, num_segments=N)
        w = ex / denom[dst]
        agg = jax.ops.segment_sum(w[:, :, None] * V[src], dst, num_segments=N)
        deg = jax.ops.segment_sum(jnp.ones((src.shape[0],), jnp.float32), dst, num_segments=N)
        msgs = jnp.where(deg[:, None, None] > 0, agg, V)
        out = msgs.reshape(N, H * D) @ Wo + bo
        x = out + node_features
        mu = jnp.mean(x, axis=-1, keepdims=True)
        var = jnp.var(x, axis=-1, keepdims=True)
        return (x - mu) / jnp.sqrt(var + 1e-05) * gamma + beta
    edge_index = jnp.stack([src, dst])
    h = jnp.maximum(_layernorm(x, axis=-1), 0.0)
    x = x + _L0_gnn_ref(h, L0_gnn_k_linears, L0_gnn_q_linears, L0_gnn_v_linears, L0_gnn_a_linears, L0_gnn_relation_att, L0_gnn_relation_msg, L0_gnn_relation_pri, L0_gnn_skip, node_type_4, edge_type_8, src, dst)
    h = jnp.maximum(_layernorm(x, axis=-1), 0.0)
    x = x + _L1_gnn_ref(h, edge_index, L1_gnn_weight, L1_gnn_attn_l, L1_gnn_attn_r)
    h = jnp.maximum(_layernorm(x, axis=-1), 0.0)
    x = x + _L2_gnn_ref(h, L2_gnn_W_gc, L2_gnn_b_gc, L2_gnn_W_res, L2_gnn_b_res, L2_gnn_Wg, L2_gnn_bg, L2_gnn_w1, L2_gnn_b1, L2_gnn_w2, L2_gnn_b2, L2_gnn_gamma, L2_gnn_beta, src, dst)
    h = jnp.maximum(_layernorm(x, axis=-1), 0.0)
    x = x + _L3_gnn_ref(h, edge_index, edge_type_64, L3_gnn_query_emb, L3_gnn_Wq, L3_gnn_bq, L3_gnn_Wk, L3_gnn_bk, L3_gnn_Wv, L3_gnn_bv, L3_gnn_rel_w, L3_gnn_Wo, L3_gnn_bo, L3_gnn_gamma, L3_gnn_beta)
    return x

_drawn_inputs = setup_inputs


def setup_inputs(seed=0):
    import zlib

    import numpy as np

    out = dict(_drawn_inputs(seed))
    spreads = {'L0_gnn_relation_pri': (1.0, 0.2),
     'L0_gnn_skip': (1.0, 0.2),
     'L2_gnn_b_gc': (0.0, 0.1),
     'L2_gnn_b_res': (0.0, 0.1),
     'L2_gnn_bg': (0.0, 0.1),
     'L2_gnn_b1': (0.0, 0.1),
     'L2_gnn_b2': (0.0, 0.1),
     'L2_gnn_gamma': (1.0, 0.2),
     'L2_gnn_beta': (0.0, 0.1),
     'L3_gnn_bq': (0.0, 2.0),
     'L3_gnn_bk': (0.0, 2.0),
     'L3_gnn_bv': (0.0, 0.363),
     'L3_gnn_bo': (0.0, 0.1),
     'L3_gnn_gamma': (1.0, 0.2),
     'L3_gnn_beta': (0.0, 0.1)}
    factors = {'L3_gnn_query_emb': 8.0, 'L3_gnn_Wq': 8.0, 'L3_gnn_Wk': 8.0, 'L3_gnn_rel_w': 200.0}
    for name, (base, spread) in spreads.items():
        noise = np.random.default_rng([zlib.crc32(name.encode()), seed]).standard_normal(out[name].shape)
        drawn = base * np.exp(spread * noise) if base else spread * noise
        out[name] = jnp.asarray(drawn.astype(out[name].dtype))
    for name, factor in factors.items():
        out[name] = (out[name] * factor).astype(out[name].dtype)
    return out
```

```python
import concourse.bass as bass
from concourse import mybir
from contextlib import ExitStack, contextmanager

F32, BF16, I32, U32 = mybir.dt.float32, mybir.dt.bfloat16, mybir.dt.int32, mybir.dt.uint32
ALU, ACT, AX = mybir.AluOpType, mybir.ActivationFunctionType, mybir.AxisListType

P = 128
N, E, D = 3125, 103125, 256
H, DK = 4, 64
NT, R8, R64 = 4, 8, 64
NB = -(-N // P)
NBP = NB + 1
NP = NBP * P
G = 4
SL = 4
EW = P * G
EP = E + EW
NI = -(-(E // EW + NB + 1) // SL) * SL
EC = 125
ER = E // EC
PAD_DST = 4000.0
BIG = float(2 ** 100)
HV = DK + 1
EX, HID, CAP = 64, 512, 1024
NTILE = N * 2 // P + EX
SLOTS = NTILE * P
EPS = 1e-5


class Stage:

    def __init__(self, nc, name):
        self.nc, self.name, self.ctx, self.sems = nc, name, ExitStack(), []

    def sb(self, name, shape, dt=F32):
        return self.ctx.enter_context(self.nc.sbuf_tensor(f"{self.name}_{name}", shape, dt))

    def ps(self, name, shape, dt=F32):
        return self.ctx.enter_context(self.nc.psum_tensor(f"{self.name}_{name}", shape, dt))

    def sem(self, name):
        s = self.nc.alloc_semaphore(f"{self.name}_{name}")
        self.sems.append(s)
        return s

    def sems_of(self, name, k):
        return [self.sem(f"{name}{i}") for i in range(k)]

    def block(self):
        return self.blk.enter_context(self.nc.Block())

    def __enter__(self):
        self.ctx.__enter__()
        self.blk = ExitStack()
        return self

    def __exit__(self, *a):
        self.blk.close()
        self.nc.clear_and_free_semaphores(self.sems)
        self.nc.all_engine_barrier()
        return self.ctx.__exit__(*a)


def rows(t, start, count=P):
    return t[bass.ds(start, count), :]


def prepare(nc, A, T, K):
    with Stage(nc, "prep") as S:
        src = S.sb("src", [EC, ER], I32)
        dst = S.sb("dst", [EC, ER], I32)
        t8 = S.sb("t8", [EC, ER], I32)
        t64 = S.sb("t64", [EC, ER], I32)
        rec = S.sb("rec", [EC, ER, 4], I32)
        dstf = S.sb("dstf", [EC, ER])
        junk = S.sb("junk", [EC, ER])
        pad = S.sb("pad", [P, G * 4])
        zero = S.sb("zero", [P, D])
        nty = S.sb("nty", [P, NBP], I32)
        ntf = S.sb("ntf", [P, NBP])
        mask = S.sb("mask", [P, NBP, 2, NT])
        skip = S.sb("skip", [P, NT])
        sig = S.sb("sig", [P, NT])
        cnt = S.sb("cnt", [EC, NBP + 2])
        ones = S.sb("ones", [P, 1])
        off = S.sb("off", [NBP, 2])
        cb = S.sb("cb", [NBP, 1])
        NJ = E // EW + 2
        stepi = S.sb("stepi", [NBP, NJ])
        stepj = S.sb("stepj", [NBP, NJ])
        nit = S.sb("nit", [NBP, 1])
        lower = S.sb("lower", [NBP, NBP])
        istart = S.sb("istart", [NBP, 2])
        itn = S.sb("itn", [NBP, NI])
        sel = S.sb("sel", [NBP, 2, NI])
        val = S.sb("val", [NBP, 3, NI])
        bcol = S.sb("bcol", [NBP, 2])
        row = S.sb("row", [1, 3, NI])
        rowf = S.sb("rowf", [1, NI, 4])
        HG = 15
        lo = S.sb("lo", [EC, ER], I32)
        hi = S.sb("hi", [EC, ER], I32)
        lof = S.sb("lof", [EC, ER])
        hif = S.sb("hif", [EC, ER])
        ohl = S.sb("ohl", [EC, 2, HG, P], BF16)
        ohh = S.sb("ohh", [EC, 2, HG, NBP], BF16)
        dego = S.sb("dego", [P, NBP])
        zb = S.sb("zb", [1, P], BF16)
        pOff = S.ps("pOff", [P, 512])
        pVal = [S.ps(f"pVal{j}", [P, 512]) for j in range(3)]
        pDeg = S.ps("pDeg", [P, 512])
        edges_in, nodes_in, skip_in = S.sem("edges_in"), S.sem("nodes_in"), S.sem("skip_in")
        padded, rec_built = S.sem("padded"), S.sem("rec_built")
        stored, mask_built, sig_done = S.sem("stored"), S.sem("mask_built"), S.sem("sig_done")
        consts, cnt_built, off_ps, nit_built, ist_ps = (S.sem(x) for x in ("consts", "cnt_built", "off_ps", "nit_built", "ist_ps"))
        val_built, val_ps, rows_built = S.sem("val_built"), S.sem("val_ps"), S.sem("rows_built")
        oh_built, oh_used, deg_ps, deg_clip, deg_root, deg_built = (
            S.sems_of("oh_built", 2), S.sems_of("oh_used", 2), S.sem("deg_ps"), S.sem("deg_clip"), S.sem("deg_root"), S.sem("deg_built"))
        HK = ER // HG
        block = S.block()

        @block.sync
        def _(sp):
            for t, a in ((src, A["src"]), (dst, A["dst"]), (t8, A["edge_type_8"]), (t64, A["edge_type_64"])):
                sp.dma_start(t[:, :], a.rearrange("(p t) -> p t", p=EC)).then_inc(edges_in, 16)
            sp.wait_ge(padded, 1)
            with nc.allow_non_contiguous_dma(reason="3125 node types, once"):
                sp.dma_start(nty[:, 0:NB - 1], A["node_type_4"][0:(NB - 1) * P].rearrange("(b p) -> p b", p=P)).then_inc(nodes_in, 16)
                sp.dma_start(nty[0:N - (NB - 1) * P, NB - 1:NB],
                             A["node_type_4"][(NB - 1) * P:N].rearrange("(p o) -> p o", o=1)).then_inc(nodes_in, 16)
            sp.dma_start(skip[:, :], A["L0_gnn_skip"].rearrange("(o t) -> o t", o=1).to_broadcast([P, NT])).then_inc(skip_in, 16)
            sp.dma_start(T["x0"][0:N, :], A["x"][:, :]).then_inc(stored, 16)
            sp.dma_start(T["x0"][N:N + P, :], zero[:, :]).then_inc(stored, 16)
            sp.dma_start(T["x0"][N + P:NP, :], zero[0:NP - N - P, :]).then_inc(stored, 16)
            sp.dma_start(T["rec"][E:EP, :].rearrange("(p g) c -> p (g c)", g=G), pad[:, :].bitcast(I32)).then_inc(stored, 16)
            sp.dma_start(T["xslot"].rearrange("(b p) n -> p b n", p=P), zero[:, :].unsqueeze(1).to_broadcast([P, NTILE + 1, D])).then_inc(stored, 16)
            sp.wait_ge(rec_built, 1)
            sp.dma_start(T["rec"][0:E, :].rearrange("(p t) c -> p (t c)", p=EC), rec[:, :, :].rearrange("p t c -> p (t c)")).then_inc(stored, 16)
            sp.wait_ge(mask_built, 1)
            with nc.allow_non_contiguous_dma(reason="node-type masks, once"):
                sp.dma_start(T["tmask"].rearrange("(b p) c -> p b c", p=P), mask[:, :, :, :].rearrange("p b k t -> p b (k t)")).then_inc(stored, 16)
            sp.wait_ge(rows_built, 1)
            sp.dma_start(T["itemf"].rearrange("(o i) c -> o (i c)", o=1), rowf[:, :, :].rearrange("o i c -> o (i c)")).then_inc(stored, 16)
            sp.wait_ge(deg_built, 1)
            with nc.allow_non_contiguous_dma(reason="3328 degrees, once"):
                sp.dma_start(T["rdego"].rearrange("(b p) c -> p (b c)", p=P), dego[:, :]).then_inc(stored, 16)
            sp.wait_ge(stored, 16 * 9)

        @block.gpsimd
        def _(pool):
            pool.memset(zero[:, :], 0.0)
            pool.memset(pad[:, :], 0.0)
            pool.drain()
            pool.memset(pad[:, :].rearrange("p (g c) -> p g c", c=4)[:, :, 2:3], PAD_DST)
            pool.memset(nty[:, :], -1)
            pool.drain().then_inc(padded, 1)
            pool.iota(stepi[:, :].bitcast(I32), pattern=[[EW, NJ]], base=0, channel_multiplier=0)
            pool.iota(itn[:, :].bitcast(I32), pattern=[[1, NI]], base=0, channel_multiplier=0)
            pool.iota(bcol[:, 0:1].bitcast(I32), pattern=[[0, 1]], base=0, channel_multiplier=P)
            pool.memset(ones[:, :], 1.0)
            pool.memset(lower[:, :], 1.0)
            pool.memset(K["ident"][:, :], 0.0)
            pool.memset(K["ones"][:, :], 1.0)
            pool.memset(K["upper"][:, :], 1.0)
            pool.iota(K["iota"][:, :].bitcast(I32), pattern=[[1, P]], base=0, channel_multiplier=0)
            pool.memset(K["eps"][:, :], EPS)
            pool.drain()
            pool.affine_select(out=lower[:, :], in_=lower[:, :], compare_op=ALU.is_gt, fill=0.0, base=0, pattern=[[1, NBP]], channel_multiplier=-1)
            pool.affine_select(out=K["upper"][:, :], in_=K["upper"][:, :], compare_op=ALU.is_gt, fill=0.0, base=0, pattern=[[1, P]], channel_multiplier=-1)
            pool.affine_select(out=K["ident"][:, :], in_=K["ident"][:, :], compare_op=ALU.not_equal, fill=1.0, base=0, pattern=[[-1, P]], channel_multiplier=1)
            pool.drain().then_inc(consts, 1)

        @block.scalar
        def _(act):
            act.wait_ge(skip_in, 16)
            act.activation(sig[:, :], skip[:, :], ACT.Sigmoid).then_inc(sig_done, 1)
            act.wait_ge(deg_clip, 1)
            act.activation(dego[:, :], dego[:, :], ACT.Sqrt).then_inc(deg_root, 1)

        @block.tensor
        def _(pe):
            pe.wait_ge(consts, 1)
            pe.wait_ge(cnt_built, 1)
            pe.matmul(pOff[0:NBP, 0:1], cnt[:, 0:NBP], ones[0:EC, :], start=True, stop=True)
            pe.matmul(pOff[0:NBP, 1:2], cnt[:, 1:NBP + 1], ones[0:EC, :], start=True, stop=True).then_inc(off_ps, 1)
            pe.wait_ge(nit_built, 1)
            pe.matmul(pOff[0:NBP, 2:3], lower[:, :], nit[:, :], start=True, stop=True).then_inc(ist_ps, 1)
            pe.wait_ge(val_built, 1)
            for j in range(3):
                last = pe.matmul(pVal[j][0:1, 0:NI], ones[0:NBP, :], val[:, j, :], start=True, stop=True)
            last.then_inc(val_ps, 1)
            pe.matmul(pDeg[:, 0:NBP], zb[:, :], zb[:, 0:NBP], start=True, stop=False)

            def degrees(u, n):
                pe.wait_ge(oh_built[u], n)
                for k in range(HG):
                    last = pe.matmul(pDeg[:, 0:NBP], ohl[:, u, k, :], ohh[:, u, k, :], start=False, stop=False)
                last.then_inc(oh_used[u], 1)

            with pe.Fori(0, HK // 2) as i:
                n = pe.snap(i + 1)
                degrees(0, n)
                degrees(1, n)
            degrees(0, HK // 2 + 1)
            pe.matmul(pDeg[:, 0:NBP], zb[:, :], zb[:, 0:NBP], start=False, stop=True).then_inc(deg_ps, 1)

        @block.vector
        def _(dve):
            dve.memset(zb[:, :], 0.0)
            dve.wait_ge(edges_in, 64)
            recf = rec[:, :, :].bitcast(F32)
            dve.scalar_tensor_tensor(out=rec[:, :, 0], in0=src[:, :], scalar=float(R8), in1=t8[:, :], op0=ALU.mult, op1=ALU.add)
            dve.tensor_copy(rec[:, :, 1], src[:, :])
            dve.tensor_copy(recf[:, :, 2], dst[:, :])
            dve.tensor_copy(recf[:, :, 3], t64[:, :]).then_inc(rec_built, 1)
            dve.tensor_copy(dstf[:, :], dst[:, :])
            dve.drain()
            for b in range(NBP + 1):
                dve.tensor_scalar(junk[:, :], dstf[:, :], float(b * P), 0.0, ALU.is_lt, ALU.add, accum_out=cnt[:, b:b + 1])
                dve.drain()
            dve.sem_inc(cnt_built, 1)
            dve.wait_ge(nodes_in, 32)
            dve.tensor_copy(ntf[:, :], nty[:, :])
            dve.drain()
            for t in range(NT):
                dve.tensor_scalar(mask[:, :, 0, t], ntf[:, :], float(t), None, ALU.is_equal)
            dve.wait_ge(sig_done, 1)
            dve.drain()
            dve.tensor_tensor(mask[:, :, 1, :], mask[:, :, 0, :], sig[:, :].unsqueeze(1).to_broadcast([P, NBP, NT]), ALU.mult).then_inc(mask_built, 1)
            dve.wait_ge(consts, 1)
            dve.wait_ge(off_ps, 1)
            dve.tensor_copy(off[:, :], pOff[0:NBP, 0:2])
            dve.tensor_copy(stepj[:, :], stepi[:, :].bitcast(I32))
            dve.tensor_copy(bcol[:, 1:2], bcol[:, 0:1].bitcast(I32))
            dve.tensor_copy(K["iota"][:, :], K["iota"][:, :].bitcast(I32))
            dve.tensor_copy(sel[:, 0, :], itn[:, :].bitcast(I32))
            dve.drain()
            dve.tensor_copy(itn[:, :], sel[:, 0, :])
            dve.tensor_tensor(cb[:, :], off[:, 1:2], off[:, 0:1], ALU.subtract)
            dve.drain()
            dve.tensor_scalar(stepj[:, :], stepj[:, :], cb[:, 0:1], 0.0, ALU.is_lt, ALU.add, accum_out=nit[:, 0:1])
            dve.drain()
            dve.tensor_scalar(nit[:, :], nit[:, :], 1.0, None, ALU.max)
            dve.drain().then_inc(nit_built, 1)
            dve.wait_ge(ist_ps, 1)
            dve.tensor_copy(istart[:, 0:1], pOff[0:NBP, 2:3])
            dve.drain()
            dve.tensor_scalar(istart[:, 1:2], bcol[:, 1:2], float(NB * P), float(NI + 1), ALU.is_ge, ALU.mult)
            dve.drain()
            dve.tensor_tensor(istart[:, 1:2], istart[:, 1:2], istart[:, 0:1], ALU.add)
            dve.drain()
            dve.tensor_tensor(istart[:, 1:2], istart[:, 1:2], nit[:, 0:1], ALU.add)
            dve.drain()
            dve.tensor_scalar(sel[:, 0, :], itn[:, :], istart[:, 0:1], None, ALU.is_ge)
            dve.tensor_scalar(sel[:, 1, :], itn[:, :], istart[:, 1:2], None, ALU.is_lt)
            dve.tensor_scalar(val[:, 0, :], itn[:, :], istart[:, 0:1], float(EW), ALU.subtract, ALU.mult)
            dve.tensor_scalar(val[:, 2, :], itn[:, :], istart[:, 0:1], None, ALU.is_gt)
            dve.drain()
            dve.tensor_tensor(sel[:, 0, :], sel[:, 0, :], sel[:, 1, :], ALU.mult)
            dve.tensor_scalar(val[:, 0, :], val[:, 0, :], off[:, 0:1], float(E), ALU.add, ALU.min)
            dve.drain()
            dve.tensor_tensor(val[:, 0, :], val[:, 0, :], sel[:, 0, :], ALU.mult)
            dve.tensor_scalar(val[:, 1, :], sel[:, 0, :], bcol[:, 1:2], None, ALU.mult)
            dve.tensor_tensor(val[:, 2, :], val[:, 2, :], sel[:, 0, :], ALU.mult)
            dve.drain().then_inc(val_built, 1)
            dve.wait_ge(val_ps, 1)
            for j in range(3):
                dve.tensor_copy(row[:, j, :], pVal[j][0:1, 0:NI])
            dve.drain()
            dve.tensor_copy(K["items"][0:1, 0, :], row[:, 0, :])
            dve.tensor_copy(K["items"][0:1, 1, :], row[:, 1, :])
            dve.tensor_copy(rowf[:, :, 0], row[:, 1, :])
            dve.tensor_copy(rowf[:, :, 1], row[:, 2, :])
            dve.tensor_scalar(rowf[:, :, 2], row[:, 2, :], 1.0, BIG, ALU.subtract, ALU.mult)
            dve.tensor_copy(rowf[:, :, 3], row[:, 2, :])
            dve.drain().then_inc(rows_built, 1)
            dve.tensor_scalar(lo[:, :], src[:, :], P - 1, None, ALU.bitwise_and)
            dve.tensor_scalar(hi[:, :], src[:, :], 7, None, ALU.logical_shift_right)
            dve.drain()
            dve.tensor_copy(lof[:, :], lo[:, :])
            dve.tensor_copy(hif[:, :], hi[:, :])
            dve.drain()

            def onehots(u, c0, free, n):
                if free is not None:
                    dve.wait_ge(oh_used[u], free)
                for out, w, v in ((ohl, P, lof), (ohh, NBP, hif)):
                    last = dve.tensor_tensor(out[:, u, :, :], K["iota"][0:EC, 0:w].unsqueeze(1).to_broadcast([EC, HG, w]),
                                             v[:, bass.ds(c0, HG)].unsqueeze(2).to_broadcast([EC, HG, w]), ALU.is_equal)
                last.then_inc(oh_built[u], 1)

            onehots(0, 0, None, 1)
            onehots(1, HG, None, 1)
            with dve.Fori(1, HK // 2) as i:
                n = dve.snap(i)
                onehots(0, i * (2 * HG), n, None)
                onehots(1, i * (2 * HG) + HG, n, None)
            onehots(0, (HK - 1) * HG, HK // 2, None)
            dve.wait_ge(deg_ps, 1)
            dve.tensor_scalar(dego[:, :], pDeg[:, 0:NBP], 1.0, None, ALU.max).then_inc(deg_clip, 1)
            dve.wait_ge(deg_root, 1)
            dve.reciprocal(dego[:, :], dego[:, :]).then_inc(deg_built, 1)


def at_least(eng, sem, count):
    if not isinstance(count, int) or count > 0:
        eng.wait_ge(sem, count)


def repeat(eng, times, body):
    body(0)
    with eng.Fori(1, times) as i:
        body(i)


def snap(eng, v):
    return v if isinstance(v, int) else eng.snap(v)


def normalise(nc, dve, x, stats, mv, out, var_ready, root_ready, n):
    dve.bn_stats(stats, x)
    dve.drain()
    dve.bn_aggr(mv[:, 0:2], stats).then_inc(var_ready, 1)
    dve.wait_ge(root_ready, n)
    dve.reciprocal(mv[:, 2:3], mv[:, 2:3])
    dve.drain()
    dve.tensor_scalar(out, x, mv[:, 0:1], mv[:, 2:3], ALU.subtract, ALU.mult)
    dve.drain()


def root(nc, act, mv, eps, var_ready, root_ready, n):
    act.wait_ge(var_ready, n)
    act.activation(mv[:, 2:3], mv[:, 1:2], ACT.Sqrt, bias=eps[:, 0:1]).then_inc(root_ready, 1)


def layer0_nodes(nc, A, T, K):
    with Stage(nc, "l0n") as S:
        wq, wk, wv = (S.sb(f"w{c}", [P, NT, 2, D]) for c in "qkv")
        ra = S.sb("ra", [DK, 2, R8, 2, DK])
        rk = S.sb("rk", [P, 2, R8, DK])
        rv = S.sb("rv", [P, 2, R8, DK])
        pri = S.sb("pri", [P, 2, R8])
        x = S.sb("x", [P, 2, D])
        mk = S.sb("mk", [P, 2, 2 * NT])
        st = S.sb("st", [P, 2, 6])
        mv = S.sb("mv", [P, 2, 4])
        h = S.sb("h", [P, 2, D])
        hm = S.sb("hm", [P, 2, NT, D])
        hT = S.sb("hT", [P, 2, NT * 2, P])
        qs = S.sb("qs", [P, 2, D])
        kv = S.sb("kv", [P, 2, 4, P])
        tab = S.sb("tab", [P, 2, R8, 2, D])
        pT = S.ps("pT", [P, NT * 2, P])
        pQ = S.ps("pQ", [P, 512])
        pKV = S.ps("pKV", [P, 4, P])
        pB = [S.ps(f"pB{j}", [P, R8, DK]) for j in range(4)]
        w_in, ra_in, rk_ps, rk_done = S.sem("w_in"), S.sem("ra_in"), S.sem("rk_ps"), S.sem("rk_done")
        x_in, x_used = S.sems_of("x_in", 2), S.sems_of("x_used", 2)
        var_ready, root_ready = S.sems_of("var_ready", 2), S.sems_of("root_ready", 2)
        hm_ready, t_ps, hT_ready, qkv_ps, kv_ready = (S.sems_of(k, 2) for k in ("hm_ready", "t_ps", "hT_ready", "qkv_ps", "kv_ready"))
        big_ps, big_out, tab_ready, tab_out = S.sem("big_ps"), S.sem("big_out"), S.sems_of("tab_ready", 2), S.sems_of("tab_out", 2)
        block = S.block()

        @block.sync
        def _(sp):
            for hh in range(2):
                for j in range(2):
                    sp.dma_start(ra[:, j, :, hh, :], A["L0_gnn_relation_att"][:, 2 * j + hh, :, :].rearrange("r d e -> d r e")).then_inc(ra_in, 16)
                    sp.dma_start(rv[hh * DK:(hh + 1) * DK, j, :, :],
                                 A["L0_gnn_relation_msg"][:, 2 * j + hh, :, :].rearrange("r d e -> d r e")).then_inc(ra_in, 16)
                    with nc.allow_non_contiguous_dma(reason="8 x 4 numbers"):
                        sp.dma_start(pri[hh * DK:(hh + 1) * DK, j, :],
                                     A["L0_gnn_relation_pri"][:, 2 * j + hh].rearrange("(o r) -> o r", o=1).to_broadcast([DK, R8])).then_inc(ra_in, 16)
            for w, a in ((wq, "q"), (wk, "k"), (wv, "v")):
                sp.dma_start(w[:, :, :, :].rearrange("p t c n -> p (t c) n"),
                             A[f"L0_gnn_{a}_linears"].rearrange("t (c p) n -> p (t c) n", p=P)).then_inc(w_in, 16)

            def step(i):
                n = snap(sp, i + 1)
                for u in range(2):
                    at_least(sp, x_used[u], i)
                    r = snap(sp, (2 * i + u) * P)
                    sp.dma_start(x[:, u, :], rows(T["x0"], r)).then_inc(x_in[u], 16)
                    sp.dma_start(mk[:, u, :], rows(T["tmask"], r)).then_inc(x_in[u], 16)
                for u in range(2):
                    r = snap(sp, (2 * i + u) * P)
                    sp.wait_ge(tab_ready[u], n)
                    sp.dma_start(rows(T["q0"], r), qs[:, u, :]).then_inc(tab_out[u], 16)
                    sp.dma_start(rows(T["table0"].rearrange("(n r) c -> n (r c)", r=R8), r),
                                 tab[:, u, :, :, :].rearrange("p r k c -> p (r k c)")).then_inc(tab_out[u], 16)

            repeat(sp, NBP // 2, step)
            for u in range(2):
                sp.wait_ge(tab_out[u], 32 * (NBP // 2))

        @block.vector
        def _(dve):
            dve.wait_ge(ra_in, 16 * 12)
            dve.tensor_scalar(pri[:, :, :], pri[:, :, :], DK ** -0.5, None, ALU.mult)
            dve.drain()
            for j in range(2):
                dve.wait_ge(rk_ps, j + 1)
                last = dve.tensor_tensor(rk[:, j, :, :], pB[j][:, :, :], pri[:, j, :].unsqueeze(2).to_broadcast([P, R8, DK]), ALU.mult)
                last.then_inc(rk_done, 1)

            def step(i):
                n, n32 = snap(dve, i + 1), snap(dve, (i + 1) * 32)
                for u in range(2):
                    dve.wait_ge(x_in[u], n32)
                    normalise(nc, dve, x[:, u, :], st[:, u, :], mv[:, u, :], h[:, u, :], var_ready[u], root_ready[u], n)
                    at_least(dve, t_ps[u], i)
                    for t in range(NT):
                        last = dve.tensor_scalar(hm[:, u, t, :], h[:, u, :], 0.0, mk[:, u, t:t + 1], ALU.max, ALU.mult)
                    last.then_inc(hm_ready[u], 1)
                    dve.drain().then_inc(x_used[u], 1)

            repeat(dve, NBP // 2, step)

        @block.tensor
        def _(pe):
            pe.wait_ge(ra_in, 16 * 12)
            for j in range(2):
                for r in range(R8):
                    last = pe.transpose(pB[j][:, r, :], ra[:, j, r, :, :].rearrange("p a e -> p (a e)"), K["ident"][0:DK, 0:DK])
                last.then_inc(rk_ps, 1)
            pe.wait_ge(w_in, 48)
            pe.wait_ge(rk_done, 2)

            def step(i):
                n = snap(pe, i + 1)
                for u in range(2):
                    pe.wait_ge(hm_ready[u], n)
                    for c in range(2 * NT):
                        last = pe.transpose(pT[:, c, :], hm[:, u, c // 2, (c % 2) * P:(c % 2 + 1) * P], K["ident"][:, :])
                    last.then_inc(t_ps[u], 1)
                    pe.wait_ge(hT_ready[u], n)
                    for c in range(2 * NT):
                        pe.matmul(pQ[:, 0:D], hT[:, u, c, :], wq[:, c // 2, c % 2, :], start=(c == 0), stop=(c == 2 * NT - 1))
                    for o, w in ((0, wk), (2, wv)):
                        for j in range(2):
                            for c in range(2 * NT):
                                last = pe.matmul(pKV[:, o + j, :], w[:, c // 2, c % 2, j * P:(j + 1) * P], hT[:, u, c, :],
                                                 start=(c == 0), stop=(c == 2 * NT - 1))
                    last.then_inc(qkv_ps[u], 1)
                    pe.wait_ge(kv_ready[u], n)
                    for c in range(8):
                        k, j, hh = c // 4, c // 2 % 2, c % 2
                        at_least(pe, big_out, snap(pe, (2 * i + u) * 8 + c - 3))
                        pe.matmul(pB[c % 4][:, :, :].rearrange("p r d -> p (r d)"), kv[hh * DK:(hh + 1) * DK, u, 2 * k + j, :],
                                  (rk, rv)[k][hh * DK:(hh + 1) * DK, j, :, :].rearrange("p r d -> p (r d)"), start=True, stop=True).then_inc(big_ps, 1)

            repeat(pe, NBP // 2, step)

        @block.scalar
        def _(act):
            def step(i):
                n = snap(act, i + 1)
                for u in range(2):
                    root(nc, act, mv[:, u, :], K["eps"], var_ready[u], root_ready[u], n)
                for u in range(2):
                    act.wait_ge(t_ps[u], n)
                    act.activation(hT[:, u, :, :], pT[:, :, :], ACT.Copy).then_inc(hT_ready[u], 1)
                    at_least(act, tab_out[u], snap(act, i * 32))
                    act.wait_ge(qkv_ps[u], n)
                    act.activation(qs[:, u, :], pQ[:, 0:D], ACT.Copy)
                    act.activation(kv[:, u, :, :], pKV[:, :, :], ACT.Copy).then_inc(kv_ready[u], 1)
                    for c in range(8):
                        k, hd = c // 4, c % 4
                        act.wait_ge(big_ps, snap(act, (2 * i + u) * 8 + c + 1))
                        act.activation(tab[:, u, :, k, hd * DK:(hd + 1) * DK], pB[c % 4][:, :, :], ACT.Copy).then_inc(big_out, 1)
                    act.wait_ge(big_out, snap(act, (2 * i + u) * 8 + 8))
                    act.sem_inc(tab_ready[u], 1)

            repeat(act, NBP // 2, step)


def attention_items(nc, name, table, ridx, q, agg, T, K, rel=None):
    with Stage(nc, name) as S:
        rec = S.sb("rec", [P, SL, G, 4], I32)
        itf = S.sb("itf", [P, SL, 4])
        qb = S.sb("qb", [P, SL, D])
        kv = S.sb("kv", [P, SL, G, 2 * D])
        dl = S.sb("dl", [P, SL, G, H])
        oh = S.sb("oh", [P, SL, G, P])
        ohT = S.sb("ohT", [P, SL, G, P])
        dT = S.sb("dT", [G * H, SL, P])
        pen = S.sb("pen", [G * H, SL, P + 1])
        prod = S.sb("prod", [P, G, D])
        sc = S.sb("sc", [P, SL, G, H])
        run = S.sb("run", [G * H, P])
        fl = S.sb("fl", [G * H, SL, 2, P])
        flT = S.sb("flT", [P, 2, G, H])
        crow = S.sb("crow", [1, G, 2, H])
        miss = S.sb("miss", [P, G, H])
        cand = S.sb("cand", [P, SL, H, G + 1])
        mx = S.sb("mx", [P, SL, H])
        df = S.sb("df", [P, H])
        fac = S.sb("fac", [P, SL, H])
        z = S.sb("z", [P, G, H])
        vw = S.sb("vw", [P, SL, G, H, HV])
        part = S.sb("part", [P, H, HV])
        acc = S.sb("acc", [P, SL, H, HV])
        pOT = S.ps("pOT", [P, G, P])
        pQE = [S.ps(f"pQE{j}", [P, G, D]) for j in range(2)]
        pC = S.ps("pC", [P, 512])
        pS = pC[0:G * H, 0:P]
        pFL = pC[:, 256:256 + 2 * G * H].rearrange("p (k g h) -> p k g h", k=2, g=G)
        pM = pC[:, 320:320 + 2 * G * H].rearrange("p (g k h) -> p g k h", k=2, g=G)
        pSh = pC[:, 384:384 + G * H].rearrange("p (g h) -> p g h", g=G)
        pA = S.ps("pA", [P, 512])
        pD = pA[0:G * H, 384:384 + P]
        many = lambda k: S.sems_of(k, SL)
        in_ready, kv_ready, oh_ready, oh_ps, ohT_ready, qe_ps = (many(k) for k in ("in_ready", "kv_ready", "oh_ready", "oh_ps", "ohT_ready", "qe_ps"))
        dl_done, prod_done, sc_ready, s_ps, run_done, fl_ready, fl_ps, flT_ready = (
            many(k) for k in ("dl_done", "prod_done", "sc_ready", "s_ps", "run_done", "fl_ready", "fl_ps", "flT_ready"))
        pen_done, last_done, m_ps, miss_done, cand_done, mx_ready, sh_ps, df_ready, fac_ready, z_ready, w_ready, vw_ready, a_ps, part_done = (
            many(k) for k in ("pen_done", "last_done", "m_ps", "miss_done", "cand_done", "mx_ready", "sh_ps", "df_ready", "fac_ready", "z_ready", "w_ready",
                              "vw_ready", "a_ps", "part_done"))
        item_done, stored, consts, turn = many("item_done"), many("stored"), S.sem("consts"), S.sem("turn")
        if rel is not None:
            key_done = many("key_done")
            relw = S.sb("relw", [R64, DK])
            ohr = S.sb("ohr", [P, SL, G, R64])
            ohrT = S.sb("ohrT", [R64, SL, G, P])
            pRT = S.ps("pRT", [P, G, P])
            pR = pRT[:, 0:2, :].rearrange("p a (b d) -> p (a b) d", d=DK)
        block = S.block()
        KI = NI // SL

        def over_items(eng, step, first=0):
            for s in range(SL):
                step(s, 0, s, False)
            with eng.Fori(1, KI - 1) as k:
                kk = snap(eng, k + 0)
                for s in range(SL):
                    step(s, kk, k * SL + s, False)
            for s in range(SL):
                step(s, KI - 1, (KI - 1) * SL + s, s == SL - 1)

        def nxt(s, k):
            return ((s + 1) % SL, k + (s + 1) // SL)

        def prv(s, k):
            return ((s - 1) % SL, k - (s == 0))

        def need(eng, sems, s, k, per=1):
            at_least(eng, sems[s], snap(eng, (k + 1) * per))

        @block.sync
        def _(sp):
            if rel is not None:
                sp.dma_start(relw[:, :], rel[:, :]).then_inc(consts, 16)

            def load(s, k, i):
                e0 = sp.value_load(K["items"][0:1, 0, bass.ds(i, 1)], min_val=0, max_val=E)
                b0 = sp.value_load(K["items"][0:1, 1, bass.ds(i, 1)], min_val=0, max_val=NB * P)
                need(sp, item_done, s, k - 1)
                sp.sem_inc(turn, 1)
                sp.dma_start(rec[:, s, :, :].rearrange("p g c -> p (g c)"),
                             T["rec"][bass.ds(e0, EW), :].rearrange("(p g) c -> p (g c)", g=G)).then_inc(in_ready[s], 16)
                sp.dma_start(itf[:, s, :], T["itemf"][bass.ds(i, 1), :].to_broadcast([P, 4])).then_inc(in_ready[s], 16)
                sp.dma_start(qb[:, s, :], q[bass.ds(b0, P), :]).then_inc(in_ready[s], 16)

            for s in range(SL):
                load(s, 0, s)

            def step(s, k, i, last):
                b0 = sp.value_load(K["items"][0:1, 1, bass.ds(i, 1)], min_val=0, max_val=NB * P)
                ps, pk = prv(s, k)
                mine, before = snap(sp, k + 1), snap(sp, (pk + 1) * 16)
                at_least(sp, item_done[s], mine)
                sp.sem_inc(turn, 1)
                at_least(sp, stored[ps], before)
                sp.sem_inc(turn, 1)
                sp.dma_start(agg[bass.ds(b0, P), :], acc[:, s, :, :].rearrange("p h c -> p (h c)")).then_inc(stored[s], 16)
                if not (isinstance(k, int) and k == KI - 1):
                    load(s, k + 1, i + SL)

            over_items(sp, step)
            sp.wait_ge(stored[SL - 1], 16 * KI)

        @block.gpsimd
        def _(pool):
            pool.memset(pen[:, :, 0:1], -BIG)
            pool.memset(pen[:, :, P:P + 1], -BIG)
            pool.memset(crow[:, :, 0, :], 0.0)
            pool.memset(crow[:, :, 1, :], -1.0)
            pool.memset(acc[:, SL - 1, :, :], 0.0)
            pool.memset(mx[:, SL - 1, :], 0.0)
            pool.drain().then_inc(consts, 16)

            def step(s, k, i, last):
                need(pool, in_ready, s, k, 48)
                pool.sem_inc(turn, 1)
                for g in range(G):
                    pool.indirect_dma_start(kv[:, s, g, :], None, table[:, :],
                                            bass.IndirectOffsetOnAxis(ap=rec[:, s, g, ridx:ridx + 1], axis=0)).then_inc(kv_ready[s], 16)

            over_items(pool, step)

        @block.vector
        def _(dve):
            dve.wait_ge(consts, 16 + 16 * (rel is not None))

            def onehots(s, k):
                need(dve, in_ready, s, k, 48)
                recf = rec[:, s, :, :].bitcast(F32)
                dve.tensor_scalar(dl[:, s, :, :], recf[:, :, 2:3].to_broadcast([P, G, H]), itf[:, s, 0:1], None, ALU.subtract).then_inc(dl_done[s], 1)
                need(dve, dl_done, s, k)
                for g in range(G):
                    last = dve.tensor_scalar(oh[:, s, g, :], K["iota"][:, :], dl[:, s, g, 0:1], None, ALU.is_equal)
                if rel is not None:
                    for g in range(G):
                        last = dve.tensor_scalar(ohr[:, s, g, :], K["iota"][:, 0:R64], recf[:, g, 3:4], None, ALU.is_equal)
                last.then_inc(oh_ready[s], 1)

            def segments(s, k):
                need(dve, ohT_ready, s, k)
                dve.tensor_tensor(pen[:, s, 1:P], dT[:, s, 0:P - 1], dT[:, s, 1:P], ALU.subtract).then_inc(pen_done[s], 1)
                need(dve, pen_done, s, k)
                dve.tensor_scalar(fl[:, s, 1, :], pen[:, s, 1:P + 1], 0.0, None, ALU.is_lt).then_inc(last_done[s], 1)

            def scores(s, k):
                need(dve, kv_ready, s, k, 16 * G)
                need(dve, qe_ps, s, k)
                if rel is not None:
                    key = kv[:, s, :, 0:D].rearrange("p g (h d) -> p g h d", h=H)
                    dve.tensor_tensor(key, key, pR.unsqueeze(2).to_broadcast([P, G, H, DK]), ALU.add).then_inc(key_done[s], 1)
                    need(dve, key_done, s, k)
                dve.tensor_tensor(prod[:, :, :], pQE[s % 2][:, :, :], kv[:, s, :, 0:D], ALU.mult).then_inc(prod_done[s], 1)
                need(dve, prod_done, s, k)
                dve.tensor_reduce(sc[:, s, :, :], prod[:, :, :].rearrange("p g (h d) -> p g h d", h=H), AX.X, ALU.add).then_inc(sc_ready[s], 1)

            def run_max(s, k):
                need(dve, s_ps, s, k)
                need(dve, last_done, s, k)
                dve.tensor_tensor_scan(run[:, :], pen[:, s, 0:P], pS, 0.0, ALU.add, ALU.max).then_inc(run_done[s], 1)
                need(dve, run_done, s, k)
                dve.tensor_tensor(fl[:, s, 0, :], run[:, :], fl[:, s, 1, :], ALU.mult).then_inc(fl_ready[s], 1)

            def node_max(s, k):
                ps, pk = prv(s, k)
                dve.tensor_scalar(cand[:, s, :, G], mx[:, ps, :], itf[:, s, 1:2], itf[:, s, 2:3], ALU.mult, ALU.add)
                need(dve, m_ps, s, k)
                dve.tensor_scalar(miss[:, :, :], pM[:, :, 1, :], BIG, None, ALU.mult).then_inc(miss_done[s], 1)
                need(dve, miss_done, s, k)
                dve.tensor_tensor(cand[:, s, :, 0:G].rearrange("p h g -> p g h"), pM[:, :, 0, :], miss[:, :, :], ALU.add).then_inc(cand_done[s], 1)
                need(dve, cand_done, s, k)
                dve.tensor_reduce(mx[:, s, :], cand[:, s, :, :], AX.X, ALU.max).then_inc(mx_ready[s], 1)
                need(dve, mx_ready, s, k)
                dve.tensor_tensor(df[:, :], cand[:, s, :, G], mx[:, s, :], ALU.subtract).then_inc(df_ready[s], 1)

            def shifted(s, k):
                need(dve, sh_ps, s, k)
                dve.tensor_tensor(z[:, :, :], sc[:, s, :, :], pSh, ALU.subtract).then_inc(z_ready[s], 1)

            def weigh(s, k):
                need(dve, w_ready, s, k)
                dve.tensor_tensor(vw[:, s, :, :, 0:DK], kv[:, s, :, D:2 * D].rearrange("p g (h d) -> p g h d", h=H),
                                  vw[:, s, :, :, DK:HV].to_broadcast([P, G, H, DK]), ALU.mult).then_inc(vw_ready[s], 1)

            def merge(s, k):
                ps, pk = prv(s, k)
                need(dve, fac_ready, s, k)
                need(dve, item_done, ps, pk)
                dve.tensor_tensor(part[:, :, :], acc[:, ps, :, :], fac[:, s, :].unsqueeze(2).to_broadcast([P, H, HV]), ALU.mult).then_inc(part_done[s], 1)
                need(dve, part_done, s, k)
                need(dve, a_ps, s, k)
                need(dve, stored, s, k - 1, 16)
                dve.tensor_tensor(acc[:, s, :, :], part[:, :, :], pA[:, 0:H * HV].rearrange("p (h c) -> p h c", h=H), ALU.add).then_inc(item_done[s], 1)

            onehots(0, 0)
            segments(0, 0)
            scores(0, 0)

            def step(s, k, i, last):
                ns, nk = nxt(s, k)
                ps, pk = prv(s, k)
                if not (isinstance(pk, int) and pk < 0):
                    merge(ps, pk)
                run_max(s, k)
                if not last:
                    onehots(ns, nk)
                node_max(s, k)
                if not last:
                    segments(ns, nk)
                shifted(s, k)
                weigh(s, k)
                if not last:
                    scores(ns, nk)

            over_items(dve, step)
            merge(SL - 1, KI - 1)

        @block.tensor
        def _(pe):
            pe.wait_ge(consts, 16 + 16 * (rel is not None))

            def turn_onehots(s, k):
                need(pe, oh_ready, s, k)
                pe.transpose(pD, dl[:, s, :, :].rearrange("p g h -> p (g h)"), K["ident"][:, :])
                if rel is not None:
                    for g in range(G):
                        pe.transpose(pRT[0:R64, g, :], ohr[:, s, g, :], K["ident"][:, :])
                for g in range(G):
                    last = pe.transpose(pOT[:, g, :], oh[:, s, g, :], K["ident"][:, :])
                last.then_inc(oh_ps[s], 1)

            def queries(s, k, g0, g1):
                need(pe, ohT_ready, s, k)
                if rel is not None and g0 == 0:
                    for g in range(G):
                        pe.matmul(pR[:, g, :], ohrT[:, s, g, :], relw[:, :], start=True, stop=True)
                for g in range(g0, g1):
                    last = pe.matmul(pQE[s % 2][:, g, :], ohT[:, s, g, :], qb[:, s, :], start=True, stop=True)
                if g1 == G:
                    last.then_inc(qe_ps[s], 1)

            turn_onehots(0, 0)
            queries(0, 0, 0, G)

            def step(s, k, i, last):
                ns, nk = nxt(s, k)
                need(pe, sc_ready, s, k)
                pe.transpose(pS, sc[:, s, :, :].rearrange("p g h -> p (g h)"), K["ident"][:, :]).then_inc(s_ps[s], 1)
                need(pe, fl_ready, s, k)
                pe.sem_inc(turn, 1)
                for j in range(2):
                    lastm = pe.transpose(pFL[:, j, :, :].rearrange("p g h -> p (g h)"), fl[:, s, j, :], K["ident"][0:G * H, 0:G * H])
                lastm.then_inc(fl_ps[s], 1)
                if not last:
                    turn_onehots(ns, nk)
                need(pe, flT_ready, s, k)
                pe.matmul(pM.rearrange("p g k h -> p (g k h)"), K["ones"][0:1, :], crow[:, :, :, :].rearrange("p g k h -> p (g k h)"), start=True, stop=False)
                for g in range(G):
                    lastm = pe.matmul(pM[:, g, :, :], oh[:, s, g, :], flT[:, :, g, :], start=False, stop=(g == G - 1))
                lastm.then_inc(m_ps[s], 1)
                if not last:
                    queries(ns, nk, 0, 2)
                need(pe, mx_ready, s, k)
                for g in range(G):
                    lastm = pe.matmul(pSh[:, g, :], ohT[:, s, g, :], mx[:, s, :], start=True, stop=True)
                lastm.then_inc(sh_ps[s], 1)
                if not last:
                    queries(ns, nk, 2, G)
                need(pe, vw_ready, s, k)
                ps, pk = prv(s, k)
                need(pe, item_done, ps, pk)
                for g in range(G):
                    lastm = pe.matmul(pA[:, 0:H * HV], oh[:, s, g, :], vw[:, s, g, :, :].rearrange("p h c -> p (h c)"), start=(g == 0), stop=(g == G - 1))
                lastm.then_inc(a_ps[s], 1)

            over_items(pe, step)

        @block.scalar
        def _(act):
            def turned(s, k):
                need(act, oh_ps, s, k)
                if rel is not None:
                    act.activation(ohrT[:, s, :, :], pRT[0:R64, :, :], ACT.Copy)
                act.activation(dT[:, s, :], pD, ACT.Copy, scale=BIG)
                act.activation(ohT[:, s, :, :], pOT[:, :, :], ACT.Copy).then_inc(ohT_ready[s], 1)

            turned(0, 0)

            def step(s, k, i, last):
                ns, nk = nxt(s, k)
                need(act, fl_ps, s, k)
                act.activation(flT[:, :, :, :], pFL, ACT.Copy).then_inc(flT_ready[s], 1)
                if not last:
                    turned(ns, nk)
                need(act, df_ready, s, k)
                act.activation(fac[:, s, :], df[:, :], ACT.Exp).then_inc(fac_ready[s], 1)
                need(act, z_ready, s, k)
                act.activation(vw[:, s, :, :, DK:HV].rearrange("p g h o -> p g (h o)"), z[:, :, :], ACT.Exp).then_inc(w_ready[s], 1)

            over_items(act, step)


def layer1_nodes(nc, A, T, K):
    WX = D + 2 * H
    with Stage(nc, "l1n") as S:
        wa = S.sb("wa", [P, NT, 2, D])
        wx = S.sb("wx", [P, 2, WX])
        att = S.sb("att", [P, 2, D])
        wtmp = S.sb("wtmp", [P, 2, 2, D])
        ag = S.sb("ag", [P, 2, H, HV])
        x = S.sb("x", [P, 2, D])
        mk = S.sb("mk", [P, 2, 2 * NT])
        rden = S.sb("rden", [P, 2, H])
        coef = S.sb("coef", [P, 2, NT, H])
        am = S.sb("am", [P, 2, NT, H, DK])
        aT = S.sb("aT", [P, 2, NT * 2, P])
        x1 = S.sb("x1", [P, 2, D])
        st = S.sb("st", [P, 2, 6])
        mv = S.sb("mv", [P, 2, 4])
        h = S.sb("h", [P, 2, D])
        hT = S.sb("hT", [P, 2, 2, P])
        tb = S.sb("tb", [P, 2, WX])
        pT = S.ps("pT", [P, NT * 2, P])
        pO = [S.ps(f"pO{u}", [P, 512]) for u in range(2)]
        pH = S.ps("pH", [P, 4, P])
        pX = [S.ps(f"pX{u}", [P, 512]) for u in range(2)]
        w_in, wx_ready, turn = S.sem("w_in"), S.sem("wx_ready"), S.sem("turn")
        two = lambda k: S.sems_of(k, 2)
        x_in, x_used, am_ready, t_ps, aT_ready, o_ps, x1_ready = (two(k) for k in ("x_in", "x_used", "am_ready", "t_ps", "aT_ready", "o_ps", "x1_ready"))
        var_ready, root_ready, h_ready, h_ps, hT_ready, x_ps, tb_ready, stored = (
            two(k) for k in ("var_ready", "root_ready", "h_ready", "h_ps", "hT_ready", "x_ps", "tb_ready", "stored"))
        block = S.block()

        @block.sync
        def _(sp):
            sp.dma_start(wa[:, :, :, :].rearrange("p t c n -> p (t c) n"), A["L0_gnn_a_linears"].rearrange("t (c p) n -> p (t c) n", p=P)).then_inc(w_in, 16)
            sp.dma_start(wx[:, :, 0:D], A["L1_gnn_weight"].rearrange("(c p) n -> p c n", p=P)).then_inc(w_in, 16)
            for j, a in enumerate(("L1_gnn_attn_l", "L1_gnn_attn_r")):
                sp.dma_start(att[:, j, :], A[a].rearrange("(o h) d -> o (h d)", o=1).to_broadcast([P, D])).then_inc(w_in, 16)

            def step(i):
                n = snap(sp, i + 1)
                for u in range(2):
                    r = snap(sp, (2 * i + u) * P)
                    at_least(sp, x_used[u], i)
                    sp.sem_inc(turn, 1)
                    sp.dma_start(x[:, u, :], rows(T["x0"], r)).then_inc(x_in[u], 16)
                    sp.dma_start(mk[:, u, :], rows(T["tmask"], r)).then_inc(x_in[u], 16)
                    sp.dma_start(ag[:, u, :, :].rearrange("p h c -> p (h c)"), rows(T["agg0"], r)).then_inc(x_in[u], 16)
                for u in range(2):
                    r = snap(sp, (2 * i + u) * P)
                    sp.wait_ge(x1_ready[u], n)
                    sp.sem_inc(turn, 1)
                    sp.dma_start(rows(T["x1"], r), x1[:, u, :]).then_inc(stored[u], 16)
                for u in range(2):
                    r = snap(sp, (2 * i + u) * P)
                    sp.wait_ge(tb_ready[u], n)
                    sp.sem_inc(turn, 1)
                    sp.dma_start(rows(T["table1"], r), tb[:, u, :]).then_inc(stored[u], 16)
                    sp.dma_start(rows(T["tablel"], r), tb[:, u, D:D + H]).then_inc(stored[u], 16)

            repeat(sp, NBP // 2, step)
            for u in range(2):
                sp.wait_ge(stored[u], 48 * (NBP // 2))

        @block.vector
        def _(dve):
            dve.wait_ge(w_in, 64)
            for c in range(2):
                for j in range(2):
                    dve.tensor_tensor(wtmp[:, c, j, :], wx[:, c, 0:D], att[:, j, :], ALU.mult)
            dve.drain()
            for c in range(2):
                for j in range(2):
                    last = dve.tensor_reduce(wx[:, c, D + j * H:D + (j + 1) * H], wtmp[:, c, j, :].rearrange("p (h d) -> p h d", h=H), AX.X, ALU.add)
            last.then_inc(wx_ready, 1)

            def step(i):
                n, n48 = snap(dve, i + 1), snap(dve, (i + 1) * 48)
                for u in range(2):
                    dve.wait_ge(x_in[u], n48)
                    dve.tensor_scalar(rden[:, u, :], ag[:, u, :, DK], 1e-30, None, ALU.max)
                    dve.drain()
                    dve.reciprocal(rden[:, u, :], rden[:, u, :])
                    dve.drain()
                    dve.tensor_tensor(coef[:, u, :, :], rden[:, u, :].unsqueeze(1).to_broadcast([P, NT, H]),
                                      mk[:, u, NT:2 * NT].unsqueeze(2).to_broadcast([P, NT, H]), ALU.mult)
                    dve.drain()
                    dve.tensor_tensor(am[:, u, :, :, :], ag[:, u, :, 0:DK].unsqueeze(1).to_broadcast([P, NT, H, DK]),
                                      coef[:, u, :, :].unsqueeze(3).to_broadcast([P, NT, H, DK]), ALU.mult).then_inc(am_ready[u], 1)
                for u in range(2):
                    at_least(dve, stored[u], snap(dve, i * 48))
                    dve.wait_ge(o_ps[u], n)
                    dve.tensor_tensor(x1[:, u, :], x[:, u, :], pO[u][:, 0:D], ALU.add).then_inc(x1_ready[u], 1)
                    dve.drain().then_inc(x_used[u], 1)
                    normalise(nc, dve, x1[:, u, :], st[:, u, :], mv[:, u, :], h[:, u, :], var_ready[u], root_ready[u], n)
                    dve.tensor_scalar(h[:, u, :], h[:, u, :], 0.0, None, ALU.max).then_inc(h_ready[u], 1)

            repeat(dve, NBP // 2, step)

        @block.tensor
        def _(pe):
            pe.wait_ge(w_in, 64)
            pe.wait_ge(wx_ready, 1)

            def step(i):
                n = snap(pe, i + 1)
                for u in range(2):
                    pe.wait_ge(am_ready[u], n)
                    for c in range(2 * NT):
                        last = pe.transpose(pT[:, c, :], am[:, u, c // 2, 2 * (c % 2):2 * (c % 2) + 2, :].rearrange("p h d -> p (h d)"), K["ident"][:, :])
                    last.then_inc(t_ps[u], 1)
                    pe.wait_ge(aT_ready[u], n)
                    for c in range(2 * NT):
                        last = pe.matmul(pO[u][:, 0:D], aT[:, u, c, :], wa[:, c // 2, c % 2, :], start=(c == 0), stop=(c == 2 * NT - 1))
                    last.then_inc(o_ps[u], 1)
                for u in range(2):
                    pe.wait_ge(h_ready[u], n)
                    for c in range(2):
                        last = pe.transpose(pH[:, c, :], h[:, u, c * P:(c + 1) * P], K["ident"][:, :])
                    last.then_inc(h_ps[u], 1)
                    pe.wait_ge(hT_ready[u], n)
                    for c in range(2):
                        last = pe.matmul(pX[u][:, 0:WX], hT[:, u, c, :], wx[:, c, :], start=(c == 0), stop=(c == 1))
                    last.then_inc(x_ps[u], 1)

            repeat(pe, NBP // 2, step)

        @block.scalar
        def _(act):
            def step(i):
                n = snap(act, i + 1)
                for u in range(2):
                    act.wait_ge(t_ps[u], n)
                    act.activation(aT[:, u, :, :], pT[:, :, :], ACT.Copy).then_inc(aT_ready[u], 1)
                for u in range(2):
                    root(nc, act, mv[:, u, :], K["eps"], var_ready[u], root_ready[u], n)
                    act.wait_ge(h_ps[u], n)
                    act.activation(hT[:, u, :, :], pH[:, 0:2, :], ACT.Copy).then_inc(hT_ready[u], 1)
                    at_least(act, stored[u], snap(act, i * 48))
                    act.wait_ge(x_ps[u], n)
                    act.activation(tb[:, u, :], pX[u][:, 0:WX], ACT.Copy).then_inc(tb_ready[u], 1)

            repeat(act, NBP // 2, step)


def layer2_nodes(nc, A, T, K):
    WX = D + 2 * H
    with Stage(nc, "l2n") as S:
        si = S.sb("si", [P, 2, 1], I32)
        di = S.sb("di", [P, 2, 1], I32)
        rd = S.sb("rd", [P, 2, 1])
        x = S.sb("x", [P, 2, D])
        gd = S.sb("gd", [P, 2, WX])
        gs = S.sb("gs", [P, 2, H])
        z = S.sb("z", [P, 2, H])
        al = S.sb("al", [P, 2, H])
        sm = S.sb("sm", [P, 2, 2])
        pr = S.sb("pr", [P, 2, H, DK])
        tm = S.sb("tm", [P, 2, DK])
        x2 = S.sb("x2", [P, 2, D])
        st = S.sb("st", [P, 2, 6])
        mv = S.sb("mv", [P, 2, 4])
        h = S.sb("h", [P, 2, D])
        hs = S.sb("hs", [P, 2, D])
        two = lambda k: S.sems_of(k, 2)
        x_in, x_used, g_in, z_ready, e_ready, var_ready, root_ready, out_ready, stored = (
            two(k) for k in ("x_in", "x_used", "g_in", "z_ready", "e_ready", "var_ready", "root_ready", "out_ready", "stored"))
        turn = S.sem("turn")
        block = S.block()

        @block.sync
        def _(sp):
            def step(i):
                n = snap(sp, i + 1)
                for u in range(2):
                    r = snap(sp, (2 * i + u) * P)
                    at_least(sp, x_used[u], i)
                    sp.sem_inc(turn, 1)
                    sp.dma_start(si[:, u, :], A["src"].rearrange("(n o) -> n o", o=1)[bass.ds(r, P), :]).then_inc(x_in[u], 16)
                    sp.dma_start(di[:, u, :], A["dst"].rearrange("(n o) -> n o", o=1)[bass.ds(r, P), :]).then_inc(x_in[u], 16)
                    sp.dma_start(x[:, u, :], rows(T["x1"], r)).then_inc(x_in[u], 16)
                    sp.dma_start(rd[:, u, :], rows(T["rdego"], r)).then_inc(x_in[u], 16)
                for u in range(2):
                    r = snap(sp, (2 * i + u) * P)
                    sp.wait_ge(out_ready[u], n)
                    sp.sem_inc(turn, 1)
                    sp.dma_start(rows(T["x2"], r), x2[:, u, :]).then_inc(stored[u], 16)
                    sp.dma_start(rows(T["h2"], r), h[:, u, :]).then_inc(stored[u], 16)
                    sp.dma_start(rows(T["table2"], r), hs[:, u, :]).then_inc(stored[u], 16)

            repeat(sp, NBP // 2, step)
            for u in range(2):
                sp.wait_ge(stored[u], 48 * (NBP // 2))

        @block.gpsimd
        def _(pool):
            def step(i):
                n64 = snap(pool, (i + 1) * 64)
                for u in range(2):
                    pool.wait_ge(x_in[u], n64)
                    pool.sem_inc(turn, 1)
                    pool.indirect_dma_start(gd[:, u, :], None, T["table1"][:, :], bass.IndirectOffsetOnAxis(ap=di[:, u, 0:1], axis=0)).then_inc(g_in[u], 16)
                    pool.indirect_dma_start(gs[:, u, :], None, T["tablel"][:, :], bass.IndirectOffsetOnAxis(ap=si[:, u, 0:1], axis=0)).then_inc(g_in[u], 16)

            repeat(pool, NBP // 2, step)

        @block.scalar
        def _(act):
            def step(i):
                n = snap(act, i + 1)
                for u in range(2):
                    act.wait_ge(z_ready[u], n)
                    act.activation(al[:, u, :], z[:, u, :], ACT.Exp, accum_out=sm[:, u, 0:1]).then_inc(e_ready[u], 1)
                for u in range(2):
                    root(nc, act, mv[:, u, :], K["eps"], var_ready[u], root_ready[u], n)

            repeat(act, NBP // 2, step)

        @block.vector
        def _(dve):
            def step(i):
                n, n32 = snap(dve, i + 1), snap(dve, (i + 1) * 32)
                for u in range(2):
                    dve.wait_ge(g_in[u], n32)
                    dve.tensor_tensor(z[:, u, :], gs[:, u, :], gd[:, u, D + H:WX], ALU.add)
                    dve.drain()
                    dve.scalar_tensor_tensor(out=z[:, u, :], in0=z[:, u, :], scalar=0.01, in1=z[:, u, :], op0=ALU.mult, op1=ALU.max)
                    dve.drain()
                    dve.tensor_reduce(sm[:, u, 1:2], z[:, u, :], AX.X, ALU.max)
                    dve.drain()
                    dve.tensor_scalar(z[:, u, :], z[:, u, :], sm[:, u, 1:2], None, ALU.subtract).then_inc(z_ready[u], 1)
                for u in range(2):
                    dve.wait_ge(e_ready[u], n)
                    dve.reciprocal(sm[:, u, 0:1], sm[:, u, 0:1])
                    dve.drain()
                    dve.tensor_scalar(al[:, u, :], al[:, u, :], sm[:, u, 0:1], None, ALU.mult)
                    dve.drain()
                    dve.tensor_tensor(pr[:, u, :, :], gd[:, u, 0:D].rearrange("p (h d) -> p h d", h=H), al[:, u, :].unsqueeze(2).to_broadcast([P, H, DK]), ALU.mult)
                    dve.drain()
                    dve.tensor_reduce(tm[:, u, :], pr[:, u, :, :].rearrange("p h d -> p d h"), AX.X, ALU.add)
                    dve.drain()
                    at_least(dve, stored[u], snap(dve, i * 48))
                    dve.tensor_tensor(x2[:, u, :].rearrange("p (h d) -> p h d", h=H), x[:, u, :].rearrange("p (h d) -> p h d", h=H),
                                      tm[:, u, :].unsqueeze(1).to_broadcast([P, H, DK]), ALU.add)
                    dve.drain()
                    normalise(nc, dve, x2[:, u, :], st[:, u, :], mv[:, u, :], h[:, u, :], var_ready[u], root_ready[u], n)
                    dve.tensor_scalar(h[:, u, :], h[:, u, :], 0.0, None, ALU.max)
                    dve.drain()
                    dve.tensor_scalar(hs[:, u, :], h[:, u, :], rd[:, u, 0:1], None, ALU.mult)
                    dve.drain().then_inc(out_ready[u], 1)
                    dve.sem_inc(x_used[u], 1)

            repeat(dve, NBP // 2, step)


def sum_items(nc, name, table, agg, T, K):
    with Stage(nc, name) as S:
        W = D + 1
        rec = S.sb("rec", [P, SL, G, 4], I32)
        itf = S.sb("itf", [P, SL, 4])
        row = S.sb("row", [P, SL, G, W])
        dl = S.sb("dl", [P, SL, G])
        oh = S.sb("oh", [P, SL, G, P])
        acc = S.sb("acc", [P, SL, W])
        pA = [S.ps(f"pA{j}", [P, 512]) for j in range(2)]
        many = lambda k: S.sems_of(k, SL)
        in_ready, row_ready, dl_done, oh_ready, a_ps, item_done, stored = (
            many(k) for k in ("in_ready", "row_ready", "dl_done", "oh_ready", "a_ps", "item_done", "stored"))
        consts, turn = S.sem("consts"), S.sem("turn")
        block = S.block()
        KI = NI // SL

        def over_items(eng, step):
            for s in range(SL):
                step(s, 0, s)
            with eng.Fori(1, KI - 1) as k:
                kk = snap(eng, k + 0)
                for s in range(SL):
                    step(s, kk, k * SL + s)
            for s in range(SL):
                step(s, KI - 1, (KI - 1) * SL + s)

        def prv(s, k):
            return ((s - 1) % SL, k - (s == 0))

        def need(eng, sems, s, k, per=1):
            at_least(eng, sems[s], snap(eng, (k + 1) * per))

        @block.sync
        def _(sp):
            def load(s, k, i):
                e0 = sp.value_load(K["items"][0:1, 0, bass.ds(i, 1)], min_val=0, max_val=E)
                need(sp, item_done, s, k - 1)
                sp.sem_inc(turn, 1)
                sp.dma_start(rec[:, s, :, :].rearrange("p g c -> p (g c)"),
                             T["rec"][bass.ds(e0, EW), :].rearrange("(p g) c -> p (g c)", g=G)).then_inc(in_ready[s], 16)
                sp.dma_start(itf[:, s, :], T["itemf"][bass.ds(i, 1), :].to_broadcast([P, 4])).then_inc(in_ready[s], 16)

            for s in range(SL):
                load(s, 0, s)

            def step(s, k, i):
                b0 = sp.value_load(K["items"][0:1, 1, bass.ds(i, 1)], min_val=0, max_val=NB * P)
                ps, pk = prv(s, k)
                mine, before = snap(sp, k + 1), snap(sp, (pk + 1) * 16)
                at_least(sp, item_done[s], mine)
                sp.sem_inc(turn, 1)
                at_least(sp, stored[ps], before)
                sp.sem_inc(turn, 1)
                sp.dma_start(agg[bass.ds(b0, P), :], acc[:, s, :]).then_inc(stored[s], 16)
                if not (isinstance(k, int) and k == KI - 1):
                    load(s, k + 1, i + SL)

            over_items(sp, step)
            sp.wait_ge(stored[SL - 1], 16 * KI)

        @block.gpsimd
        def _(pool):
            pool.memset(row[:, :, :, D:W], 1.0)
            pool.memset(acc[:, SL - 1, :], 0.0)
            pool.drain().then_inc(consts, 1)

            def step(s, k, i):
                need(pool, in_ready, s, k, 32)
                pool.sem_inc(turn, 1)
                for g in range(G):
                    pool.indirect_dma_start(row[:, s, g, 0:D], None, table[:, :],
                                            bass.IndirectOffsetOnAxis(ap=rec[:, s, g, 1:2], axis=0)).then_inc(row_ready[s], 16)

            over_items(pool, step)

        @block.vector
        def _(dve):
            dve.wait_ge(consts, 1)

            def onehots(s, k):
                need(dve, in_ready, s, k, 32)
                recf = rec[:, s, :, :].bitcast(F32)
                dve.tensor_scalar(dl[:, s, :], recf[:, :, 2], itf[:, s, 0:1], None, ALU.subtract).then_inc(dl_done[s], 1)
                need(dve, dl_done, s, k)
                for g in range(G):
                    last = dve.tensor_scalar(oh[:, s, g, :], K["iota"][:, :], dl[:, s, g:g + 1], None, ALU.is_equal)
                last.then_inc(oh_ready[s], 1)

            onehots(0, 0)

            def step(s, k, i):
                ps, pk = prv(s, k)
                if s < SL - 1 or not (isinstance(k, int) and k == KI - 1):
                    onehots((s + 1) % SL, k + (s + 1) // SL)
                need(dve, a_ps, s, k)
                need(dve, item_done, ps, pk)
                need(dve, stored, s, k - 1, 16)
                dve.scalar_tensor_tensor(out=acc[:, s, :], in0=acc[:, ps, :], scalar=itf[:, s, 1:2], in1=pA[s % 2][:, 0:W],
                                         op0=ALU.mult, op1=ALU.add).then_inc(item_done[s], 1)

            over_items(dve, step)

        @block.tensor
        def _(pe):
            pe.wait_ge(consts, 1)

            def step(s, k, i):
                s2, k2 = (s - 2) % SL, k - (s < 2)
                need(pe, oh_ready, s, k)
                need(pe, row_ready, s, k, 16 * G)
                need(pe, item_done, s2, k2)
                for g in range(G):
                    last = pe.matmul(pA[s % 2][:, 0:W], oh[:, s, g, :], row[:, s, g, :], start=(g == 0), stop=(g == G - 1))
                last.then_inc(a_ps[s], 1)

            over_items(pe, step)


def gate(nc, A, T, K):
    with Stage(nc, "gate") as S:
        w = S.sb("w", [P, 4, D])
        bias = S.sb("bias", [1, 2, D])
        wg = S.sb("wg", [P, 2, EX])
        bg = S.sb("bg", [1, EX])
        ag = S.sb("ag", [P, 2, D + 1])
        mh = S.sb("mh", [P, 2, 2, D])
        mk = S.sb("mk", [P, 2, 2 * NT])
        rd = S.sb("rd", [P, 2, 1])
        mT = S.sb("mT", [P, 2, 4, P])
        xx = S.sb("xx", [P, 2, D])
        xT = S.sb("xT", [P, 2, 2, P])
        lg = S.sb("lg", [P, 2, EX])
        v8 = S.sb("v8", [P, 2, 8])
        i8 = S.sb("i8", [P, 2, 8], U32)
        ef = S.sb("ef", [P, 2, 2])
        oh = S.sb("oh", [P, 2, 2, EX])
        m = S.sb("m", [P, 2, EX])
        tot = S.sb("tot", [P, EX])
        pr = S.sb("pr", [P, 2, 2, EX])
        rt = S.sb("rt", [P, 2, 8])
        dv = S.sb("dv", [P, 2, 2])
        pT = S.ps("pT", [P, 4, P])
        pXX = [S.ps(f"pXX{u}", [P, 512]) for u in range(2)]
        pT2 = S.ps("pT2", [P, 4, P])
        pL = [S.ps(f"pL{u}", [P, 512]) for u in range(2)]
        pP = [S.ps(f"pP{u}", [P, 512]) for u in range(2)]
        two = lambda k: S.sems_of(k, 2)
        w_in, turn, bias_ready = S.sem("w_in"), S.sem("turn"), S.sem("bias_ready")
        x_in, x_used, deg_ready, rt_ready, mh_ready, t_ps, mT_ready, xx_ps, xx_ready = (
            two(k) for k in ("x_in", "x_used", "deg_ready", "rt_ready", "mh_ready", "t_ps", "mT_ready", "xx_ps", "xx_ready"))
        t2_ps, xT_ready, l_ps, d_ready, e_ready, m_ready, p_ps, r_ready, stored = (
            two(k) for k in ("t2_ps", "xT_ready", "l_ps", "d_ready", "e_ready", "m_ready", "p_ps", "r_ready", "stored"))
        end_ps = S.sem("end_ps")
        block = S.block()

        @block.sync
        def _(sp):
            sp.dma_start(w[:, 0:2, :], A["L2_gnn_W_gc"].rearrange("(c p) n -> p c n", p=P)).then_inc(w_in, 16)
            sp.dma_start(w[:, 2:4, :], A["L2_gnn_W_res"].rearrange("(c p) n -> p c n", p=P)).then_inc(w_in, 16)
            sp.dma_start(wg[:, :, :], A["L2_gnn_Wg"].rearrange("(c p) n -> p c n", p=P)).then_inc(w_in, 16)
            for j, (t, a) in enumerate(((bias[:, 0, :], "b_gc"), (bias[:, 1, :], "b_res"), (bg[:, :], "bg"))):
                sp.dma_start(t, A[f"L2_gnn_{a}"].rearrange("(o n) -> o n", o=1)).then_inc(w_in, 16)

            def step(i):
                n = snap(sp, i + 1)
                for u in range(2):
                    r = snap(sp, (2 * i + u) * P)
                    at_least(sp, x_used[u], i)
                    sp.sem_inc(turn, 1)
                    sp.dma_start(ag[:, u, :], rows(T["agg2"], r)).then_inc(x_in[u], 16)
                    sp.dma_start(mh[:, u, 1, :], rows(T["h2"], r)).then_inc(x_in[u], 16)
                    sp.dma_start(mk[:, u, :], rows(T["tmask"], r)).then_inc(x_in[u], 16)
                for u in range(2):
                    r = snap(sp, (2 * i + u) * P)
                    sp.wait_ge(r_ready[u], n)
                    sp.sem_inc(turn, 1)
                    sp.dma_start(rows(T["xx"], r), xx[:, u, :]).then_inc(stored[u], 16)
                    sp.dma_start(rows(T["route"], r), rt[:, u, :]).then_inc(stored[u], 16)

            repeat(sp, NBP // 2, step)
            for u in range(2):
                sp.wait_ge(stored[u], 32 * (NBP // 2))

        @block.vector
        def _(dve):
            dve.memset(tot[:, :], 0.0)
            dve.wait_ge(w_in, 96)
            dve.tensor_tensor(bias[:, 0, :], bias[:, 0, :], bias[:, 1, :], ALU.add).then_inc(bias_ready, 1)

            def step(i):
                n, n48 = snap(dve, i + 1), snap(dve, (i + 1) * 48)
                for u in range(2):
                    dve.wait_ge(x_in[u], n48)
                    dve.tensor_scalar(rd[:, u, :], ag[:, u, D:D + 1], 1.0, None, ALU.max).then_inc(deg_ready[u], 1)
                for u in range(2):
                    dve.wait_ge(rt_ready[u], n)
                    dve.reciprocal(rd[:, u, :], rd[:, u, :])
                    dve.drain()
                    dve.tensor_scalar(mh[:, u, 0, :], ag[:, u, 0:D], rd[:, u, 0:1], None, ALU.mult).then_inc(mh_ready[u], 1)
                for u in range(2):
                    dve.wait_ge(l_ps[u], n)
                    dve.tensor_copy(lg[:, u, :], pL[u][:, 0:EX])
                    dve.drain()
                    dve.max(v8[:, u, :], lg[:, u, :])
                    dve.drain()
                    dve.max_index(i8[:, u, :], v8[:, u, :], lg[:, u, :])
                    dve.tensor_tensor(dv[:, u, 0:1], v8[:, u, 1:2], v8[:, u, 0:1], ALU.subtract).then_inc(d_ready[u], 1)
                    dve.drain()
                    dve.tensor_copy(ef[:, u, :], i8[:, u, 0:2])
                    dve.tensor_reduce(dv[:, u, 1:2], mk[:, u, 0:NT], AX.X, ALU.add)
                    dve.drain()
                    for k in range(2):
                        dve.tensor_scalar(oh[:, u, k, :], K["iota"][:, 0:EX], ef[:, u, k:k + 1], dv[:, u, 1:2], ALU.is_equal, ALU.mult)
                    dve.drain()
                    dve.tensor_tensor(m[:, u, :], oh[:, u, 0, :], oh[:, u, 1, :], ALU.add).then_inc(m_ready[u], 1)
                    dve.wait_ge(p_ps[u], n)
                    dve.tensor_tensor(tot[:, :], tot[:, :], m[:, u, :], ALU.add)
                    at_least(dve, stored[u], snap(dve, i * 32))
                    dve.tensor_tensor(pr[:, u, :, :], oh[:, u, :, :], pP[u][:, 0:EX].unsqueeze(1).to_broadcast([P, 2, EX]), ALU.mult)
                    dve.drain()
                    dve.tensor_reduce(rt[:, u, 2:4], pr[:, u, :, :], AX.X, ALU.add)
                    dve.tensor_copy(rt[:, u, 0:2], ef[:, u, :])
                    dve.tensor_copy(rt[:, u, 6:7], dv[:, u, 1:2])
                    dve.tensor_copy(rt[:, u, 7:8], dv[:, u, 1:2])
                    dve.wait_ge(e_ready[u], n)
                    dve.tensor_scalar(rt[:, u, 4:5], rt[:, u, 5:6], 1.0, None, ALU.add)
                    dve.drain()
                    dve.reciprocal(rt[:, u, 4:5], rt[:, u, 4:5])
                    dve.drain()
                    dve.tensor_tensor(rt[:, u, 5:6], rt[:, u, 5:6], rt[:, u, 4:5], ALU.mult)
                    dve.drain().then_inc(r_ready[u], 1)
                    dve.sem_inc(x_used[u], 1)

            repeat(dve, NBP // 2, step)
            dve.wait_ge(end_ps, 1)
            dve.tensor_copy(K["count"][:, :], pP[0][0:EX, 0:1])

        @block.scalar
        def _(act):
            def step(i):
                n = snap(act, i + 1)
                for u in range(2):
                    act.wait_ge(deg_ready[u], n)
                    act.activation(rd[:, u, :], rd[:, u, :], ACT.Sqrt).then_inc(rt_ready[u], 1)
                for u in range(2):
                    act.wait_ge(t_ps[u], n)
                    act.activation(mT[:, u, :, :], pT[:, :, :], ACT.Copy).then_inc(mT_ready[u], 1)
                    at_least(act, stored[u], snap(act, i * 32))
                    act.wait_ge(xx_ps[u], n)
                    act.activation(xx[:, u, :], pXX[u][:, 0:D], ACT.Copy).then_inc(xx_ready[u], 1)
                    act.wait_ge(t2_ps[u], n)
                    act.activation(xT[:, u, :, :], pT2[:, 0:2, :], ACT.Copy).then_inc(xT_ready[u], 1)
                for u in range(2):
                    act.wait_ge(d_ready[u], n)
                    act.activation(rt[:, u, 5:6], dv[:, u, 0:1], ACT.Exp).then_inc(e_ready[u], 1)

            repeat(act, NBP // 2, step)

        @block.tensor
        def _(pe):
            pe.wait_ge(w_in, 96)
            pe.wait_ge(bias_ready, 1)

            def step(i):
                n = snap(pe, i + 1)
                for u in range(2):
                    pe.wait_ge(mh_ready[u], n)
                    for c in range(4):
                        last = pe.transpose(pT[:, c, :], mh[:, u, c // 2, (c % 2) * P:(c % 2 + 1) * P], K["ident"][:, :])
                    last.then_inc(t_ps[u], 1)
                    pe.wait_ge(mT_ready[u], n)
                    for c in range(4):
                        pe.matmul(pXX[u][:, 0:D], mT[:, u, c, :], w[:, c, :], start=(c == 0), stop=False)
                    pe.matmul(pXX[u][:, 0:D], K["ones"][0:1, :], bias[:, 0, :], start=False, stop=True).then_inc(xx_ps[u], 1)
                    pe.wait_ge(xx_ready[u], n)
                    for c in range(2):
                        last = pe.transpose(pT2[:, c, :], xx[:, u, c * P:(c + 1) * P], K["ident"][:, :])
                    last.then_inc(t2_ps[u], 1)
                    pe.wait_ge(xT_ready[u], n)
                    for c in range(2):
                        pe.matmul(pL[u][:, 0:EX], xT[:, u, c, :], wg[:, c, :], start=(c == 0), stop=False)
                    pe.matmul(pL[u][:, 0:EX], K["ones"][0:1, :], bg[:, :], start=False, stop=True).then_inc(l_ps[u], 1)
                for u in range(2):
                    pe.wait_ge(m_ready[u], n)
                    pe.sem_inc(turn, 1)
                    pe.matmul(pP[u][:, 0:EX], K["ones"][:, :], tot[:, :], start=True, stop=False)
                    pe.matmul(pP[u][:, 0:EX], K["upper"][:, :], m[:, u, :], start=False, stop=True).then_inc(p_ps[u], 1)

            repeat(pe, NBP // 2, step)
            pe.wait_ge(r_ready[1], NBP // 2)
            pe.matmul(pP[0][0:EX, 0:1], tot[:, :], K["ones"][:, 0:1], start=True, stop=True).then_inc(end_ps, 1)


def slots(nc, A, T, K):
    with Stage(nc, "slot") as S:
        cc = S.sb("cc", [EX, 1])
        s8 = S.sb("s8", [EX, CAP // P])
        nt = S.sb("nt", [EX, 1])
        ts = S.sb("ts", [EX, 2])
        dg = S.sb("dg", [EX, EX])
        ji = S.sb("ji", [EX, NTILE], I32)
        jf = S.sb("jf", [EX, NTILE])
        s8i = S.sb("s8i", [EX, CAP // P], I32)
        pi = S.sb("pi", [P, 1], I32)
        pf = S.sb("pf", [P, 1])
        sr = S.sb("sr", [P, EX])
        tf = S.sb("tf", [1, NTILE])
        rt = S.sb("rt", [P, NBP, 8])
        oh = S.sb("oh", [P, NBP, EX])
        sl = S.sb("sl", [P, NBP, 2])
        ok = S.sb("ok", [P, NBP, 2])
        sli = S.sb("sli", [P, NBP, 2], I32)
        pa = S.ps("pa", [P, 512])
        pb = S.ps("pb", [P, 512])
        pc = S.ps("pc", [P, 512])
        rt_in, iotas, nt_ready, ts_ps, dg_ready, sr_ps, sl_ready, stored = (
            S.sem(k) for k in ("rt_in", "iotas", "nt_ready", "ts_ps", "dg_ready", "sr_ps", "sl_ready", "stored"))
        block = S.block()

        @block.sync
        def _(sp):
            sp.dma_start(rt[:, :, :], T["route"].rearrange("(b p) c -> p b c", p=P)).then_inc(rt_in, 16)
            sp.wait_ge(sl_ready, 1)
            sp.dma_start(T["slot"].rearrange("(b p) c -> p b c", p=P), sli[:, :, :]).then_inc(stored, 16)
            sp.dma_start(T["gates"].rearrange("(b p) c -> p b c", p=P), ok[:, :, :]).then_inc(stored, 16)
            sp.wait_ge(stored, 32)

        @block.gpsimd
        def _(pool):
            pool.iota(s8i[:, :], pattern=[[P, CAP // P]], base=0, channel_multiplier=0)
            pool.iota(ji[:, :], pattern=[[1, NTILE]], base=0, channel_multiplier=0)
            pool.iota(pi[:, :], pattern=[[0, 1]], base=SLOTS, channel_multiplier=1)
            pool.drain().then_inc(iotas, 1)

        @block.tensor
        def _(pe):
            pe.wait_ge(nt_ready, 1)
            pe.matmul(pa[0:EX, 0:1], K["upper"][0:EX, 0:EX], nt[:, :], start=True, stop=True).then_inc(ts_ps, 1)
            pe.wait_ge(dg_ready, 1)
            pe.matmul(pb[:, 0:EX], K["ones"][0:EX, :], dg[:, :], start=True, stop=True)
            pe.matmul(pc[0:1, 0:NTILE], K["ones"][0:EX, 0:1], jf[:, :], start=True, stop=True).then_inc(sr_ps, 1)

        @block.vector
        def _(dve):
            dve.wait_ge(iotas, 1)
            dve.tensor_scalar(cc[:, :], K["count"][:, :], float(CAP), None, ALU.min)
            dve.tensor_copy(s8[:, :], s8i[:, :])
            dve.tensor_copy(jf[:, :], ji[:, :])
            dve.tensor_copy(pf[:, :], pi[:, :])
            dve.drain()
            dve.tensor_scalar(s8[:, :], s8[:, :], cc[:, 0:1], 0.0, ALU.is_lt, ALU.add, accum_out=nt[:, 0:1])
            dve.drain().then_inc(nt_ready, 1)
            dve.wait_ge(ts_ps, 1)
            dve.tensor_copy(ts[:, 0:1], pa[0:EX, 0:1])
            dve.drain()
            dve.tensor_tensor(ts[:, 1:2], ts[:, 0:1], nt[:, :], ALU.add)
            dve.tensor_scalar(dg[:, :], K["ident"][0:EX, 0:EX], ts[:, 0:1], float(P), ALU.mult, ALU.mult)
            dve.drain()
            dve.tensor_scalar(jf[:, :], jf[:, :], ts[:, 1:2], None, ALU.is_ge)
            dve.drain().then_inc(dg_ready, 1)
            dve.wait_ge(sr_ps, 1)
            dve.tensor_copy(sr[:, :], pb[:, 0:EX])
            dve.tensor_scalar(tf[:, :], pc[0:1, 0:NTILE], float(EX - 1), None, ALU.min)
            dve.wait_ge(rt_in, 16)
            dve.drain()
            dve.tensor_copy(K["tiles"][:, :], tf[:, :])
            for k in range(2):
                dve.tensor_tensor(oh[:, :, :], K["iota"][:, 0:EX].unsqueeze(1).to_broadcast([P, NBP, EX]), rt[:, :, k:k + 1].to_broadcast([P, NBP, EX]), ALU.is_equal)
                dve.drain()
                dve.tensor_tensor(oh[:, :, :], oh[:, :, :], sr[:, :].unsqueeze(1).to_broadcast([P, NBP, EX]), ALU.mult)
                dve.drain()
                dve.tensor_reduce(sl[:, :, k], oh[:, :, :], AX.X, ALU.add)
                dve.drain()
            dve.tensor_scalar(ok[:, :, :], rt[:, :, 2:4], float(CAP), None, ALU.is_lt)
            dve.tensor_tensor(sl[:, :, :], sl[:, :, :], rt[:, :, 2:4], ALU.add)
            dve.drain()
            dve.tensor_tensor(ok[:, :, :], ok[:, :, :], rt[:, :, 6:8], ALU.mult)
            dve.tensor_scalar(sl[:, :, :], sl[:, :, :], pf[:, 0:1], None, ALU.subtract)
            dve.drain()
            dve.tensor_tensor(sl[:, :, :], sl[:, :, :], ok[:, :, :], ALU.mult)
            dve.drain()
            dve.tensor_scalar(sl[:, :, :], sl[:, :, :], pf[:, 0:1], None, ALU.add)
            dve.drain()
            dve.tensor_copy(sli[:, :, :], sl[:, :, :])
            dve.tensor_tensor(ok[:, :, :], ok[:, :, :], rt[:, :, 4:6], ALU.mult)
            dve.drain().then_inc(sl_ready, 1)


def dispatch(nc, A, T, K):
    with Stage(nc, "disp") as S:
        x = S.sb("x", [P, 2, D])
        sl = S.sb("sl", [P, 2, 2], I32)
        two = lambda k: S.sems_of(k, 2)
        x_in, sent = two("x_in"), two("sent")
        turn = S.sem("turn")
        block = S.block()

        @block.sync
        def _(sp):
            def step(i):
                for u in range(2):
                    r = snap(sp, (2 * i + u) * P)
                    at_least(sp, sent[u], snap(sp, i * 32))
                    sp.sem_inc(turn, 1)
                    sp.dma_start(x[:, u, :], rows(T["xx"], r)).then_inc(x_in[u], 16)
                    sp.dma_start(sl[:, u, :], rows(T["slot"], r)).then_inc(x_in[u], 16)

            repeat(sp, NBP // 2, step)

        @block.gpsimd
        def _(pool):
            def step(i):
                n32 = snap(pool, (i + 1) * 32)
                for u in range(2):
                    before = snap(pool, i * 32)
                    pool.wait_ge(x_in[u], n32)
                    pool.sem_inc(turn, 1)
                    if u == 1:
                        pool.wait_ge(sent[0], n32)
                        pool.sem_inc(turn, 1)
                    else:
                        at_least(pool, sent[1], before)
                        pool.sem_inc(turn, 1)
                    pool.indirect_dma_start(T["xslot"][:, :], bass.IndirectOffsetOnAxis(ap=sl[:, u, 0:1], axis=0), x[:, u, :], None).then_inc(sent[u], 16)
                    pool.wait_ge(sent[u], snap(pool, i * 32 + 16))
                    pool.sem_inc(turn, 1)
                    pool.indirect_dma_start(T["xslot"][:, :], bass.IndirectOffsetOnAxis(ap=sl[:, u, 1:2], axis=0), x[:, u, :], None).then_inc(sent[u], 16)

            repeat(pool, NBP // 2, step)
            for u in range(2):
                pool.wait_ge(sent[u], 32 * (NBP // 2))


def experts(nc, A, T, K):
    with Stage(nc, "exp") as S:
        HC = HID // P
        w1 = S.sb("w1", [P, 2, 2, HID])
        w2 = S.sb("w2", [P, 2, HC, D])
        b1 = S.sb("b1", [1, 2, HID])
        b2 = S.sb("b2", [1, 2, D])
        x = S.sb("x", [P, 2, D])
        xT = S.sb("xT", [P, 2, 2, P])
        h1 = S.sb("h1", [P, 2, HC, P])
        y = S.sb("y", [P, 2, D])
        zero = S.sb("zero", [P, D])
        pX = [S.ps(f"pX{u}", [P, 4, P]) for u in range(2)]
        pH = [S.ps(f"pH{u}", [P, HC, P]) for u in range(2)]
        pY = [S.ps(f"pY{u}", [P, 512]) for u in range(2)]
        two = lambda k: S.sems_of(k, 2)
        w_in, x_ps, xT_ready, h_ps, h_ready, y_ps, y_ready, stored = (
            two(k) for k in ("w_in", "x_ps", "xT_ready", "h_ps", "h_ready", "y_ps", "y_ready", "stored"))
        turn, zeroed, dump = S.sem("turn"), S.sem("zeroed"), S.sem("dump")
        block = S.block()

        @block.sync
        def _(sp):
            sp.wait_ge(zeroed, 1)
            sp.dma_start(T["yslot"][SLOTS:SLOTS + P, :], zero[:, :]).then_inc(dump, 16)

            def load(i, u):
                e = sp.value_load(K["tiles"][0:1, bass.ds(2 * i + u, 1)], min_val=0, max_val=EX - 1)
                at_least(sp, y_ready[u], i)
                sp.sem_inc(turn, 1)
                sp.dma_start(x[:, u, :], rows(T["xslot"], snap(sp, (2 * i + u) * P))).then_inc(w_in[u], 16)
                sp.dma_start(b1[:, u, :], A["L2_gnn_b1"][bass.ds(e, 1), :]).then_inc(w_in[u], 16)
                sp.dma_start(b2[:, u, :], A["L2_gnn_b2"][bass.ds(e, 1), :]).then_inc(w_in[u], 16)
                sp.dma_start(w1[:, u, :, :], A["L2_gnn_w1"][bass.ds(e, 1), :, :].rearrange("e (c p) n -> p (e c) n", p=P)).then_inc(w_in[u], 16)
                sp.dma_start(w2[:, u, :, :], A["L2_gnn_w2"][bass.ds(e, 1), :, :].rearrange("e (c p) n -> p (e c) n", p=P)).then_inc(w_in[u], 16)

            load(0, 0)
            load(0, 1)

            def step(i):
                n = snap(sp, i + 1)
                for u in range(2):
                    r = snap(sp, (2 * i + u) * P)
                    sp.wait_ge(y_ready[u], n)
                    sp.sem_inc(turn, 1)
                    sp.dma_start(rows(T["yslot"], r), y[:, u, :]).then_inc(stored[u], 16)
                    if not (isinstance(i, int) and i == NTILE // 2 - 1):
                        load(i + 1, u)

            step(0)
            with sp.Fori(1, NTILE // 2 - 1) as i:
                step(i)
            step(NTILE // 2 - 1)
            sp.wait_ge(dump, 16)
            for u in range(2):
                sp.wait_ge(stored[u], 16 * (NTILE // 2))

        @block.gpsimd
        def _(pool):
            pool.memset(zero[:, :], 0.0).then_inc(zeroed, 1)

        @block.tensor
        def _(pe):
            def step(i):
                n = snap(pe, i + 1)
                for u in range(2):
                    pe.wait_ge(w_in[u], snap(pe, (i + 1) * 80))
                    for c in range(2):
                        last = pe.transpose(pX[u][:, c, :], x[:, u, c * P:(c + 1) * P], K["ident"][:, :])
                    last.then_inc(x_ps[u], 1)
                for u in range(2):
                    pe.wait_ge(xT_ready[u], n)
                    for m in range(HC):
                        for c in range(2):
                            pe.matmul(pH[u][:, m, :], w1[:, u, c, m * P:(m + 1) * P], xT[:, u, c, :], start=(c == 0), stop=False)
                        last = pe.matmul(pH[u][:, m, :], b1[:, u, m * P:(m + 1) * P], K["ones"][0:1, :], start=False, stop=True)
                    last.then_inc(h_ps[u], 1)
                for u in range(2):
                    pe.wait_ge(h_ready[u], n)
                    for m in range(HC):
                        pe.matmul(pY[u][:, 0:D], h1[:, u, m, :], w2[:, u, m, :], start=(m == 0), stop=False)
                    pe.matmul(pY[u][:, 0:D], K["ones"][0:1, :], b2[:, u, :], start=False, stop=True).then_inc(y_ps[u], 1)

            repeat(pe, NTILE // 2, step)

        @block.scalar
        def _(act):
            def step(i):
                n = snap(act, i + 1)
                for u in range(2):
                    act.wait_ge(h_ps[u], n)
                    act.activation(h1[:, u, :, :], pH[u][:, :, :], ACT.Gelu).then_inc(h_ready[u], 1)

            repeat(act, NTILE // 2, step)

        @block.vector
        def _(dve):
            def step(i):
                n = snap(dve, i + 1)
                for u in range(2):
                    dve.wait_ge(x_ps[u], n)
                    dve.tensor_copy(xT[:, u, :, :], pX[u][:, 0:2, :]).then_inc(xT_ready[u], 1)
                for u in range(2):
                    at_least(dve, stored[u], snap(dve, i * 16))
                    dve.wait_ge(y_ps[u], n)
                    dve.tensor_copy(y[:, u, :], pY[u][:, 0:D]).then_inc(y_ready[u], 1)

            repeat(dve, NTILE // 2, step)


def combine(nc, A, T, K):
    with Stage(nc, "comb") as S:
        Y = S.sb("Y", [P, NBP * D])
        X2 = S.sb("X2", [P, NBP, D])
        SQ = S.sb("SQ", [P, NBP * D])
        x = S.sb("x", [P, 2, D])
        sl = S.sb("sl", [P, 2, 2], I32)
        gt = S.sb("gt", [P, 2, 2])
        ya = S.sb("ya", [P, 2, 2, D])
        tmp = S.sb("tmp", [P, 2, D])
        mk = S.sb("mk", [P, NBP, 2 * NT])
        va = S.sb("va", [P, NBP])
        gb = S.sb("gb", [P, 2, D])
        mean = S.sb("mean", [P, D])
        sd = S.sb("sd", [P, D])
        zero = S.sb("zero", [P, D])
        pM = S.ps("pM", [P, 512])
        two = lambda k: S.sems_of(k, 2)
        x_in, y_in, used = two("x_in"), two("y_in"), two("used")
        turn, c_in, m_ps, sq_ready, v_ps, v_ready, s_ready, out_ready, stored, y_all, zr = (
            S.sem(k) for k in ("turn", "c_in", "m_ps", "sq_ready", "v_ps", "v_ready", "s_ready", "out_ready", "stored", "y_all", "zr"))
        block = S.block()
        Y3 = Y[:, :].rearrange("p (b n) -> p b n", b=NBP)

        @block.sync
        def _(sp):
            for j, a in enumerate(("gamma", "beta")):
                sp.dma_start(gb[:, j, :], A[f"L2_gnn_{a}"].rearrange("(o n) -> o n", o=1).to_broadcast([P, D])).then_inc(c_in, 16)
            sp.dma_start(mk[:, :, :], T["tmask"].rearrange("(b p) c -> p b c", p=P)).then_inc(c_in, 16)
            sp.dma_start(X2[:, :, :], T["x2"].rearrange("(b p) c -> p b c", p=P)).then_inc(c_in, 16)

            def step(i):
                for u in range(2):
                    r = snap(sp, (2 * i + u) * P)
                    at_least(sp, used[u], i)
                    sp.sem_inc(turn, 1)
                    sp.dma_start(x[:, u, :], rows(T["xx"], r)).then_inc(x_in[u], 16)
                    sp.dma_start(sl[:, u, :], rows(T["slot"], r)).then_inc(x_in[u], 16)
                    sp.dma_start(gt[:, u, :], rows(T["gates"], r)).then_inc(x_in[u], 16)

            repeat(sp, NBP // 2, step)
            sp.wait_ge(out_ready, 1)
            sp.dma_start(T["x3"].rearrange("(b p) c -> p b c", p=P), X2[:, :, :]).then_inc(stored, 16)
            sp.wait_ge(stored, 16)

        @block.gpsimd
        def _(pool):
            pool.memset(zero[:, :], 0.0).then_inc(zr, 1)

            def step(i):
                n48 = snap(pool, (i + 1) * 48)
                for u in range(2):
                    pool.wait_ge(x_in[u], n48)
                    pool.sem_inc(turn, 1)
                    for k in range(2):
                        pool.indirect_dma_start(ya[:, u, k, :], None, T["yslot"][:, :], bass.IndirectOffsetOnAxis(ap=sl[:, u, k:k + 1], axis=0)).then_inc(y_in[u], 16)

            repeat(pool, NBP // 2, step)

        @block.vector
        def _(dve):
            def step(i):
                n32 = snap(dve, (i + 1) * 32)
                for u in range(2):
                    dve.wait_ge(y_in[u], n32)
                    dve.scalar_tensor_tensor(out=tmp[:, u, :], in0=ya[:, u, 0, :], scalar=gt[:, u, 0:1], in1=x[:, u, :], op0=ALU.mult, op1=ALU.add)
                    dve.drain()
                    dve.scalar_tensor_tensor(out=Y[:, bass.ds((2 * i + u) * D, D)], in0=ya[:, u, 1, :], scalar=gt[:, u, 1:2], in1=tmp[:, u, :], op0=ALU.mult, op1=ALU.add)
                    dve.drain().then_inc(used[u], 1)

            repeat(dve, NBP // 2, step)
            dve.wait_ge(c_in, 64)
            dve.tensor_reduce(va[:, :], mk[:, :, 0:NT], AX.X, ALU.add)
            dve.drain()
            valid = va[:, :].unsqueeze(2).to_broadcast([P, NBP, D])
            dve.tensor_tensor(Y3, Y3, valid, ALU.mult)
            dve.drain().then_inc(y_all, 1)
            dve.wait_ge(m_ps, 1)
            dve.tensor_scalar(mean[:, :], pM[:, 0:D], 1.0 / N, None, ALU.mult)
            dve.drain()
            dve.tensor_tensor(Y3, Y3, mean[:, :].unsqueeze(1).to_broadcast([P, NBP, D]), ALU.subtract)
            dve.drain()
            dve.tensor_tensor(Y3, Y3, valid, ALU.mult)
            dve.drain()
            dve.tensor_tensor(SQ[:, :], Y[:, :], Y[:, :], ALU.mult)
            dve.drain().then_inc(sq_ready, 1)
            dve.wait_ge(v_ps, 1)
            dve.tensor_scalar(sd[:, :], pM[:, 0:D], 1.0 / N, EPS, ALU.mult, ALU.add).then_inc(v_ready, 1)
            dve.wait_ge(s_ready, 1)
            dve.reciprocal(sd[:, :], sd[:, :])
            dve.drain()
            dve.tensor_tensor(sd[:, :], sd[:, :], gb[:, 0, :], ALU.mult)
            dve.drain()
            dve.tensor_tensor(Y3, Y3, sd[:, :].unsqueeze(1).to_broadcast([P, NBP, D]), ALU.mult)
            dve.tensor_tensor(X2[:, :, :], X2[:, :, :], gb[:, 1, :].unsqueeze(1).to_broadcast([P, NBP, D]), ALU.add)
            dve.drain()
            dve.tensor_tensor(X2[:, :, :], X2[:, :, :], Y3, ALU.add)
            dve.drain().then_inc(out_ready, 1)

        @block.tensor
        def _(pe):
            pe.wait_ge(zr, 1)
            for go, t, done in ((y_all, Y, m_ps), (sq_ready, SQ, v_ps)):
                pe.wait_ge(go, 1)
                pe.matmul(pM[:, 0:D], K["ones"][:, :], zero[:, :], start=True, stop=False)
                with pe.Fori(0, NBP) as b:
                    pe.matmul(pM[:, 0:D], K["ones"][:, :], t[:, bass.ds(b * D, D)], start=False, stop=False)
                pe.matmul(pM[:, 0:D], K["ones"][:, :], zero[:, :], start=False, stop=True).then_inc(done, 1)

        @block.scalar
        def _(act):
            act.wait_ge(v_ready, 1)
            act.activation(sd[:, :], sd[:, :], ACT.Sqrt).then_inc(s_ready, 1)


def layer3_nodes(nc, A, T, K):
    with Stage(nc, "l3n") as S:
        w = S.sb("w", [P, 2, 3, D])
        b = S.sb("b", [1, 3, D])
        qe = S.sb("qe", [P, D])
        rel = S.sb("rel", [R64, DK])
        x = S.sb("x", [P, 2, D])
        st = S.sb("st", [P, 2, 6])
        mv = S.sb("mv", [P, 2, 4])
        h = S.sb("h", [P, 2, D])
        en = S.sb("en", [P, 2, D])
        eT = S.sb("eT", [P, 2, 2, P])
        qs = S.sb("qs", [P, 2, D])
        kv = S.sb("kv", [P, 2, 2, D])
        pE = [S.ps(f"pE{u}", [P, 4, P]) for u in range(2)]
        pQ = [S.ps(f"pQ{u}", [P, 512]) for u in range(2)]
        pK = [S.ps(f"pK{u}", [P, 512]) for u in range(2)]
        two = lambda k: S.sems_of(k, 2)
        w_in, rel_in, rel_ready, rel_out, turn = (S.sem(k) for k in ("w_in", "rel_in", "rel_ready", "rel_out", "turn"))
        x_in, var_ready, root_ready, h_done, en_ready, e_ps, eT_ready, q_ps, kv_ready, stored = (
            two(k) for k in ("x_in", "var_ready", "root_ready", "h_done", "en_ready", "e_ps", "eT_ready", "q_ps", "kv_ready", "stored"))
        block = S.block()

        @block.sync
        def _(sp):
            for j, a in enumerate("qkv"):
                sp.dma_start(w[:, :, j, :], A[f"L3_gnn_W{a}"].rearrange("(c p) n -> p c n", p=P)).then_inc(w_in, 16)
                sp.dma_start(b[:, j, :], A[f"L3_gnn_b{a}"].rearrange("(o n) -> o n", o=1)).then_inc(w_in, 16)
            sp.dma_start(qe[:, :], A["L3_gnn_query_emb"].rearrange("(o n) -> o n", o=1).to_broadcast([P, D])).then_inc(w_in, 16)
            sp.dma_start(rel[:, :], A["L3_gnn_rel_w"][:, :]).then_inc(rel_in, 16)

            def step(i):
                n = snap(sp, i + 1)
                for u in range(2):
                    r = snap(sp, (2 * i + u) * P)
                    at_least(sp, en_ready[u], i)
                    sp.sem_inc(turn, 1)
                    sp.dma_start(x[:, u, :], rows(T["x3"], r)).then_inc(x_in[u], 16)
                for u in range(2):
                    r = snap(sp, (2 * i + u) * P)
                    sp.wait_ge(kv_ready[u], n)
                    sp.sem_inc(turn, 1)
                    sp.dma_start(rows(T["q3"], r), qs[:, u, :]).then_inc(stored[u], 16)
                    sp.dma_start(rows(T["table3"], r), kv[:, u, :, :].rearrange("p k n -> p (k n)")).then_inc(stored[u], 16)
                    sp.dma_start(rows(T["h3"], r), h[:, u, :]).then_inc(stored[u], 16)

            repeat(sp, NBP // 2, step)
            sp.wait_ge(rel_ready, 1)
            sp.dma_start(T["rel"][:, :], rel[:, :]).then_inc(rel_out, 16)
            sp.wait_ge(rel_out, 16)
            for u in range(2):
                sp.wait_ge(stored[u], 48 * (NBP // 2))

        @block.vector
        def _(dve):
            dve.wait_ge(w_in, 16 * 7)
            dve.tensor_scalar(qe[:, :], qe[:, :], 0.1, None, ALU.mult)
            dve.wait_ge(rel_in, 16)
            dve.tensor_scalar(rel[:, :], rel[:, :], 0.2, None, ALU.mult).then_inc(rel_ready, 1)
            dve.drain()

            def step(i):
                n, n16 = snap(dve, i + 1), snap(dve, (i + 1) * 16)
                for u in range(2):
                    dve.wait_ge(x_in[u], n16)
                    dve.sem_inc(turn, 1)
                    at_least(dve, stored[u], snap(dve, i * 48))
                    normalise(nc, dve, x[:, u, :], st[:, u, :], mv[:, u, :], h[:, u, :], var_ready[u], root_ready[u], n)
                    dve.tensor_scalar(h[:, u, :], h[:, u, :], 0.0, None, ALU.max)
                    dve.drain()
                    dve.tensor_tensor(en[:, u, :], h[:, u, :], qe[:, :], ALU.add).then_inc(en_ready[u], 1)

            repeat(dve, NBP // 2, step)

        @block.tensor
        def _(pe):
            pe.wait_ge(w_in, 16 * 7)

            def step(i):
                n = snap(pe, i + 1)
                for u in range(2):
                    pe.wait_ge(en_ready[u], n)
                    for c in range(2):
                        last = pe.transpose(pE[u][:, c, :], en[:, u, c * P:(c + 1) * P], K["ident"][:, :])
                    last.then_inc(e_ps[u], 1)
                for u in range(2):
                    pe.wait_ge(eT_ready[u], n)
                    for out, rhs, bias in ((pQ[u][:, 0:D], lambda c: w[:, c, 0, :], b[:, 0, :]),
                                           (pK[u][:, :], lambda c: w[:, c, 1:3, :].rearrange("p k n -> p (k n)"), b[:, 1:3, :].rearrange("p k n -> p (k n)"))):
                        for c in range(2):
                            pe.matmul(out, eT[:, u, c, :], rhs(c), start=(c == 0), stop=False)
                        last = pe.matmul(out, K["ones"][0:1, :], bias, start=False, stop=True)
                    last.then_inc(q_ps[u], 1)

            repeat(pe, NBP // 2, step)

        @block.scalar
        def _(act):
            def step(i):
                n = snap(act, i + 1)
                for u in range(2):
                    root(nc, act, mv[:, u, :], K["eps"], var_ready[u], root_ready[u], n)
                    act.wait_ge(e_ps[u], n)
                    act.activation(eT[:, u, :, :], pE[u][:, 0:2, :], ACT.Copy).then_inc(eT_ready[u], 1)
                for u in range(2):
                    at_least(act, stored[u], snap(act, i * 48))
                    act.wait_ge(q_ps[u], n)
                    act.activation(qs[:, u, :], pQ[u][:, 0:D], ACT.Copy, scale=DK ** -0.5)
                    act.activation(kv[:, u, :, :].rearrange("p k n -> p (k n)"), pK[u][:, :], ACT.Copy).then_inc(kv_ready[u], 1)

            repeat(act, NBP // 2, step)


def output(nc, A, T, K, out):
    with Stage(nc, "fin") as S:
        w = S.sb("w", [P, 2, D])
        bo = S.sb("bo", [1, D])
        gb = S.sb("gb", [P, 2, D])
        ag = S.sb("ag", [P, 2, H, HV])
        v = S.sb("v", [P, 2, D])
        h = S.sb("h", [P, 2, D])
        x = S.sb("x", [P, 2, D])
        rd = S.sb("rd", [P, 2, 2, H])
        a = S.sb("a", [P, 2, D])
        b = S.sb("b", [P, 2, D])
        aT = S.sb("aT", [P, 2, 2, P])
        xo = S.sb("xo", [P, 2, D])
        st = S.sb("st", [P, 2, 6])
        mv = S.sb("mv", [P, 2, 4])
        y = S.sb("y", [P, 2, D])
        pA = [S.ps(f"pA{u}", [P, 4, P]) for u in range(2)]
        pO = [S.ps(f"pO{u}", [P, 512]) for u in range(2)]
        two = lambda k: S.sems_of(k, 2)
        w_in, turn = S.sem("w_in"), S.sem("turn")
        x_in, a_ready, a_ps, aT_ready, o_ps, var_ready, root_ready, y_ready, stored = (
            two(k) for k in ("x_in", "a_ready", "a_ps", "aT_ready", "o_ps", "var_ready", "root_ready", "y_ready", "stored"))
        FULL = N // P
        block = S.block()

        def over_blocks(eng, step):
            repeat(eng, FULL // 2, lambda i: step(i, (0, 1)))
            step(FULL // 2, (0,))

        @block.sync
        def _(sp):
            sp.dma_start(w[:, :, :], A["L3_gnn_Wo"].rearrange("(c p) n -> p c n", p=P)).then_inc(w_in, 16)
            sp.dma_start(bo[:, :], A["L3_gnn_bo"].rearrange("(o n) -> o n", o=1)).then_inc(w_in, 16)
            for j, g in enumerate(("gamma", "beta")):
                sp.dma_start(gb[:, j, :], A[f"L3_gnn_{g}"].rearrange("(o n) -> o n", o=1).to_broadcast([P, D])).then_inc(w_in, 16)

            def step(i, us):
                n = snap(sp, i + 1)
                for u in us:
                    r = snap(sp, (2 * i + u) * P)
                    at_least(sp, y_ready[u], i)
                    sp.sem_inc(turn, 1)
                    sp.dma_start(ag[:, u, :, :].rearrange("p h c -> p (h c)"), rows(T["agg3"], r)).then_inc(x_in[u], 16)
                    sp.dma_start(v[:, u, :], T["table3"][bass.ds(r, P), D:2 * D]).then_inc(x_in[u], 16)
                    sp.dma_start(h[:, u, :], rows(T["h3"], r)).then_inc(x_in[u], 16)
                    sp.dma_start(x[:, u, :], rows(T["x3"], r)).then_inc(x_in[u], 16)
                for u in us:
                    r = snap(sp, (2 * i + u) * P)
                    sp.wait_ge(y_ready[u], n)
                    sp.sem_inc(turn, 1)
                    m = N - FULL * P if isinstance(i, int) and i == FULL // 2 else P
                    sp.dma_start(out[bass.ds(r, m), :], y[0:m, u, :]).then_inc(stored[u], 16)

            over_blocks(sp, step)
            sp.wait_ge(stored[0], 16 * (FULL // 2 + 1))
            sp.wait_ge(stored[1], 16 * (FULL // 2))

        @block.vector
        def _(dve):
            dve.wait_ge(w_in, 64)

            def heads(t, u):
                return t[:, u, :].rearrange("p (h d) -> p h d", h=H)

            def step(i, us):
                n, n64 = snap(dve, i + 1), snap(dve, (i + 1) * 64)
                for u in us:
                    dve.wait_ge(x_in[u], n64)
                    dve.tensor_scalar(rd[:, u, 0, :], ag[:, u, :, DK], 1e-30, None, ALU.max)
                    dve.tensor_scalar(rd[:, u, 1, :], ag[:, u, :, DK], 0.0, None, ALU.is_equal)
                    dve.drain()
                    dve.reciprocal(rd[:, u, 0, :], rd[:, u, 0, :])
                    dve.tensor_tensor(heads(b, u), heads(v, u), rd[:, u, 1, :].unsqueeze(2).to_broadcast([P, H, DK]), ALU.mult)
                    dve.drain()
                    dve.tensor_tensor(heads(a, u), ag[:, u, :, 0:DK], rd[:, u, 0, :].unsqueeze(2).to_broadcast([P, H, DK]), ALU.mult)
                    dve.drain()
                    dve.tensor_tensor(a[:, u, :], a[:, u, :], b[:, u, :], ALU.add).then_inc(a_ready[u], 1)
                for u in us:
                    dve.wait_ge(o_ps[u], n)
                    dve.tensor_tensor(xo[:, u, :], h[:, u, :], pO[u][:, 0:D], ALU.add)
                    dve.drain()
                    normalise(nc, dve, xo[:, u, :], st[:, u, :], mv[:, u, :], xo[:, u, :], var_ready[u], root_ready[u], n)
                    dve.tensor_tensor(xo[:, u, :], xo[:, u, :], gb[:, 0, :], ALU.mult)
                    dve.tensor_tensor(x[:, u, :], x[:, u, :], gb[:, 1, :], ALU.add)
                    dve.drain()
                    at_least(dve, stored[u], snap(dve, i * 16))
                    dve.tensor_tensor(y[:, u, :], xo[:, u, :], x[:, u, :], ALU.add).then_inc(y_ready[u], 1)

            over_blocks(dve, step)

        @block.tensor
        def _(pe):
            pe.wait_ge(w_in, 64)

            def step(i, us):
                n = snap(pe, i + 1)
                for u in us:
                    pe.wait_ge(a_ready[u], n)
                    for c in range(2):
                        last = pe.transpose(pA[u][:, c, :], a[:, u, c * P:(c + 1) * P], K["ident"][:, :])
                    last.then_inc(a_ps[u], 1)
                for u in us:
                    pe.wait_ge(aT_ready[u], n)
                    for c in range(2):
                        pe.matmul(pO[u][:, 0:D], aT[:, u, c, :], w[:, c, :], start=(c == 0), stop=False)
                    pe.matmul(pO[u][:, 0:D], K["ones"][0:1, :], bo[:, :], start=False, stop=True).then_inc(o_ps[u], 1)

            over_blocks(pe, step)

        @block.scalar
        def _(act):
            def step(i, us):
                n = snap(act, i + 1)
                for u in us:
                    act.wait_ge(a_ps[u], n)
                    act.activation(aT[:, u, :, :], pA[u][:, 0:2, :], ACT.Copy).then_inc(aT_ready[u], 1)
                for u in us:
                    root(nc, act, mv[:, u, :], K["eps"], var_ready[u], root_ready[u], n)

            over_blocks(act, step)


SCRATCH = {"x0": ([NP, D], F32), "rec": ([EP, 4], I32), "tmask": ([NP, 2 * NT], F32), "itemf": ([NI, 4], F32), "rdego": ([NP, 1], F32),
           "q0": ([NP, D], F32), "table0": ([NP * R8, 2 * D], F32), "agg0": ([NP, H * HV], F32),
           "x1": ([NP, D], F32), "table1": ([NP, D + 2 * H], F32), "tablel": ([NP, H], F32),
           "x2": ([NP, D], F32), "h2": ([NP, D], F32), "table2": ([NP, D], F32), "agg2": ([NP, D + 1], F32),
           "xx": ([NP, D], F32), "route": ([NP, 8], F32), "slot": ([NP, 2], I32), "gates": ([NP, 2], F32),
           "xslot": ([SLOTS + P, D], F32), "yslot": ([SLOTS + P, D], F32), "x3": ([NP, D], F32), "h3": ([NP, D], F32),
           "q3": ([NP, D], F32), "table3": ([NP, 2 * D], F32), "rel": ([R64, DK], F32), "agg3": ([NP, H * HV], F32)}
DEBUG = False


def build(nc, A, out):
    ctx = ExitStack()
    with ctx:
        T = {k: nc.dram_tensor(f"t_{k}", s, d, **({"kind": "ExternalOutput"} if DEBUG else {})).ap() for k, (s, d) in SCRATCH.items()}
        sb = lambda name, shape, dt=F32: ctx.enter_context(nc.sbuf_tensor(f"k_{name}", shape, dt))
        K = {"ident": sb("ident", [P, P]), "ones": sb("ones", [P, P]), "upper": sb("upper", [P, P]), "iota": sb("iota", [P, P]),
             "eps": sb("eps", [P, 1]), "items": sb("items", [1, 2, NI], I32),
             "count": sb("count", [EX, 1]), "tiles": sb("tiles", [1, NTILE], I32)}
        prepare(nc, A, T, K)
        layer0_nodes(nc, A, T, K)
        attention_items(nc, "l0e", T["table0"], 0, T["q0"], T["agg0"], T, K)
        layer1_nodes(nc, A, T, K)
        layer2_nodes(nc, A, T, K)
        sum_items(nc, "l2e", T["table2"], T["agg2"], T, K)
        gate(nc, A, T, K)
        slots(nc, A, T, K)
        dispatch(nc, A, T, K)
        experts(nc, A, T, K)
        combine(nc, A, T, K)
        layer3_nodes(nc, A, T, K)
        attention_items(nc, "l3e", T["table3"], 1, T["q3"], T["agg3"], T, K, rel=T["rel"])
        output(nc, A, T, K, out)


def kernel(**inputs):
    import numpy as _np
    import concourse.bacc as _bacc
    from concourse import mybir as _mybir
    from concourse.bass_utils import run_bass_kernel_spmd as _run

    nc = _bacc.Bacc("TRN2", target_bir_lowering=False, num_devices=1)
    arrays, args = {}, {}
    for name, a in inputs.items():
        a = _np.ascontiguousarray(a)
        arrays[f"in_{name}"] = a
        args[name] = nc.dram_tensor(f"in_{name}", a.shape, _mybir.dt.from_np(a.dtype), kind="ExternalInput").ap()
    out = nc.dram_tensor("out_x", (N, D), _mybir.dt.float32, kind="ExternalOutput").ap()
    build(nc, args, out)
    r = _run(nc, [arrays], core_ids=[0])
    return r.results[0]["out_x"]
```

```python
import concourse.bass as bass
from concourse import mybir
from contextlib import ExitStack, contextmanager

F32, BF16, I32, U32 = mybir.dt.float32, mybir.dt.bfloat16, mybir.dt.int32, mybir.dt.uint32
ALU, ACT, AX = mybir.AluOpType, mybir.ActivationFunctionType, mybir.AxisListType

P = 128
N, E, D = 3125, 103125, 256
H, DK = 4, 64
NT, R8, R64 = 4, 8, 64
NB = -(-N // P)
NBP = NB + 1
NP = NBP * P
G = 4
SL = 6
EW = P * G
EP = E + EW
NI = -(-(E // EW + NB + 1) // SL) * SL
EC = 125
ER = E // EC
PAD_DST = 4000.0
BIG = float(2 ** 100)
HV = DK + 1
EX, HID, CAP = 64, 512, 1024
NTILE = N * 2 // P + EX
SLOTS = NTILE * P
EPS = 1e-5


class Stage:

    def __init__(self, nc, name):
        self.nc, self.name, self.ctx, self.sems = nc, name, ExitStack(), []

    def sb(self, name, shape, dt=F32):
        return self.ctx.enter_context(self.nc.sbuf_tensor(f"{self.name}_{name}", shape, dt))

    def ps(self, name, shape, dt=F32):
        return self.ctx.enter_context(self.nc.psum_tensor(f"{self.name}_{name}", shape, dt))

    def sem(self, name):
        s = self.nc.alloc_semaphore(f"{self.name}_{name}")
        self.sems.append(s)
        return s

    def sems_of(self, name, k):
        return [self.sem(f"{name}{i}") for i in range(k)]

    def block(self):
        return self.blk.enter_context(self.nc.Block())

    def __enter__(self):
        self.ctx.__enter__()
        self.blk = ExitStack()
        return self

    def __exit__(self, *a):
        self.blk.close()
        self.nc.clear_and_free_semaphores(self.sems)
        self.nc.all_engine_barrier()
        return self.ctx.__exit__(*a)


def rows(t, start, count=P):
    return t[bass.ds(start, count), :]


def prepare(nc, A, T, K):
    with Stage(nc, "prep") as S:
        src = S.sb("src", [EC, ER], I32)
        dst = S.sb("dst", [EC, ER], I32)
        t8 = S.sb("t8", [EC, ER], I32)
        t64 = S.sb("t64", [EC, ER], I32)
        rec = S.sb("rec", [EC, ER, 4], I32)
        dstf = S.sb("dstf", [EC, ER])
        junk = S.sb("junk", [EC, ER])
        pad = S.sb("pad", [P, G * 4])
        zero = S.sb("zero", [P, D])
        nty = S.sb("nty", [P, NBP], I32)
        ntf = S.sb("ntf", [P, NBP])
        mask = S.sb("mask", [P, NBP, 2, NT])
        skip = S.sb("skip", [P, NT])
        sig = S.sb("sig", [P, NT])
        cnt = S.sb("cnt", [EC, NBP + 2])
        ones = S.sb("ones", [P, 1])
        off = S.sb("off", [NBP, 2])
        cb = S.sb("cb", [NBP, 1])
        NJ = E // EW + 2
        stepi = S.sb("stepi", [NBP, NJ])
        stepj = S.sb("stepj", [NBP, NJ])
        nit = S.sb("nit", [NBP, 1])
        lower = S.sb("lower", [NBP, NBP])
        istart = S.sb("istart", [NBP, 2])
        itn = S.sb("itn", [NBP, NI])
        sel = S.sb("sel", [NBP, 2, NI])
        val = S.sb("val", [NBP, 3, NI])
        bcol = S.sb("bcol", [NBP, 2])
        row = S.sb("row", [1, 3, NI])
        rowf = S.sb("rowf", [1, NI, 4])
        HG = 15
        lo = S.sb("lo", [EC, ER], I32)
        hi = S.sb("hi", [EC, ER], I32)
        lof = S.sb("lof", [EC, ER])
        hif = S.sb("hif", [EC, ER])
        ohl = S.sb("ohl", [EC, 2, HG, P], BF16)
        ohh = S.sb("ohh", [EC, 2, HG, NBP], BF16)
        dego = S.sb("dego", [P, NBP])
        zb = S.sb("zb", [1, P], BF16)
        pOff = S.ps("pOff", [P, 512])
        pVal = [S.ps(f"pVal{j}", [P, 512]) for j in range(3)]
        pDeg = S.ps("pDeg", [P, 512])
        edges_in, nodes_in, skip_in = S.sem("edges_in"), S.sem("nodes_in"), S.sem("skip_in")
        padded, rec_built = S.sem("padded"), S.sem("rec_built")
        stored, mask_built, sig_done = S.sem("stored"), S.sem("mask_built"), S.sem("sig_done")
        consts, cnt_built, off_ps, nit_built, ist_ps = (S.sem(x) for x in ("consts", "cnt_built", "off_ps", "nit_built", "ist_ps"))
        val_built, val_ps, rows_built = S.sem("val_built"), S.sem("val_ps"), S.sem("rows_built")
        oh_built, oh_used, deg_ps, deg_clip, deg_root, deg_built = (
            S.sems_of("oh_built", 2), S.sems_of("oh_used", 2), S.sem("deg_ps"), S.sem("deg_clip"), S.sem("deg_root"), S.sem("deg_built"))
        HK = ER // HG
        block = S.block()

        @block.sync
        def _(sp):
            for t, a in ((src, A["src"]), (dst, A["dst"]), (t8, A["edge_type_8"]), (t64, A["edge_type_64"])):
                sp.dma_start(t[:, :], a.rearrange("(p t) -> p t", p=EC)).then_inc(edges_in, 16)
            sp.wait_ge(padded, 1)
            with nc.allow_non_contiguous_dma(reason="3125 node types, once"):
                sp.dma_start(nty[:, 0:NB - 1], A["node_type_4"][0:(NB - 1) * P].rearrange("(b p) -> p b", p=P)).then_inc(nodes_in, 16)
                sp.dma_start(nty[0:N - (NB - 1) * P, NB - 1:NB],
                             A["node_type_4"][(NB - 1) * P:N].rearrange("(p o) -> p o", o=1)).then_inc(nodes_in, 16)
            sp.dma_start(skip[:, :], A["L0_gnn_skip"].rearrange("(o t) -> o t", o=1).to_broadcast([P, NT])).then_inc(skip_in, 16)
            sp.dma_start(T["x0"][0:N, :], A["x"][:, :]).then_inc(stored, 16)
            sp.dma_start(T["x0"][N:N + P, :], zero[:, :]).then_inc(stored, 16)
            sp.dma_start(T["x0"][N + P:NP, :], zero[0:NP - N - P, :]).then_inc(stored, 16)
            sp.dma_start(T["rec"][E:EP, :].rearrange("(p g) c -> p (g c)", g=G), pad[:, :].bitcast(I32)).then_inc(stored, 16)
            sp.dma_start(T["xslot"].rearrange("(b p) n -> p b n", p=P), zero[:, :].unsqueeze(1).to_broadcast([P, NTILE + 1, D])).then_inc(stored, 16)
            sp.wait_ge(rec_built, 1)
            sp.dma_start(T["rec"][0:E, :].rearrange("(p t) c -> p (t c)", p=EC), rec[:, :, :].rearrange("p t c -> p (t c)")).then_inc(stored, 16)
            sp.wait_ge(mask_built, 1)
            with nc.allow_non_contiguous_dma(reason="node-type masks, once"):
                sp.dma_start(T["tmask"].rearrange("(b p) c -> p b c", p=P), mask[:, :, :, :].rearrange("p b k t -> p b (k t)")).then_inc(stored, 16)
            sp.wait_ge(rows_built, 1)
            sp.dma_start(T["itemf"].rearrange("(o i) c -> o (i c)", o=1), rowf[:, :, :].rearrange("o i c -> o (i c)")).then_inc(stored, 16)
            sp.wait_ge(deg_built, 1)
            with nc.allow_non_contiguous_dma(reason="3328 degrees, once"):
                sp.dma_start(T["rdego"].rearrange("(b p) c -> p (b c)", p=P), dego[:, :]).then_inc(stored, 16)
            sp.wait_ge(stored, 16 * 9)

        @block.gpsimd
        def _(pool):
            pool.memset(zero[:, :], 0.0)
            pool.memset(pad[:, :], 0.0)
            pool.drain()
            pool.memset(pad[:, :].rearrange("p (g c) -> p g c", c=4)[:, :, 2:3], PAD_DST)
            pool.memset(nty[:, :], -1)
            pool.drain().then_inc(padded, 1)
            pool.iota(stepi[:, :].bitcast(I32), pattern=[[EW, NJ]], base=0, channel_multiplier=0)
            pool.iota(itn[:, :].bitcast(I32), pattern=[[1, NI]], base=0, channel_multiplier=0)
            pool.iota(bcol[:, 0:1].bitcast(I32), pattern=[[0, 1]], base=0, channel_multiplier=P)
            pool.memset(ones[:, :], 1.0)
            pool.memset(lower[:, :], 1.0)
            pool.memset(K["ident"][:, :], 0.0)
            pool.memset(K["ones"][:, :], 1.0)
            pool.memset(K["upper"][:, :], 1.0)
            pool.iota(K["iota"][:, :].bitcast(I32), pattern=[[1, P]], base=0, channel_multiplier=0)
            pool.memset(K["eps"][:, :], EPS)
            pool.drain()
            pool.affine_select(out=lower[:, :], in_=lower[:, :], compare_op=ALU.is_gt, fill=0.0, base=0, pattern=[[1, NBP]], channel_multiplier=-1)
            pool.affine_select(out=K["upper"][:, :], in_=K["upper"][:, :], compare_op=ALU.is_gt, fill=0.0, base=0, pattern=[[1, P]], channel_multiplier=-1)
            pool.affine_select(out=K["ident"][:, :], in_=K["ident"][:, :], compare_op=ALU.not_equal, fill=1.0, base=0, pattern=[[-1, P]], channel_multiplier=1)
            pool.drain().then_inc(consts, 1)

        @block.scalar
        def _(act):
            act.wait_ge(skip_in, 16)
            act.activation(sig[:, :], skip[:, :], ACT.Sigmoid).then_inc(sig_done, 1)
            act.wait_ge(deg_clip, 1)
            act.activation(dego[:, :], dego[:, :], ACT.Sqrt).then_inc(deg_root, 1)

        @block.tensor
        def _(pe):
            pe.wait_ge(consts, 1)
            pe.wait_ge(cnt_built, 1)
            pe.matmul(pOff[0:NBP, 0:1], cnt[:, 0:NBP], ones[0:EC, :], start=True, stop=True)
            pe.matmul(pOff[0:NBP, 1:2], cnt[:, 1:NBP + 1], ones[0:EC, :], start=True, stop=True).then_inc(off_ps, 1)
            pe.wait_ge(nit_built, 1)
            pe.matmul(pOff[0:NBP, 2:3], lower[:, :], nit[:, :], start=True, stop=True).then_inc(ist_ps, 1)
            pe.wait_ge(val_built, 1)
            for j in range(3):
                last = pe.matmul(pVal[j][0:1, 0:NI], ones[0:NBP, :], val[:, j, :], start=True, stop=True)
            last.then_inc(val_ps, 1)
            pe.matmul(pDeg[:, 0:NBP], zb[:, :], zb[:, 0:NBP], start=True, stop=False)

            def degrees(u, n):
                pe.wait_ge(oh_built[u], n)
                for k in range(HG):
                    last = pe.matmul(pDeg[:, 0:NBP], ohl[:, u, k, :], ohh[:, u, k, :], start=False, stop=False)
                last.then_inc(oh_used[u], 1)

            with pe.Fori(0, HK // 2) as i:
                n = pe.snap(i + 1)
                degrees(0, n)
                degrees(1, n)
            degrees(0, HK // 2 + 1)
            pe.matmul(pDeg[:, 0:NBP], zb[:, :], zb[:, 0:NBP], start=False, stop=True).then_inc(deg_ps, 1)

        @block.vector
        def _(dve):
            dve.memset(zb[:, :], 0.0)
            dve.wait_ge(edges_in, 64)
            recf = rec[:, :, :].bitcast(F32)
            dve.scalar_tensor_tensor(out=rec[:, :, 0], in0=src[:, :], scalar=float(R8), in1=t8[:, :], op0=ALU.mult, op1=ALU.add)
            dve.tensor_copy(rec[:, :, 1], src[:, :])
            dve.tensor_copy(recf[:, :, 2], dst[:, :])
            dve.tensor_copy(recf[:, :, 3], t64[:, :]).then_inc(rec_built, 1)
            dve.tensor_copy(dstf[:, :], dst[:, :])
            dve.drain()
            for b in range(NBP + 1):
                dve.tensor_scalar(junk[:, :], dstf[:, :], float(b * P), 0.0, ALU.is_lt, ALU.add, accum_out=cnt[:, b:b + 1])
                dve.drain()
            dve.sem_inc(cnt_built, 1)
            dve.wait_ge(nodes_in, 32)
            dve.tensor_copy(ntf[:, :], nty[:, :])
            dve.drain()
            for t in range(NT):
                dve.tensor_scalar(mask[:, :, 0, t], ntf[:, :], float(t), None, ALU.is_equal)
            dve.wait_ge(sig_done, 1)
            dve.drain()
            dve.tensor_tensor(mask[:, :, 1, :], mask[:, :, 0, :], sig[:, :].unsqueeze(1).to_broadcast([P, NBP, NT]), ALU.mult).then_inc(mask_built, 1)
            dve.wait_ge(consts, 1)
            dve.wait_ge(off_ps, 1)
            dve.tensor_copy(off[:, :], pOff[0:NBP, 0:2])
            dve.tensor_copy(stepj[:, :], stepi[:, :].bitcast(I32))
            dve.tensor_copy(bcol[:, 1:2], bcol[:, 0:1].bitcast(I32))
            dve.tensor_copy(K["iota"][:, :], K["iota"][:, :].bitcast(I32))
            dve.tensor_copy(sel[:, 0, :], itn[:, :].bitcast(I32))
            dve.tensor_copy(K["identb"][:, :], K["ident"][:, :])
            dve.drain()
            dve.tensor_copy(K["iotab"][:, :], K["iota"][:, :])
            dve.tensor_copy(itn[:, :], sel[:, 0, :])
            dve.tensor_tensor(cb[:, :], off[:, 1:2], off[:, 0:1], ALU.subtract)
            dve.drain()
            dve.tensor_scalar(stepj[:, :], stepj[:, :], cb[:, 0:1], 0.0, ALU.is_lt, ALU.add, accum_out=nit[:, 0:1])
            dve.drain()
            dve.tensor_scalar(nit[:, :], nit[:, :], 1.0, None, ALU.max)
            dve.drain().then_inc(nit_built, 1)
            dve.wait_ge(ist_ps, 1)
            dve.tensor_copy(istart[:, 0:1], pOff[0:NBP, 2:3])
            dve.drain()
            dve.tensor_scalar(istart[:, 1:2], bcol[:, 1:2], float(NB * P), float(NI + 1), ALU.is_ge, ALU.mult)
            dve.drain()
            dve.tensor_tensor(istart[:, 1:2], istart[:, 1:2], istart[:, 0:1], ALU.add)
            dve.drain()
            dve.tensor_tensor(istart[:, 1:2], istart[:, 1:2], nit[:, 0:1], ALU.add)
            dve.drain()
            dve.tensor_scalar(sel[:, 0, :], itn[:, :], istart[:, 0:1], None, ALU.is_ge)
            dve.tensor_scalar(sel[:, 1, :], itn[:, :], istart[:, 1:2], None, ALU.is_lt)
            dve.tensor_scalar(val[:, 0, :], itn[:, :], istart[:, 0:1], float(EW), ALU.subtract, ALU.mult)
            dve.tensor_scalar(val[:, 2, :], itn[:, :], istart[:, 0:1], None, ALU.is_gt)
            dve.drain()
            dve.tensor_tensor(sel[:, 0, :], sel[:, 0, :], sel[:, 1, :], ALU.mult)
            dve.tensor_scalar(val[:, 0, :], val[:, 0, :], off[:, 0:1], float(E), ALU.add, ALU.min)
            dve.drain()
            dve.tensor_tensor(val[:, 0, :], val[:, 0, :], sel[:, 0, :], ALU.mult)
            dve.tensor_scalar(val[:, 1, :], sel[:, 0, :], bcol[:, 1:2], None, ALU.mult)
            dve.tensor_tensor(val[:, 2, :], val[:, 2, :], sel[:, 0, :], ALU.mult)
            dve.drain().then_inc(val_built, 1)
            dve.wait_ge(val_ps, 1)
            for j in range(3):
                dve.tensor_copy(row[:, j, :], pVal[j][0:1, 0:NI])
            dve.drain()
            dve.tensor_copy(K["items"][0:1, 0, :], row[:, 0, :])
            dve.tensor_copy(K["items"][0:1, 1, :], row[:, 1, :])
            dve.tensor_copy(rowf[:, :, 0], row[:, 1, :])
            dve.tensor_copy(rowf[:, :, 1], row[:, 2, :])
            dve.tensor_scalar(rowf[:, :, 2], row[:, 2, :], 1.0, BIG, ALU.subtract, ALU.mult)
            dve.tensor_copy(rowf[:, :, 3], row[:, 2, :])
            dve.drain().then_inc(rows_built, 1)
            dve.tensor_scalar(lo[:, :], src[:, :], P - 1, None, ALU.bitwise_and)
            dve.tensor_scalar(hi[:, :], src[:, :], 7, None, ALU.logical_shift_right)
            dve.drain()
            dve.tensor_copy(lof[:, :], lo[:, :])
            dve.tensor_copy(hif[:, :], hi[:, :])
            dve.drain()

            def onehots(u, c0, free, n):
                if free is not None:
                    dve.wait_ge(oh_used[u], free)
                for out, w, v in ((ohl, P, lof), (ohh, NBP, hif)):
                    last = dve.tensor_tensor(out[:, u, :, :], K["iota"][0:EC, 0:w].unsqueeze(1).to_broadcast([EC, HG, w]),
                                             v[:, bass.ds(c0, HG)].unsqueeze(2).to_broadcast([EC, HG, w]), ALU.is_equal)
                last.then_inc(oh_built[u], 1)

            onehots(0, 0, None, 1)
            onehots(1, HG, None, 1)
            with dve.Fori(1, HK // 2) as i:
                n = dve.snap(i)
                onehots(0, i * (2 * HG), n, None)
                onehots(1, i * (2 * HG) + HG, n, None)
            onehots(0, (HK - 1) * HG, HK // 2, None)
            dve.wait_ge(deg_ps, 1)
            dve.tensor_scalar(dego[:, :], pDeg[:, 0:NBP], 1.0, None, ALU.max).then_inc(deg_clip, 1)
            dve.wait_ge(deg_root, 1)
            dve.reciprocal(dego[:, :], dego[:, :]).then_inc(deg_built, 1)


def at_least(eng, sem, count):
    if not isinstance(count, int) or count > 0:
        eng.wait_ge(sem, count)


def repeat(eng, times, body):
    body(0)
    with eng.Fori(1, times) as i:
        body(i)


def run_ahead(eng, times, body):
    body(0, True)
    with eng.Fori(1, times - 1) as i:
        body(snap(eng, i + 0), True)
    body(times - 1, False)


def snap(eng, v):
    return v if isinstance(v, int) else eng.snap(v)


def normalise(nc, dve, x, stats, mv, out, var_ready, root_ready, n):
    dve.bn_stats(stats, x)
    dve.drain()
    dve.bn_aggr(mv[:, 0:2], stats).then_inc(var_ready, 1)
    dve.wait_ge(root_ready, n)
    dve.reciprocal(mv[:, 2:3], mv[:, 2:3])
    dve.drain()
    dve.tensor_scalar(out, x, mv[:, 0:1], mv[:, 2:3], ALU.subtract, ALU.mult)
    dve.drain()


def root(nc, act, mv, eps, var_ready, root_ready, n):
    act.wait_ge(var_ready, n)
    act.activation(mv[:, 2:3], mv[:, 1:2], ACT.Sqrt, bias=eps[:, 0:1]).then_inc(root_ready, 1)


def split3(dve, parts, rest, x):
    dve.tensor_copy(parts[0], x)
    dve.drain()
    dve.tensor_tensor(rest, x, parts[0], ALU.subtract)
    dve.drain()
    dve.tensor_copy(parts[1], rest)
    dve.drain()
    dve.tensor_tensor(parts[2], rest, parts[1], ALU.subtract)


def layer0_nodes(nc, A, T, K):
    with Stage(nc, "l0n") as S:
        wq, wk, wv = (S.sb(f"w{c}", [P, NT, 2, D]) for c in "qkv")
        ra = S.sb("ra", [DK, 2, R8, 2, DK])
        rk = S.sb("rk", [P, 2, R8, DK])
        rv = S.sb("rv", [P, 2, R8, DK])
        pri = S.sb("pri", [P, 2, R8])
        x = S.sb("x", [P, 2, D])
        mk = S.sb("mk", [P, 2, 2 * NT])
        st = S.sb("st", [P, 2, 6])
        mv = S.sb("mv", [P, 2, 4])
        h = S.sb("h", [P, 2, D])
        hm = S.sb("hm", [P, 2, NT, D])
        hT = S.sb("hT", [P, NT * 2, 2, P])
        qs = S.sb("qs", [P, 2, D])
        q3 = S.sb("q3", [P, 2, 3, D], BF16)
        qr = S.sb("qr", [P, 2, D])
        kv = S.sb("kv", [P, 4, 2, P])
        tab = S.sb("tab", [P, 2, R8, 2, D])
        pT = S.ps("pT", [P, NT * 2, P])
        pQ = S.ps("pQ", [P, 512])
        pKV = S.ps("pKV", [P, 4, 2, P])
        pB = [S.ps(f"pB{j}", [P, R8, DK]) for j in range(2)]
        w_in, ra_in, rk_ps, rk_done = S.sem("w_in"), S.sem("ra_in"), S.sem("rk_ps"), S.sem("rk_done")
        x_in, x_used = S.sems_of("x_in", 2), S.sems_of("x_used", 2)
        var_ready, root_ready = S.sems_of("var_ready", 2), S.sems_of("root_ready", 2)
        hm_ready, t_ps = S.sems_of("hm_ready", 2), S.sems_of("t_ps", 2)
        hT_ready, qkv_ps, kv_ready = (S.sem(k) for k in ("hT_ready", "qkv_ps", "kv_ready"))
        q_split, turn = S.sems_of("q_split", 2), S.sem("turn")
        big_ps, big_out, tab_ready, tab_out = S.sem("big_ps"), S.sem("big_out"), S.sems_of("tab_ready", 2), S.sems_of("tab_out", 2)
        block = S.block()

        @block.sync
        def _(sp):
            for hh in range(2):
                for j in range(2):
                    sp.dma_start(ra[:, j, :, hh, :], A["L0_gnn_relation_att"][:, 2 * j + hh, :, :].rearrange("r d e -> d r e")).then_inc(ra_in, 16)
                    sp.dma_start(rv[hh * DK:(hh + 1) * DK, j, :, :],
                                 A["L0_gnn_relation_msg"][:, 2 * j + hh, :, :].rearrange("r d e -> d r e")).then_inc(ra_in, 16)
                    with nc.allow_non_contiguous_dma(reason="8 x 4 numbers"):
                        sp.dma_start(pri[hh * DK:(hh + 1) * DK, j, :],
                                     A["L0_gnn_relation_pri"][:, 2 * j + hh].rearrange("(o r) -> o r", o=1).to_broadcast([DK, R8])).then_inc(ra_in, 16)
            for w, a in ((wq, "q"), (wk, "k"), (wv, "v")):
                sp.dma_start(w[:, :, :, :].rearrange("p t c n -> p (t c) n"),
                             A[f"L0_gnn_{a}_linears"].rearrange("t (c p) n -> p (t c) n", p=P)).then_inc(w_in, 16)

            def load(i):
                for u in range(2):
                    at_least(sp, x_used[u], i)
                    r = snap(sp, (2 * i + u) * P)
                    sp.dma_start(x[:, u, :], rows(T["x0"], r)).then_inc(x_in[u], 16)
                    sp.dma_start(mk[:, u, :], rows(T["tmask"], r)).then_inc(x_in[u], 16)

            def step(i, more):
                n = snap(sp, i + 1)
                if more:
                    load(n)
                for u in range(2):
                    r = snap(sp, (2 * i + u) * P)
                    sp.wait_ge(tab_ready[u], n)
                    sp.wait_ge(q_split[u], n)
                    sp.sem_inc(turn, 1)
                    sp.dma_start(rows(T["q0"], r), q3[:, u, :, :].rearrange("p j n -> p (j n)")).then_inc(tab_out[u], 16)
                    sp.dma_start(rows(T["table0"].rearrange("(n r) c -> n (r c)", r=R8), r),
                                 tab[:, u, :, :, :].rearrange("p r k c -> p (r k c)")).then_inc(tab_out[u], 16)

            load(0)
            run_ahead(sp, NBP // 2, step)
            for u in range(2):
                sp.wait_ge(tab_out[u], 32 * (NBP // 2))

        @block.vector
        def _(dve):
            dve.wait_ge(ra_in, 16 * 12)
            dve.tensor_scalar(pri[:, :, :], pri[:, :, :], DK ** -0.5, None, ALU.mult)
            dve.drain()
            for j in range(2):
                dve.wait_ge(rk_ps, j + 1)
                last = dve.tensor_tensor(rk[:, j, :, :], pB[j][:, :, :], pri[:, j, :].unsqueeze(2).to_broadcast([P, R8, DK]), ALU.mult)
                last.then_inc(rk_done, 1)

            def masked(i):
                for u in range(2):
                    dve.wait_ge(x_in[u], snap(dve, (i + 1) * 32))
                    normalise(nc, dve, x[:, u, :], st[:, u, :], mv[:, u, :], h[:, u, :], var_ready[u], root_ready[u], snap(dve, i + 1))
                    at_least(dve, t_ps[u], i)
                    for t in range(NT):
                        last = dve.tensor_scalar(hm[:, u, t, :], h[:, u, :], 0.0, mk[:, u, t:t + 1], ALU.max, ALU.mult)
                    last.then_inc(hm_ready[u], 1)
                    dve.drain().then_inc(x_used[u], 1)

            def step(i, more):
                n = snap(dve, i + 1)
                if more:
                    masked(n)
                for u in range(2):
                    at_least(dve, tab_out[u], snap(dve, i * 32))
                    dve.wait_ge(kv_ready, n)
                    split3(dve, [q3[:, u, j, :] for j in range(3)], qr[:, u, :], qs[:, u, :])
                    dve.drain().then_inc(q_split[u], 1)

            masked(0)
            run_ahead(dve, NBP // 2, step)

        @block.tensor
        def _(pe):
            pe.wait_ge(ra_in, 16 * 12)
            for j in range(2):
                for r in range(R8):
                    last = pe.transpose(pB[j][:, r, :], ra[:, j, r, :, :].rearrange("p a e -> p (a e)"), K["ident"][0:DK, 0:DK])
                last.then_inc(rk_ps, 1)
            pe.wait_ge(w_in, 48)
            pe.wait_ge(rk_done, 2)

            def turn_rows(i):
                for u in range(2):
                    pe.wait_ge(hm_ready[u], snap(pe, i + 1))
                    at_least(pe, hT_ready, snap(pe, 2 * i + u))
                    for c in range(2 * NT):
                        last = pe.transpose(pT[:, c, :], hm[:, u, c // 2, (c % 2) * P:(c % 2 + 1) * P], K["ident"][:, :])
                    last.then_inc(t_ps[u], 1)

            def step(i, more):
                n = snap(pe, i + 1)
                pe.wait_ge(hT_ready, snap(pe, 2 * i + 2))
                for u in range(2):
                    for c in range(2 * NT):
                        pe.matmul(pQ[:, u * D:(u + 1) * D], hT[:, c, u, :], wq[:, c // 2, c % 2, :], start=(c == 0), stop=(c == 2 * NT - 1))
                for o, w in ((0, wk), (2, wv)):
                    for j in range(2):
                        for c in range(2 * NT):
                            last = pe.matmul(pKV[:, o + j, :, :].rearrange("p u n -> p (u n)"), w[:, c // 2, c % 2, j * P:(j + 1) * P],
                                             hT[:, c, :, :].rearrange("p u n -> p (u n)"), start=(c == 0), stop=(c == 2 * NT - 1))
                last.then_inc(qkv_ps, 1)
                if more:
                    turn_rows(n)
                pe.wait_ge(kv_ready, n)
                for u in range(2):
                    for c in range(8):
                        k, j, hh = c // 4, c // 2 % 2, c % 2
                        at_least(pe, big_out, snap(pe, i * 16 + (u * 8 + c - 1)))
                        pe.matmul(pB[c % 2][:, :, :].rearrange("p r d -> p (r d)"), kv[hh * DK:(hh + 1) * DK, 2 * k + j, u, :],
                                  (rk, rv)[k][hh * DK:(hh + 1) * DK, j, :, :].rearrange("p r d -> p (r d)"), start=True, stop=True).then_inc(big_ps, 1)

            turn_rows(0)
            run_ahead(pe, NBP // 2, step)

        @block.scalar
        def _(act):
            def roots(i):
                for u in range(2):
                    root(nc, act, mv[:, u, :], K["eps"], var_ready[u], root_ready[u], snap(act, i + 1))

            def turned(i):
                for u in range(2):
                    act.wait_ge(t_ps[u], snap(act, i + 1))
                    act.activation(hT[:, :, u, :], pT[:, :, :], ACT.Copy).then_inc(hT_ready, 1)

            def step(i, more):
                n = snap(act, i + 1)
                if more:
                    roots(n)
                for u in range(2):
                    at_least(act, q_split[u], i)
                act.wait_ge(qkv_ps, n)
                act.activation(qs[:, :, :].rearrange("p u n -> p (u n)"), pQ[:, :], ACT.Copy)
                act.activation(kv[:, :, :, :], pKV[:, :, :, :], ACT.Copy).then_inc(kv_ready, 1)
                if more:
                    turned(n)
                for u in range(2):
                    at_least(act, tab_out[u], snap(act, i * 32))
                    for c in range(8):
                        k, hd = c // 4, c % 4
                        act.wait_ge(big_ps, snap(act, i * 16 + (u * 8 + c + 1)))
                        act.activation(tab[:, u, :, k, hd * DK:(hd + 1) * DK], pB[c % 2][:, :, :], ACT.Copy).then_inc(big_out, 1)
                    act.wait_ge(big_out, snap(act, i * 16 + (u * 8 + 8)))
                    act.sem_inc(tab_ready[u], 1)

            roots(0)
            turned(0)
            run_ahead(act, NBP // 2, step)


def attention_items(nc, name, table, ridx, q, agg, T, K, rel=None):
    with Stage(nc, name) as S:
        rec = S.sb("rec", [P, SL, G, 4], I32)
        itf = S.sb("itf", [P, SL, 4])
        qb = S.sb("qb", [P, SL, 3, D], BF16)
        kv = S.sb("kv", [P, SL, G, 2 * D])
        dl = S.sb("dl", [P, SL, G, H])
        oh = S.sb("oh", [P, SL, G, P], BF16)
        ohf = S.sb("ohf", [P, SL, G, P])
        ohT = S.sb("ohT", [P, SL, G, P], BF16)
        dT = S.sb("dT", [G * H, SL, P])
        pen = S.sb("pen", [G * H, SL, P + 1])
        prod = S.sb("prod", [P, G, D])
        sc = S.sb("sc", [P, SL, G, H])
        run = S.sb("run", [G * H, P])
        fl = S.sb("fl", [G * H, SL, 2, P], BF16)
        flT = S.sb("flT", [P, 2, G, H], BF16)
        crow = S.sb("crow", [1, G, 2, H], BF16)
        oneb = S.sb("oneb", [1, P], BF16)
        miss = S.sb("miss", [P, G, H])
        cand = S.sb("cand", [P, SL, H, G + 1])
        mx = S.sb("mx", [P, SL, H])
        mxb = S.sb("mxb", [P, H], BF16)
        df = S.sb("df", [P, H])
        fac = S.sb("fac", [P, SL, H])
        z = S.sb("z", [P, G, H])
        vw = S.sb("vw", [P, SL, G, H, HV])
        part = S.sb("part", [P, H, HV])
        acc = S.sb("acc", [P, SL, H, HV])
        pOT = S.ps("pOT", [P, 2 * G, P], BF16)
        pQE = [S.ps(f"pQE{j}", [P, G, D]) for j in range(2)]
        pC = S.ps("pC", [P, 512])
        pS = pC[0:G * H, 0:P]
        pFL = pC[:, 256:256 + G * H].bitcast(BF16).rearrange("p (k g h) -> p k g h", k=2, g=G)
        pM = pC[:, 320:320 + 2 * G * H].rearrange("p (g k h) -> p g k h", k=2, g=G)
        pSh = pC[:, 384:384 + G * H].rearrange("p (g h) -> p g h", g=G)
        pA = S.ps("pA", [P, 512])
        pD = S.ps("pD", [P, 512])
        in_ready, kv_ready, stored = (S.sems_of(k, SL) for k in ("in_ready", "kv_ready", "stored"))
        dl_done, oh_ready, oh_ps, ohT_ready, qe_ps = (S.sem(k) for k in ("dl_done", "oh_ready", "oh_ps", "ohT_ready", "qe_ps"))
        key_done, prod_done, sc_ready, s_ps, pen_done, last_done = (S.sem(k) for k in ("key_done", "prod_done", "sc_ready", "s_ps", "pen_done", "last_done"))
        run_done, fl_ready, fl_ps, flT_ready, m_ps = (S.sem(k) for k in ("run_done", "fl_ready", "fl_ps", "flT_ready", "m_ps"))
        miss_done, cand_done, mx_done, mx_ready, df_ready = (S.sem(k) for k in ("miss_done", "cand_done", "mx_done", "mx_ready", "df_ready"))
        sh_ps, z_ready, w_ready, vw_ready, vwa_ready = (S.sem(k) for k in ("sh_ps", "z_ready", "w_ready", "vw_ready", "vwa_ready"))
        fac_ready, part_done, a_ps, item_done = (S.sem(k) for k in ("fac_ready", "part_done", "a_ps", "item_done"))
        consts, turn = S.sem("consts"), S.sem("turn")
        AW = 3
        if rel is not None:
            ohr_ready = S.sem("ohr_ready")
            relw = S.sb("relw", [R64, 3, DK], BF16)
            ohr = S.sb("ohr", [P, SL, G, R64], BF16)
            ohrT = S.sb("ohrT", [R64, SL, G, P], BF16)
            pR = pD[:, 256:512].rearrange("p (g d) -> p g d", g=G)
        block = S.block()
        KI = NI // SL
        LEAD = 2

        def over_items(eng, step):
            for s in range(SL):
                step(s, 0, s, SL)
            with eng.Fori(1, KI - 1) as k:
                kk = snap(eng, k + 0)
                for s in range(SL):
                    step(s, kk, k * SL + s, SL)
            for s in range(SL):
                step(s, KI - 1, (KI - 1) * SL + s, SL - 1 - s)

        def later(s, k, d=1):
            return ((s + d) % SL, k + (s + d) // SL)

        def need(eng, sem, s, k, per=1):
            if isinstance(sem, list):
                at_least(eng, sem[s], snap(eng, (k + 1) * per))
            else:
                at_least(eng, sem, snap(eng, k * SL + (s + 1)))

        def is_before_first(k):
            return isinstance(k, int) and k < 0

        @block.sync
        def _(sp):
            if rel is not None:
                sp.dma_start(relw[:, :, :].rearrange("p j d -> p (j d)"), rel[:, :]).then_inc(consts, 16)

            def load(s, k, i):
                e0 = sp.value_load(K["items"][0:1, 0, bass.ds(i, 1)], min_val=0, max_val=E)
                b0 = sp.value_load(K["items"][0:1, 1, bass.ds(i, 1)], min_val=0, max_val=NB * P)
                need(sp, item_done, s, k - 1)
                sp.sem_inc(turn, 1)
                sp.dma_start(rec[:, s, :, :].rearrange("p g c -> p (g c)"),
                             T["rec"][bass.ds(e0, EW), :].rearrange("(p g) c -> p (g c)", g=G)).then_inc(in_ready[s], 16)
                sp.dma_start(itf[:, s, :], T["itemf"][bass.ds(i, 1), :].to_broadcast([P, 4])).then_inc(in_ready[s], 16)
                sp.dma_start(qb[:, s, :, :].rearrange("p j n -> p (j n)"), q[bass.ds(b0, P), :]).then_inc(in_ready[s], 16)

            for s in range(SL):
                load(s, 0, s)

            def step(s, k, i, left):
                b0 = sp.value_load(K["items"][0:1, 1, bass.ds(i, 1)], min_val=0, max_val=NB * P)
                ps, pk = later(s, k, -1)
                mine, before = snap(sp, k * SL + (s + 1)), snap(sp, (pk + 1) * 16)
                at_least(sp, item_done, mine)
                sp.sem_inc(turn, 1)
                at_least(sp, stored[ps], before)
                sp.sem_inc(turn, 1)
                sp.dma_start(agg[bass.ds(b0, P), :], acc[:, s, :, :].rearrange("p h c -> p (h c)")).then_inc(stored[s], 16)
                if not (isinstance(k, int) and k == KI - 1):
                    load(s, k + 1, i + SL)

            over_items(sp, step)
            sp.wait_ge(stored[SL - 1], 16 * KI)

        @block.gpsimd
        def _(pool):
            pool.memset(pen[:, :, 0:1], -BIG)
            pool.memset(pen[:, :, P:P + 1], -BIG)
            pool.memset(crow[:, :, 0, :], 0.0)
            pool.memset(crow[:, :, 1, :], -1.0)
            pool.memset(oneb[:, :], 1.0)
            pool.memset(acc[:, SL - 1, :, :], 0.0)
            pool.memset(mx[:, SL - 1, :], 0.0)
            pool.drain().then_inc(consts, 16)

            def step(s, k, i, left):
                need(pool, in_ready, s, k, 48)
                pool.sem_inc(turn, 1)
                recf = rec[:, s, :, :].bitcast(F32)
                pool.tensor_scalar(dl[:, s, :, :], recf[:, :, 2:3].to_broadcast([P, G, H]), itf[:, s, 0:1], None, ALU.subtract).then_inc(dl_done, 1)
                if rel is not None:
                    for g in range(G):
                        last = pool.tensor_scalar(ohr[:, s, g, :], K["iotab"][:, 0:R64], recf[:, g, 3:4], None, ALU.is_equal)
                    last.then_inc(ohr_ready, 1)
                for g in range(G):
                    pool.indirect_dma_start(kv[:, s, g, :], None, table[:, :],
                                            bass.IndirectOffsetOnAxis(ap=rec[:, s, g, ridx:ridx + 1], axis=0)).then_inc(kv_ready[s], 16)

            over_items(pool, step)

        @block.vector
        def _(dve):
            dve.wait_ge(consts, 16 + 16 * (rel is not None))

            def onehot(s, k, g):
                if g == 0:
                    need(dve, dl_done, s, k)
                last = dve.tensor_scalar(oh[:, s, g, :], K["iotab"][:, :], dl[:, s, g, 0:1], None, ALU.is_equal)
                if g == G - 1:
                    last.then_inc(oh_ready, 1)

            AT_RUN, AT_MISS, AT_CAND, AT_END = ((0, 1), (2,), (3,), ()) if rel is None else ((), (0,), (1,), (2, 3))

            def onehots_ahead(s, k, left, tiles):
                if left > LEAD:
                    for g in tiles:
                        onehot(*later(s, k, LEAD + 1), g)

            def penalties(s, k):
                need(dve, ohT_ready, s, k)
                dve.tensor_tensor(pen[:, s, 1:P], dT[:, s, 0:P - 1], dT[:, s, 1:P], ALU.subtract).then_inc(pen_done, 1)

            def run_ends(s, k):
                need(dve, pen_done, s, k)
                dve.tensor_scalar(fl[:, s, 1, :], pen[:, s, 1:P + 1], 0.0, None, ALU.is_lt).then_inc(last_done, 1)

            def keys(s, k):
                need(dve, kv_ready, s, k, 16 * G)
                need(dve, qe_ps, s, k)
                if rel is not None:
                    key = kv[:, s, :, 0:D].rearrange("p g (h d) -> p g h d", h=H)
                    dve.tensor_tensor(key, key, pR.unsqueeze(2).to_broadcast([P, G, H, DK]), ALU.add).then_inc(key_done, 1)

            def products(s, k):
                if rel is not None:
                    need(dve, key_done, s, k)
                dve.tensor_tensor(prod[:, :, :], pQE[s % 2][:, :, :], kv[:, s, :, 0:D], ALU.mult).then_inc(prod_done, 1)

            def scores(s, k):
                need(dve, prod_done, s, k)
                dve.tensor_reduce(sc[:, s, :, :], prod[:, :, :].rearrange("p g (h d) -> p g h d", h=H), AX.X, ALU.add).then_inc(sc_ready, 1)

            def run_max(s, k):
                need(dve, s_ps, s, k)
                need(dve, last_done, s, k)
                dve.tensor_tensor_scan(run[:, :], pen[:, s, 0:P], pS, 0.0, ALU.add, ALU.max).then_inc(run_done, 1)
                need(dve, run_done, s, k)
                dve.scalar_tensor_tensor(out=fl[:, s, 0, :], in0=pen[:, s, 1:P + 1], scalar=0.0, in1=run[:, :], op0=ALU.is_lt, op1=ALU.mult).then_inc(fl_ready, 1)

            def node_max(s, k, left):
                ps, pk = later(s, k, -1)
                dve.tensor_scalar(cand[:, s, :, G], mx[:, ps, :], itf[:, s, 1:2], itf[:, s, 2:3], ALU.mult, ALU.add)
                need(dve, m_ps, s, k)
                dve.tensor_scalar(miss[:, :, :], pM[:, :, 1, :], BIG, None, ALU.mult).then_inc(miss_done, 1)
                onehots_ahead(s, k, left, AT_MISS)
                need(dve, miss_done, s, k)
                dve.tensor_tensor(cand[:, s, :, 0:G].rearrange("p h g -> p g h"), pM[:, :, 0, :], miss[:, :, :], ALU.add).then_inc(cand_done, 1)
                onehots_ahead(s, k, left, AT_CAND)
                need(dve, cand_done, s, k)
                dve.tensor_reduce(mxb[:, :], cand[:, s, :, :], AX.X, ALU.max).then_inc(mx_ready, 1)
                dve.tensor_reduce(mx[:, s, :], cand[:, s, :, :], AX.X, ALU.max).then_inc(mx_done, 1)
                if left:
                    penalties(*later(s, k))
                need(dve, mx_done, s, k)
                dve.tensor_tensor(df[:, :], cand[:, s, :, G], mx[:, s, :], ALU.subtract).then_inc(df_ready, 1)
                if left:
                    run_ends(*later(s, k))
                onehots_ahead(s, k, left, AT_END)

            def shifted(s, k):
                need(dve, sh_ps, s, k)
                dve.tensor_tensor(z[:, :, :], sc[:, s, :, :], pSh, ALU.subtract).then_inc(z_ready, 1)

            def weigh(s, k):
                need(dve, w_ready, s, k)
                dve.tensor_tensor(vw[:, s, AW:G, :, 0:DK], kv[:, s, AW:G, D:2 * D].rearrange("p g (h d) -> p g h d", h=H),
                                  vw[:, s, AW:G, :, DK:HV].to_broadcast([P, G - AW, H, DK]), ALU.mult).then_inc(vw_ready, 1)

            def rescale(s, k):
                ps, pk = later(s, k, -1)
                need(dve, fac_ready, s, k)
                need(dve, item_done, ps, pk)
                dve.tensor_tensor(part[:, :, :], acc[:, ps, :, :], fac[:, s, :].unsqueeze(2).to_broadcast([P, H, HV]), ALU.mult).then_inc(part_done, 1)

            def merge(s, k):
                need(dve, part_done, s, k)
                need(dve, a_ps, s, k)
                need(dve, stored, s, k - 1, 16)
                dve.tensor_tensor(acc[:, s, :, :], part[:, :, :], pA[:, 0:H * HV].rearrange("p (h c) -> p h c", h=H), ALU.add).then_inc(item_done, 1)

            for d in range(LEAD + 1):
                for g in range(G):
                    onehot(d, 0, g)
            keys(0, 0)
            products(0, 0)
            scores(0, 0)
            penalties(0, 0)
            run_ends(0, 0)

            def step(s, k, i, left):
                before = later(s, k, -1)
                first = is_before_first(before[1])
                run_max(s, k)
                onehots_ahead(s, k, left, AT_RUN)
                if left:
                    keys(*later(s, k))
                need(dve, fl_ps, s, k)
                dve.tensor_copy(flT[:, :, :, :], pFL).then_inc(flT_ready, 1)
                if left:
                    products(*later(s, k))
                node_max(s, k, left)
                shifted(s, k)
                if not first:
                    rescale(*before)
                if left:
                    scores(*later(s, k))
                if not first:
                    merge(*before)
                weigh(s, k)

            over_items(dve, step)
            rescale(SL - 1, KI - 1)
            merge(SL - 1, KI - 1)

        @block.tensor
        def _(pe):
            pe.wait_ge(consts, 16 + 16 * (rel is not None))

            def turn_onehots(s, k):
                need(pe, oh_ready, s, k)
                if rel is not None:
                    need(pe, ohr_ready, s, k)
                pe.transpose(pD[0:G * H, 0:P], dl[:, s, :, :].rearrange("p g h -> p (g h)"), K["ident"][:, :])
                if rel is not None:
                    for g in range(G):
                        pe.transpose(pOT[0:R64, G + g, :], ohr[:, s, g, :], K["identb"][:, :])
                for g in range(G):
                    last = pe.transpose(pOT[:, g, :], oh[:, s, g, :], K["identb"][:, :])
                last.then_inc(oh_ps, 1)

            def queries(s, k):
                need(pe, ohT_ready, s, k)
                if rel is not None:
                    for g in range(G):
                        for j in range(3):
                            pe.matmul(pR[:, g, :], ohrT[:, s, g, :], relw[:, j, :], start=(j == 0), stop=(j == 2))
                for g in range(G):
                    for j in range(3):
                        last = pe.matmul(pQE[s % 2][:, g, :], ohT[:, s, g, :], qb[:, s, j, :], start=(j == 0), stop=(j == 2))
                last.then_inc(qe_ps, 1)

            def turn_scores(s, k):
                need(pe, sc_ready, s, k)
                pe.transpose(pS, sc[:, s, :, :].rearrange("p g h -> p (g h)"), K["ident"][:, :]).then_inc(s_ps, 1)

            def sums(s, k, g0, g1):
                need(pe, vw_ready, s, k)
                need(pe, vwa_ready, s, k)
                ps, pk = later(s, k, -1)
                need(pe, item_done, ps, pk)
                for g in range(g0, g1):
                    last = pe.matmul(pA[:, 0:H * HV], ohf[:, s, g, :], vw[:, s, g, :, :].rearrange("p h c -> p (h c)"), start=(g == 0), stop=(g == G - 1))
                if g1 == G:
                    last.then_inc(a_ps, 1)

            for d in range(LEAD):
                if rel is not None and d > 0:
                    need(pe, key_done, d - 1, 0)
                turn_onehots(d, 0)
                queries(d, 0)
            turn_scores(0, 0)

            def step(s, k, i, left):
                before = later(s, k, -1)
                first = is_before_first(before[1])
                need(pe, fl_ready, s, k)
                pe.sem_inc(turn, 1)
                for j in range(2):
                    last = pe.transpose(pFL[:, j, :, :].rearrange("p g h -> p (g h)"), fl[:, s, j, :], K["identb"][0:G * H, 0:G * H])
                last.then_inc(fl_ps, 1)
                if left >= LEAD and rel is None:
                    turn_onehots(*later(s, k, LEAD))
                if not first:
                    sums(*before, 0, 1)
                need(pe, flT_ready, s, k)
                pe.matmul(pM.rearrange("p g k h -> p (g k h)"), oneb[:, :], crow[:, :, :, :].rearrange("p g k h -> p (g k h)"), start=True, stop=False)
                for g in range(G):
                    last = pe.matmul(pM[:, g, :, :], oh[:, s, g, :], flT[:, :, g, :], start=False, stop=(g == G - 1))
                last.then_inc(m_ps, 1)
                if left >= LEAD and rel is not None:
                    need(pe, key_done, *later(s, k))
                    turn_onehots(*later(s, k, LEAD))
                if not first:
                    sums(*before, 1, G - 1)
                need(pe, mx_ready, s, k)
                for g in range(G):
                    last = pe.matmul(pSh[:, g, :], ohT[:, s, g, :], mxb[:, :], start=True, stop=True)
                last.then_inc(sh_ps, 1)
                if not first:
                    sums(*before, G - 1, G)
                if left >= LEAD:
                    queries(*later(s, k, LEAD))
                if left:
                    turn_scores(*later(s, k))

            over_items(pe, step)
            sums(SL - 1, KI - 1, 0, G)

        @block.scalar
        def _(act):
            def turned(s, k):
                need(act, oh_ps, s, k)
                if rel is not None:
                    act.activation(ohrT[:, s, :, :], pOT[0:R64, G:2 * G, :], ACT.Copy)
                act.activation(dT[:, s, :], pD[0:G * H, 0:P], ACT.Copy, scale=BIG)
                act.activation(ohT[:, s, :, :], pOT[:, 0:G, :], ACT.Copy).then_inc(ohT_ready, 1)

            for d in range(LEAD):
                turned(d, 0)

            def step(s, k, i, left):
                if left >= LEAD and rel is None:
                    turned(*later(s, k, LEAD))
                act.activation(ohf[:, s, :, :], oh[:, s, :, :], ACT.Copy)
                if left >= LEAD and rel is not None:
                    turned(*later(s, k, LEAD))
                need(act, df_ready, s, k)
                act.activation(fac[:, s, :], df[:, :], ACT.Exp).then_inc(fac_ready, 1)
                need(act, z_ready, s, k)
                act.activation(vw[:, s, :, :, DK:HV].rearrange("p g h o -> p g (h o)"), z[:, :, :], ACT.Exp).then_inc(w_ready, 1)
                need(act, w_ready, s, k)
                for g in range(AW):
                    for h in range(H):
                        last = act.activation(vw[:, s, g, h, 0:DK], kv[:, s, g, D + h * DK:D + (h + 1) * DK], ACT.Copy, scale=vw[:, s, g, h, DK:HV])
                last.then_inc(vwa_ready, 1)

            over_items(act, step)


def layer1_nodes(nc, A, T, K):
    WX = D + 2 * H
    with Stage(nc, "l1n") as S:
        wa = S.sb("wa", [P, NT, 2, D])
        wx = S.sb("wx", [P, 2, WX])
        att = S.sb("att", [P, 2, D])
        wtmp = S.sb("wtmp", [P, 2, 2, D])
        ag = S.sb("ag", [P, 2, H, HV])
        x = S.sb("x", [P, 2, D])
        mk = S.sb("mk", [P, 2, 2 * NT])
        rden = S.sb("rden", [P, 2, H])
        coef = S.sb("coef", [P, 2, NT, H])
        am = S.sb("am", [P, 2, NT, H, DK])
        aT = S.sb("aT", [P, 2, NT * 2, P])
        x1 = S.sb("x1", [P, 2, D])
        st = S.sb("st", [P, 2, 6])
        mv = S.sb("mv", [P, 2, 4])
        h = S.sb("h", [P, 2, D])
        hT = S.sb("hT", [P, 2, 2, P])
        tb = S.sb("tb", [P, 2, WX])
        pT = S.ps("pT", [P, NT * 2, P])
        pO = [S.ps(f"pO{u}", [P, 512]) for u in range(2)]
        pH = S.ps("pH", [P, 4, P])
        pX = [S.ps(f"pX{u}", [P, 512]) for u in range(2)]
        w_in, wx_ready, turn = S.sem("w_in"), S.sem("wx_ready"), S.sem("turn")
        two = lambda k: S.sems_of(k, 2)
        x_in, x_used, am_ready, t_ps, aT_ready, o_ps, x1_ready = (two(k) for k in ("x_in", "x_used", "am_ready", "t_ps", "aT_ready", "o_ps", "x1_ready"))
        var_ready, root_ready, h_ready, h_ps, hT_ready, x_ps, tb_ready, stored = (
            two(k) for k in ("var_ready", "root_ready", "h_ready", "h_ps", "hT_ready", "x_ps", "tb_ready", "stored"))
        block = S.block()

        @block.sync
        def _(sp):
            sp.dma_start(wa[:, :, :, :].rearrange("p t c n -> p (t c) n"), A["L0_gnn_a_linears"].rearrange("t (c p) n -> p (t c) n", p=P)).then_inc(w_in, 16)
            sp.dma_start(wx[:, :, 0:D], A["L1_gnn_weight"].rearrange("(c p) n -> p c n", p=P)).then_inc(w_in, 16)
            for j, a in enumerate(("L1_gnn_attn_l", "L1_gnn_attn_r")):
                sp.dma_start(att[:, j, :], A[a].rearrange("(o h) d -> o (h d)", o=1).to_broadcast([P, D])).then_inc(w_in, 16)

            def load(i):
                for u in range(2):
                    r = snap(sp, (2 * i + u) * P)
                    at_least(sp, x_used[u], i)
                    sp.sem_inc(turn, 1)
                    sp.dma_start(x[:, u, :], rows(T["x0"], r)).then_inc(x_in[u], 16)
                    sp.dma_start(mk[:, u, :], rows(T["tmask"], r)).then_inc(x_in[u], 16)
                    sp.dma_start(ag[:, u, :, :].rearrange("p h c -> p (h c)"), rows(T["agg0"], r)).then_inc(x_in[u], 16)

            def step(i, more):
                n = snap(sp, i + 1)
                if more:
                    load(n)
                for u in range(2):
                    r = snap(sp, (2 * i + u) * P)
                    sp.wait_ge(x1_ready[u], n)
                    sp.sem_inc(turn, 1)
                    sp.dma_start(rows(T["x1"], r), x1[:, u, :]).then_inc(stored[u], 16)
                for u in range(2):
                    r = snap(sp, (2 * i + u) * P)
                    sp.wait_ge(tb_ready[u], n)
                    sp.sem_inc(turn, 1)
                    sp.dma_start(rows(T["table1"], r), tb[:, u, :]).then_inc(stored[u], 16)
                    sp.dma_start(rows(T["tablel"], r), tb[:, u, D:D + H]).then_inc(stored[u], 16)

            load(0)
            run_ahead(sp, NBP // 2, step)
            for u in range(2):
                sp.wait_ge(stored[u], 48 * (NBP // 2))

        @block.vector
        def _(dve):
            dve.wait_ge(w_in, 64)
            for c in range(2):
                for j in range(2):
                    dve.tensor_tensor(wtmp[:, c, j, :], wx[:, c, 0:D], att[:, j, :], ALU.mult)
            dve.drain()
            for c in range(2):
                for j in range(2):
                    last = dve.tensor_reduce(wx[:, c, D + j * H:D + (j + 1) * H], wtmp[:, c, j, :].rearrange("p (h d) -> p h d", h=H), AX.X, ALU.add)
            last.then_inc(wx_ready, 1)

            def step(i):
                n, n48 = snap(dve, i + 1), snap(dve, (i + 1) * 48)
                for u in range(2):
                    dve.wait_ge(x_in[u], n48)
                    dve.tensor_scalar(rden[:, u, :], ag[:, u, :, DK], 1e-30, None, ALU.max)
                    dve.drain()
                    dve.reciprocal(rden[:, u, :], rden[:, u, :])
                    dve.drain()
                    dve.tensor_tensor(coef[:, u, :, :], rden[:, u, :].unsqueeze(1).to_broadcast([P, NT, H]),
                                      mk[:, u, NT:2 * NT].unsqueeze(2).to_broadcast([P, NT, H]), ALU.mult)
                    dve.drain()
                    dve.tensor_tensor(am[:, u, :, :, :], ag[:, u, :, 0:DK].unsqueeze(1).to_broadcast([P, NT, H, DK]),
                                      coef[:, u, :, :].unsqueeze(3).to_broadcast([P, NT, H, DK]), ALU.mult).then_inc(am_ready[u], 1)
                for u in range(2):
                    at_least(dve, stored[u], snap(dve, i * 48))
                    dve.wait_ge(o_ps[u], n)
                    dve.tensor_tensor(x1[:, u, :], x[:, u, :], pO[u][:, 0:D], ALU.add).then_inc(x1_ready[u], 1)
                    dve.drain().then_inc(x_used[u], 1)
                    normalise(nc, dve, x1[:, u, :], st[:, u, :], mv[:, u, :], h[:, u, :], var_ready[u], root_ready[u], n)
                    dve.tensor_scalar(h[:, u, :], h[:, u, :], 0.0, None, ALU.max).then_inc(h_ready[u], 1)

            repeat(dve, NBP // 2, step)

        @block.tensor
        def _(pe):
            pe.wait_ge(w_in, 64)
            pe.wait_ge(wx_ready, 1)

            def step(i):
                n = snap(pe, i + 1)
                for u in range(2):
                    pe.wait_ge(am_ready[u], n)
                    for c in range(2 * NT):
                        last = pe.transpose(pT[:, c, :], am[:, u, c // 2, 2 * (c % 2):2 * (c % 2) + 2, :].rearrange("p h d -> p (h d)"), K["ident"][:, :])
                    last.then_inc(t_ps[u], 1)
                    pe.wait_ge(aT_ready[u], n)
                    for c in range(2 * NT):
                        last = pe.matmul(pO[u][:, 0:D], aT[:, u, c, :], wa[:, c // 2, c % 2, :], start=(c == 0), stop=(c == 2 * NT - 1))
                    last.then_inc(o_ps[u], 1)
                for u in range(2):
                    pe.wait_ge(h_ready[u], n)
                    for c in range(2):
                        last = pe.transpose(pH[:, c, :], h[:, u, c * P:(c + 1) * P], K["ident"][:, :])
                    last.then_inc(h_ps[u], 1)
                    pe.wait_ge(hT_ready[u], n)
                    for c in range(2):
                        last = pe.matmul(pX[u][:, 0:WX], hT[:, u, c, :], wx[:, c, :], start=(c == 0), stop=(c == 1))
                    last.then_inc(x_ps[u], 1)

            repeat(pe, NBP // 2, step)

        @block.scalar
        def _(act):
            def step(i):
                n = snap(act, i + 1)
                for u in range(2):
                    act.wait_ge(t_ps[u], n)
                    act.activation(aT[:, u, :, :], pT[:, :, :], ACT.Copy).then_inc(aT_ready[u], 1)
                for u in range(2):
                    root(nc, act, mv[:, u, :], K["eps"], var_ready[u], root_ready[u], n)
                    act.wait_ge(h_ps[u], n)
                    act.activation(hT[:, u, :, :], pH[:, 0:2, :], ACT.Copy).then_inc(hT_ready[u], 1)
                    at_least(act, stored[u], snap(act, i * 48))
                    act.wait_ge(x_ps[u], n)
                    act.activation(tb[:, u, :], pX[u][:, 0:WX], ACT.Copy).then_inc(tb_ready[u], 1)

            repeat(act, NBP // 2, step)


def layer2_nodes(nc, A, T, K):
    WX = D + 2 * H
    with Stage(nc, "l2n") as S:
        si = S.sb("si", [P, 2, 1], I32)
        di = S.sb("di", [P, 2, 1], I32)
        rd = S.sb("rd", [P, 2, 1])
        x = S.sb("x", [P, 2, D])
        gd = S.sb("gd", [P, 2, WX])
        gs = S.sb("gs", [P, 2, H])
        z = S.sb("z", [P, 2, H])
        al = S.sb("al", [P, 2, H])
        sm = S.sb("sm", [P, 2, 2])
        pr = S.sb("pr", [P, 2, H, DK])
        tm = S.sb("tm", [P, 2, DK])
        x2 = S.sb("x2", [P, 2, D])
        st = S.sb("st", [P, 2, 6])
        mv = S.sb("mv", [P, 2, 4])
        h = S.sb("h", [P, 2, D])
        hs = S.sb("hs", [P, 2, D])
        two = lambda k: S.sems_of(k, 2)
        x_in, x_used, g_in, z_ready, e_ready, var_ready, root_ready, out_ready, stored = (
            two(k) for k in ("x_in", "x_used", "g_in", "z_ready", "e_ready", "var_ready", "root_ready", "out_ready", "stored"))
        turn = S.sem("turn")
        block = S.block()

        @block.sync
        def _(sp):
            def load(i):
                for u in range(2):
                    r = snap(sp, (2 * i + u) * P)
                    at_least(sp, x_used[u], i)
                    sp.sem_inc(turn, 1)
                    sp.dma_start(si[:, u, :], A["src"].rearrange("(n o) -> n o", o=1)[bass.ds(r, P), :]).then_inc(x_in[u], 16)
                    sp.dma_start(di[:, u, :], A["dst"].rearrange("(n o) -> n o", o=1)[bass.ds(r, P), :]).then_inc(x_in[u], 16)
                    sp.dma_start(x[:, u, :], rows(T["x1"], r)).then_inc(x_in[u], 16)
                    sp.dma_start(rd[:, u, :], rows(T["rdego"], r)).then_inc(x_in[u], 16)

            def step(i, more):
                n = snap(sp, i + 1)
                if more:
                    load(n)
                for u in range(2):
                    r = snap(sp, (2 * i + u) * P)
                    sp.wait_ge(out_ready[u], n)
                    sp.sem_inc(turn, 1)
                    sp.dma_start(rows(T["x2"], r), x2[:, u, :]).then_inc(stored[u], 16)
                    sp.dma_start(rows(T["h2"], r), h[:, u, :]).then_inc(stored[u], 16)
                    sp.dma_start(rows(T["table2"], r), hs[:, u, :]).then_inc(stored[u], 16)

            load(0)
            run_ahead(sp, NBP // 2, step)
            for u in range(2):
                sp.wait_ge(stored[u], 48 * (NBP // 2))

        @block.gpsimd
        def _(pool):
            def step(i):
                n64 = snap(pool, (i + 1) * 64)
                for u in range(2):
                    pool.wait_ge(x_in[u], n64)
                    pool.sem_inc(turn, 1)
                    pool.indirect_dma_start(gd[:, u, :], None, T["table1"][:, :], bass.IndirectOffsetOnAxis(ap=di[:, u, 0:1], axis=0)).then_inc(g_in[u], 16)
                    pool.indirect_dma_start(gs[:, u, :], None, T["tablel"][:, :], bass.IndirectOffsetOnAxis(ap=si[:, u, 0:1], axis=0)).then_inc(g_in[u], 16)

            repeat(pool, NBP // 2, step)

        @block.scalar
        def _(act):
            def step(i):
                n = snap(act, i + 1)
                for u in range(2):
                    act.wait_ge(z_ready[u], n)
                    act.activation(al[:, u, :], z[:, u, :], ACT.Exp, accum_out=sm[:, u, 0:1]).then_inc(e_ready[u], 1)
                for u in range(2):
                    root(nc, act, mv[:, u, :], K["eps"], var_ready[u], root_ready[u], n)

            repeat(act, NBP // 2, step)

        @block.vector
        def _(dve):
            def step(i):
                n, n32 = snap(dve, i + 1), snap(dve, (i + 1) * 32)
                for u in range(2):
                    dve.wait_ge(g_in[u], n32)
                    dve.tensor_tensor(z[:, u, :], gs[:, u, :], gd[:, u, D + H:WX], ALU.add)
                    dve.drain()
                    dve.scalar_tensor_tensor(out=z[:, u, :], in0=z[:, u, :], scalar=0.01, in1=z[:, u, :], op0=ALU.mult, op1=ALU.max)
                    dve.drain()
                    dve.tensor_reduce(sm[:, u, 1:2], z[:, u, :], AX.X, ALU.max)
                    dve.drain()
                    dve.tensor_scalar(z[:, u, :], z[:, u, :], sm[:, u, 1:2], None, ALU.subtract).then_inc(z_ready[u], 1)
                for u in range(2):
                    dve.wait_ge(e_ready[u], n)
                    dve.reciprocal(sm[:, u, 0:1], sm[:, u, 0:1])
                    dve.drain()
                    dve.tensor_scalar(al[:, u, :], al[:, u, :], sm[:, u, 0:1], None, ALU.mult)
                    dve.drain()
                    dve.tensor_tensor(pr[:, u, :, :], gd[:, u, 0:D].rearrange("p (h d) -> p h d", h=H), al[:, u, :].unsqueeze(2).to_broadcast([P, H, DK]), ALU.mult)
                    dve.drain()
                    dve.tensor_reduce(tm[:, u, :], pr[:, u, :, :].rearrange("p h d -> p d h"), AX.X, ALU.add)
                    dve.drain()
                    at_least(dve, stored[u], snap(dve, i * 48))
                    dve.tensor_tensor(x2[:, u, :].rearrange("p (h d) -> p h d", h=H), x[:, u, :].rearrange("p (h d) -> p h d", h=H),
                                      tm[:, u, :].unsqueeze(1).to_broadcast([P, H, DK]), ALU.add)
                    dve.drain()
                    normalise(nc, dve, x2[:, u, :], st[:, u, :], mv[:, u, :], h[:, u, :], var_ready[u], root_ready[u], n)
                    dve.tensor_scalar(h[:, u, :], h[:, u, :], 0.0, None, ALU.max)
                    dve.drain()
                    dve.tensor_scalar(hs[:, u, :], h[:, u, :], rd[:, u, 0:1], None, ALU.mult)
                    dve.drain().then_inc(out_ready[u], 1)
                    dve.sem_inc(x_used[u], 1)

            repeat(dve, NBP // 2, step)


def sum_items(nc, name, table, agg, T, K):
    with Stage(nc, name) as S:
        W = D + 1
        rec = S.sb("rec", [P, SL, G, 4], I32)
        itf = S.sb("itf", [P, SL, 4])
        row = S.sb("row", [P, SL, G, W])
        dl = S.sb("dl", [P, SL, G])
        oh = S.sb("oh", [P, SL, G, P])
        acc = S.sb("acc", [P, SL, W])
        pA = [S.ps(f"pA{j}", [P, 512]) for j in range(2)]
        many = lambda k: S.sems_of(k, SL)
        in_ready, row_ready, dl_done, oh_ready, a_ps, item_done, stored = (
            many(k) for k in ("in_ready", "row_ready", "dl_done", "oh_ready", "a_ps", "item_done", "stored"))
        consts, turn = S.sem("consts"), S.sem("turn")
        block = S.block()
        KI = NI // SL

        def over_items(eng, step):
            for s in range(SL):
                step(s, 0, s)
            with eng.Fori(1, KI - 1) as k:
                kk = snap(eng, k + 0)
                for s in range(SL):
                    step(s, kk, k * SL + s)
            for s in range(SL):
                step(s, KI - 1, (KI - 1) * SL + s)

        def prv(s, k):
            return ((s - 1) % SL, k - (s == 0))

        def need(eng, sems, s, k, per=1):
            at_least(eng, sems[s], snap(eng, (k + 1) * per))

        @block.sync
        def _(sp):
            def load(s, k, i):
                e0 = sp.value_load(K["items"][0:1, 0, bass.ds(i, 1)], min_val=0, max_val=E)
                need(sp, item_done, s, k - 1)
                sp.sem_inc(turn, 1)
                sp.dma_start(rec[:, s, :, :].rearrange("p g c -> p (g c)"),
                             T["rec"][bass.ds(e0, EW), :].rearrange("(p g) c -> p (g c)", g=G)).then_inc(in_ready[s], 16)
                sp.dma_start(itf[:, s, :], T["itemf"][bass.ds(i, 1), :].to_broadcast([P, 4])).then_inc(in_ready[s], 16)

            for s in range(SL):
                load(s, 0, s)

            def step(s, k, i):
                b0 = sp.value_load(K["items"][0:1, 1, bass.ds(i, 1)], min_val=0, max_val=NB * P)
                ps, pk = prv(s, k)
                mine, before = snap(sp, k + 1), snap(sp, (pk + 1) * 16)
                at_least(sp, item_done[s], mine)
                sp.sem_inc(turn, 1)
                at_least(sp, stored[ps], before)
                sp.sem_inc(turn, 1)
                sp.dma_start(agg[bass.ds(b0, P), :], acc[:, s, :]).then_inc(stored[s], 16)
                if not (isinstance(k, int) and k == KI - 1):
                    load(s, k + 1, i + SL)

            over_items(sp, step)
            sp.wait_ge(stored[SL - 1], 16 * KI)

        @block.gpsimd
        def _(pool):
            pool.memset(row[:, :, :, D:W], 1.0)
            pool.memset(acc[:, SL - 1, :], 0.0)
            pool.drain().then_inc(consts, 1)

            def step(s, k, i):
                need(pool, in_ready, s, k, 32)
                pool.sem_inc(turn, 1)
                for g in range(G):
                    pool.indirect_dma_start(row[:, s, g, 0:D], None, table[:, :],
                                            bass.IndirectOffsetOnAxis(ap=rec[:, s, g, 1:2], axis=0)).then_inc(row_ready[s], 16)

            over_items(pool, step)

        @block.vector
        def _(dve):
            dve.wait_ge(consts, 1)

            def onehots(s, k):
                need(dve, in_ready, s, k, 32)
                recf = rec[:, s, :, :].bitcast(F32)
                dve.tensor_scalar(dl[:, s, :], recf[:, :, 2], itf[:, s, 0:1], None, ALU.subtract).then_inc(dl_done[s], 1)
                need(dve, dl_done, s, k)
                for g in range(G):
                    last = dve.tensor_scalar(oh[:, s, g, :], K["iota"][:, :], dl[:, s, g:g + 1], None, ALU.is_equal)
                last.then_inc(oh_ready[s], 1)

            onehots(0, 0)

            def step(s, k, i):
                ps, pk = prv(s, k)
                if s < SL - 1 or not (isinstance(k, int) and k == KI - 1):
                    onehots((s + 1) % SL, k + (s + 1) // SL)
                need(dve, a_ps, s, k)
                need(dve, item_done, ps, pk)
                need(dve, stored, s, k - 1, 16)
                dve.scalar_tensor_tensor(out=acc[:, s, :], in0=acc[:, ps, :], scalar=itf[:, s, 1:2], in1=pA[s % 2][:, 0:W],
                                         op0=ALU.mult, op1=ALU.add).then_inc(item_done[s], 1)

            over_items(dve, step)

        @block.tensor
        def _(pe):
            pe.wait_ge(consts, 1)

            def step(s, k, i):
                s2, k2 = (s - 2) % SL, k - (s < 2)
                need(pe, oh_ready, s, k)
                need(pe, row_ready, s, k, 16 * G)
                need(pe, item_done, s2, k2)
                for g in range(G):
                    last = pe.matmul(pA[s % 2][:, 0:W], oh[:, s, g, :], row[:, s, g, :], start=(g == 0), stop=(g == G - 1))
                last.then_inc(a_ps[s], 1)

            over_items(pe, step)


def gate(nc, A, T, K):
    with Stage(nc, "gate") as S:
        w = S.sb("w", [P, 4, D])
        bias = S.sb("bias", [1, 2, D])
        wg = S.sb("wg", [P, 2, EX])
        bg = S.sb("bg", [1, EX])
        ag = S.sb("ag", [P, 2, D + 1])
        mh = S.sb("mh", [P, 2, 2, D])
        mk = S.sb("mk", [P, 2, 2 * NT])
        rd = S.sb("rd", [P, 2, 1])
        mT = S.sb("mT", [P, 2, 4, P])
        xx = S.sb("xx", [P, 2, D])
        xT = S.sb("xT", [P, 2, 2, P])
        lg = S.sb("lg", [P, 2, EX])
        v8 = S.sb("v8", [P, 2, 8])
        i8 = S.sb("i8", [P, 2, 8], U32)
        ef = S.sb("ef", [P, 2, 2])
        oh = S.sb("oh", [P, 2, 2, EX])
        m = S.sb("m", [P, 2, EX])
        tot = S.sb("tot", [P, EX])
        pr = S.sb("pr", [P, 2, 2, EX])
        rt = S.sb("rt", [P, 2, 8])
        dv = S.sb("dv", [P, 2, 2])
        pT = S.ps("pT", [P, 4, P])
        pXX = [S.ps(f"pXX{u}", [P, 512]) for u in range(2)]
        pT2 = S.ps("pT2", [P, 4, P])
        pL = [S.ps(f"pL{u}", [P, 512]) for u in range(2)]
        pP = [S.ps(f"pP{u}", [P, 512]) for u in range(2)]
        two = lambda k: S.sems_of(k, 2)
        w_in, turn, bias_ready = S.sem("w_in"), S.sem("turn"), S.sem("bias_ready")
        x_in, x_used, deg_ready, rt_ready, mh_ready, t_ps, mT_ready, xx_ps, xx_ready = (
            two(k) for k in ("x_in", "x_used", "deg_ready", "rt_ready", "mh_ready", "t_ps", "mT_ready", "xx_ps", "xx_ready"))
        t2_ps, xT_ready, l_ps, d_ready, e_ready, m_ready, p_ps, r_ready, stored = (
            two(k) for k in ("t2_ps", "xT_ready", "l_ps", "d_ready", "e_ready", "m_ready", "p_ps", "r_ready", "stored"))
        end_ps = S.sem("end_ps")
        block = S.block()

        @block.sync
        def _(sp):
            sp.dma_start(w[:, 0:2, :], A["L2_gnn_W_gc"].rearrange("(c p) n -> p c n", p=P)).then_inc(w_in, 16)
            sp.dma_start(w[:, 2:4, :], A["L2_gnn_W_res"].rearrange("(c p) n -> p c n", p=P)).then_inc(w_in, 16)
            sp.dma_start(wg[:, :, :], A["L2_gnn_Wg"].rearrange("(c p) n -> p c n", p=P)).then_inc(w_in, 16)
            for j, (t, a) in enumerate(((bias[:, 0, :], "b_gc"), (bias[:, 1, :], "b_res"), (bg[:, :], "bg"))):
                sp.dma_start(t, A[f"L2_gnn_{a}"].rearrange("(o n) -> o n", o=1)).then_inc(w_in, 16)

            def load(i):
                for u in range(2):
                    r = snap(sp, (2 * i + u) * P)
                    at_least(sp, x_used[u], i)
                    sp.sem_inc(turn, 1)
                    sp.dma_start(ag[:, u, :], rows(T["agg2"], r)).then_inc(x_in[u], 16)
                    sp.dma_start(mh[:, u, 1, :], rows(T["h2"], r)).then_inc(x_in[u], 16)
                    sp.dma_start(mk[:, u, :], rows(T["tmask"], r)).then_inc(x_in[u], 16)

            def step(i, more):
                n = snap(sp, i + 1)
                if more:
                    load(n)
                for u in range(2):
                    r = snap(sp, (2 * i + u) * P)
                    sp.wait_ge(r_ready[u], n)
                    sp.sem_inc(turn, 1)
                    sp.dma_start(rows(T["xx"], r), xx[:, u, :]).then_inc(stored[u], 16)
                    sp.dma_start(rows(T["route"], r), rt[:, u, :]).then_inc(stored[u], 16)

            load(0)
            run_ahead(sp, NBP // 2, step)
            for u in range(2):
                sp.wait_ge(stored[u], 32 * (NBP // 2))

        @block.vector
        def _(dve):
            dve.memset(tot[:, :], 0.0)
            dve.wait_ge(w_in, 96)
            dve.tensor_tensor(bias[:, 0, :], bias[:, 0, :], bias[:, 1, :], ALU.add).then_inc(bias_ready, 1)

            def step(i):
                n, n48 = snap(dve, i + 1), snap(dve, (i + 1) * 48)
                for u in range(2):
                    dve.wait_ge(x_in[u], n48)
                    dve.tensor_scalar(rd[:, u, :], ag[:, u, D:D + 1], 1.0, None, ALU.max).then_inc(deg_ready[u], 1)
                for u in range(2):
                    dve.wait_ge(rt_ready[u], n)
                    dve.reciprocal(rd[:, u, :], rd[:, u, :])
                    dve.drain()
                    dve.tensor_scalar(mh[:, u, 0, :], ag[:, u, 0:D], rd[:, u, 0:1], None, ALU.mult).then_inc(mh_ready[u], 1)
                for u in range(2):
                    dve.wait_ge(l_ps[u], n)
                    dve.tensor_copy(lg[:, u, :], pL[u][:, 0:EX])
                    dve.drain()
                    dve.max(v8[:, u, :], lg[:, u, :])
                    dve.drain()
                    dve.max_index(i8[:, u, :], v8[:, u, :], lg[:, u, :])
                    dve.tensor_tensor(dv[:, u, 0:1], v8[:, u, 1:2], v8[:, u, 0:1], ALU.subtract).then_inc(d_ready[u], 1)
                    dve.drain()
                    dve.tensor_copy(ef[:, u, :], i8[:, u, 0:2])
                    dve.tensor_reduce(dv[:, u, 1:2], mk[:, u, 0:NT], AX.X, ALU.add)
                    dve.drain()
                    for k in range(2):
                        dve.tensor_scalar(oh[:, u, k, :], K["iota"][:, 0:EX], ef[:, u, k:k + 1], dv[:, u, 1:2], ALU.is_equal, ALU.mult)
                    dve.drain()
                    dve.tensor_tensor(m[:, u, :], oh[:, u, 0, :], oh[:, u, 1, :], ALU.add).then_inc(m_ready[u], 1)
                    dve.wait_ge(p_ps[u], n)
                    dve.tensor_tensor(tot[:, :], tot[:, :], m[:, u, :], ALU.add)
                    at_least(dve, stored[u], snap(dve, i * 32))
                    dve.tensor_tensor(pr[:, u, :, :], oh[:, u, :, :], pP[u][:, 0:EX].unsqueeze(1).to_broadcast([P, 2, EX]), ALU.mult)
                    dve.drain()
                    dve.tensor_reduce(rt[:, u, 2:4], pr[:, u, :, :], AX.X, ALU.add)
                    dve.tensor_copy(rt[:, u, 0:2], ef[:, u, :])
                    dve.tensor_copy(rt[:, u, 6:7], dv[:, u, 1:2])
                    dve.tensor_copy(rt[:, u, 7:8], dv[:, u, 1:2])
                    dve.wait_ge(e_ready[u], n)
                    dve.tensor_scalar(rt[:, u, 4:5], rt[:, u, 5:6], 1.0, None, ALU.add)
                    dve.drain()
                    dve.reciprocal(rt[:, u, 4:5], rt[:, u, 4:5])
                    dve.drain()
                    dve.tensor_tensor(rt[:, u, 5:6], rt[:, u, 5:6], rt[:, u, 4:5], ALU.mult)
                    dve.drain().then_inc(r_ready[u], 1)
                    dve.sem_inc(x_used[u], 1)

            repeat(dve, NBP // 2, step)
            dve.wait_ge(end_ps, 1)
            dve.tensor_copy(K["count"][:, :], pP[0][0:EX, 0:1])

        @block.scalar
        def _(act):
            def step(i):
                n = snap(act, i + 1)
                for u in range(2):
                    act.wait_ge(deg_ready[u], n)
                    act.activation(rd[:, u, :], rd[:, u, :], ACT.Sqrt).then_inc(rt_ready[u], 1)
                for u in range(2):
                    act.wait_ge(t_ps[u], n)
                    act.activation(mT[:, u, :, :], pT[:, :, :], ACT.Copy).then_inc(mT_ready[u], 1)
                    at_least(act, stored[u], snap(act, i * 32))
                    act.wait_ge(xx_ps[u], n)
                    act.activation(xx[:, u, :], pXX[u][:, 0:D], ACT.Copy).then_inc(xx_ready[u], 1)
                    act.wait_ge(t2_ps[u], n)
                    act.activation(xT[:, u, :, :], pT2[:, 0:2, :], ACT.Copy).then_inc(xT_ready[u], 1)
                for u in range(2):
                    act.wait_ge(d_ready[u], n)
                    act.activation(rt[:, u, 5:6], dv[:, u, 0:1], ACT.Exp).then_inc(e_ready[u], 1)

            repeat(act, NBP // 2, step)

        @block.tensor
        def _(pe):
            pe.wait_ge(w_in, 96)
            pe.wait_ge(bias_ready, 1)

            def step(i):
                n = snap(pe, i + 1)
                for u in range(2):
                    pe.wait_ge(mh_ready[u], n)
                    for c in range(4):
                        last = pe.transpose(pT[:, c, :], mh[:, u, c // 2, (c % 2) * P:(c % 2 + 1) * P], K["ident"][:, :])
                    last.then_inc(t_ps[u], 1)
                    pe.wait_ge(mT_ready[u], n)
                    for c in range(4):
                        pe.matmul(pXX[u][:, 0:D], mT[:, u, c, :], w[:, c, :], start=(c == 0), stop=False)
                    pe.matmul(pXX[u][:, 0:D], K["ones"][0:1, :], bias[:, 0, :], start=False, stop=True).then_inc(xx_ps[u], 1)
                    pe.wait_ge(xx_ready[u], n)
                    for c in range(2):
                        last = pe.transpose(pT2[:, c, :], xx[:, u, c * P:(c + 1) * P], K["ident"][:, :])
                    last.then_inc(t2_ps[u], 1)
                    pe.wait_ge(xT_ready[u], n)
                    for c in range(2):
                        pe.matmul(pL[u][:, 0:EX], xT[:, u, c, :], wg[:, c, :], start=(c == 0), stop=False)
                    pe.matmul(pL[u][:, 0:EX], K["ones"][0:1, :], bg[:, :], start=False, stop=True).then_inc(l_ps[u], 1)
                for u in range(2):
                    pe.wait_ge(m_ready[u], n)
                    pe.sem_inc(turn, 1)
                    pe.matmul(pP[u][:, 0:EX], K["ones"][:, :], tot[:, :], start=True, stop=False)
                    pe.matmul(pP[u][:, 0:EX], K["upper"][:, :], m[:, u, :], start=False, stop=True).then_inc(p_ps[u], 1)

            repeat(pe, NBP // 2, step)
            pe.wait_ge(r_ready[1], NBP // 2)
            pe.matmul(pP[0][0:EX, 0:1], tot[:, :], K["ones"][:, 0:1], start=True, stop=True).then_inc(end_ps, 1)


def slots(nc, A, T, K):
    with Stage(nc, "slot") as S:
        cc = S.sb("cc", [EX, 1])
        s8 = S.sb("s8", [EX, CAP // P])
        nt = S.sb("nt", [EX, 1])
        ts = S.sb("ts", [EX, 2])
        dg = S.sb("dg", [EX, EX])
        ji = S.sb("ji", [EX, NTILE], I32)
        jf = S.sb("jf", [EX, NTILE])
        s8i = S.sb("s8i", [EX, CAP // P], I32)
        pi = S.sb("pi", [P, 1], I32)
        pf = S.sb("pf", [P, 1])
        sr = S.sb("sr", [P, EX])
        tf = S.sb("tf", [1, NTILE])
        rt = S.sb("rt", [P, NBP, 8])
        oh = S.sb("oh", [P, NBP, EX])
        sl = S.sb("sl", [P, NBP, 2])
        ok = S.sb("ok", [P, NBP, 2])
        sli = S.sb("sli", [P, NBP, 2], I32)
        pa = S.ps("pa", [P, 512])
        pb = S.ps("pb", [P, 512])
        pc = S.ps("pc", [P, 512])
        rt_in, iotas, nt_ready, ts_ps, dg_ready, sr_ps, sl_ready, stored = (
            S.sem(k) for k in ("rt_in", "iotas", "nt_ready", "ts_ps", "dg_ready", "sr_ps", "sl_ready", "stored"))
        block = S.block()

        @block.sync
        def _(sp):
            sp.dma_start(rt[:, :, :], T["route"].rearrange("(b p) c -> p b c", p=P)).then_inc(rt_in, 16)
            sp.wait_ge(sl_ready, 1)
            sp.dma_start(T["slot"].rearrange("(b p) c -> p b c", p=P), sli[:, :, :]).then_inc(stored, 16)
            sp.dma_start(T["gates"].rearrange("(b p) c -> p b c", p=P), ok[:, :, :]).then_inc(stored, 16)
            sp.wait_ge(stored, 32)

        @block.gpsimd
        def _(pool):
            pool.iota(s8i[:, :], pattern=[[P, CAP // P]], base=0, channel_multiplier=0)
            pool.iota(ji[:, :], pattern=[[1, NTILE]], base=0, channel_multiplier=0)
            pool.iota(pi[:, :], pattern=[[0, 1]], base=SLOTS, channel_multiplier=1)
            pool.drain().then_inc(iotas, 1)

        @block.tensor
        def _(pe):
            pe.wait_ge(nt_ready, 1)
            pe.matmul(pa[0:EX, 0:1], K["upper"][0:EX, 0:EX], nt[:, :], start=True, stop=True).then_inc(ts_ps, 1)
            pe.wait_ge(dg_ready, 1)
            pe.matmul(pb[:, 0:EX], K["ones"][0:EX, :], dg[:, :], start=True, stop=True)
            pe.matmul(pc[0:1, 0:NTILE], K["ones"][0:EX, 0:1], jf[:, :], start=True, stop=True).then_inc(sr_ps, 1)

        @block.vector
        def _(dve):
            dve.wait_ge(iotas, 1)
            dve.tensor_scalar(cc[:, :], K["count"][:, :], float(CAP), None, ALU.min)
            dve.tensor_copy(s8[:, :], s8i[:, :])
            dve.tensor_copy(jf[:, :], ji[:, :])
            dve.tensor_copy(pf[:, :], pi[:, :])
            dve.drain()
            dve.tensor_scalar(s8[:, :], s8[:, :], cc[:, 0:1], 0.0, ALU.is_lt, ALU.add, accum_out=nt[:, 0:1])
            dve.drain().then_inc(nt_ready, 1)
            dve.wait_ge(ts_ps, 1)
            dve.tensor_copy(ts[:, 0:1], pa[0:EX, 0:1])
            dve.drain()
            dve.tensor_tensor(ts[:, 1:2], ts[:, 0:1], nt[:, :], ALU.add)
            dve.tensor_scalar(dg[:, :], K["ident"][0:EX, 0:EX], ts[:, 0:1], float(P), ALU.mult, ALU.mult)
            dve.drain()
            dve.tensor_scalar(jf[:, :], jf[:, :], ts[:, 1:2], None, ALU.is_ge)
            dve.drain().then_inc(dg_ready, 1)
            dve.wait_ge(sr_ps, 1)
            dve.tensor_copy(sr[:, :], pb[:, 0:EX])
            dve.tensor_scalar(tf[:, :], pc[0:1, 0:NTILE], float(EX - 1), None, ALU.min)
            dve.wait_ge(rt_in, 16)
            dve.drain()
            dve.tensor_copy(K["tiles"][:, :], tf[:, :])
            for k in range(2):
                dve.tensor_tensor(oh[:, :, :], K["iota"][:, 0:EX].unsqueeze(1).to_broadcast([P, NBP, EX]), rt[:, :, k:k + 1].to_broadcast([P, NBP, EX]), ALU.is_equal)
                dve.drain()
                dve.tensor_tensor(oh[:, :, :], oh[:, :, :], sr[:, :].unsqueeze(1).to_broadcast([P, NBP, EX]), ALU.mult)
                dve.drain()
                dve.tensor_reduce(sl[:, :, k], oh[:, :, :], AX.X, ALU.add)
                dve.drain()
            dve.tensor_scalar(ok[:, :, :], rt[:, :, 2:4], float(CAP), None, ALU.is_lt)
            dve.tensor_tensor(sl[:, :, :], sl[:, :, :], rt[:, :, 2:4], ALU.add)
            dve.drain()
            dve.tensor_tensor(ok[:, :, :], ok[:, :, :], rt[:, :, 6:8], ALU.mult)
            dve.tensor_scalar(sl[:, :, :], sl[:, :, :], pf[:, 0:1], None, ALU.subtract)
            dve.drain()
            dve.tensor_tensor(sl[:, :, :], sl[:, :, :], ok[:, :, :], ALU.mult)
            dve.drain()
            dve.tensor_scalar(sl[:, :, :], sl[:, :, :], pf[:, 0:1], None, ALU.add)
            dve.drain()
            dve.tensor_copy(sli[:, :, :], sl[:, :, :])
            dve.tensor_tensor(ok[:, :, :], ok[:, :, :], rt[:, :, 4:6], ALU.mult)
            dve.drain().then_inc(sl_ready, 1)


def dispatch(nc, A, T, K):
    with Stage(nc, "disp") as S:
        x = S.sb("x", [P, 2, D])
        sl = S.sb("sl", [P, 2, 2], I32)
        two = lambda k: S.sems_of(k, 2)
        x_in, sent = two("x_in"), two("sent")
        turn = S.sem("turn")
        block = S.block()

        @block.sync
        def _(sp):
            def step(i):
                for u in range(2):
                    r = snap(sp, (2 * i + u) * P)
                    at_least(sp, sent[u], snap(sp, i * 32))
                    sp.sem_inc(turn, 1)
                    sp.dma_start(x[:, u, :], rows(T["xx"], r)).then_inc(x_in[u], 16)
                    sp.dma_start(sl[:, u, :], rows(T["slot"], r)).then_inc(x_in[u], 16)

            repeat(sp, NBP // 2, step)

        @block.gpsimd
        def _(pool):
            def step(i):
                n32 = snap(pool, (i + 1) * 32)
                for u in range(2):
                    before = snap(pool, i * 32)
                    pool.wait_ge(x_in[u], n32)
                    pool.sem_inc(turn, 1)
                    if u == 1:
                        pool.wait_ge(sent[0], n32)
                        pool.sem_inc(turn, 1)
                    else:
                        at_least(pool, sent[1], before)
                        pool.sem_inc(turn, 1)
                    pool.indirect_dma_start(T["xslot"][:, :], bass.IndirectOffsetOnAxis(ap=sl[:, u, 0:1], axis=0), x[:, u, :], None).then_inc(sent[u], 16)
                    pool.wait_ge(sent[u], snap(pool, i * 32 + 16))
                    pool.sem_inc(turn, 1)
                    pool.indirect_dma_start(T["xslot"][:, :], bass.IndirectOffsetOnAxis(ap=sl[:, u, 1:2], axis=0), x[:, u, :], None).then_inc(sent[u], 16)

            repeat(pool, NBP // 2, step)
            for u in range(2):
                pool.wait_ge(sent[u], 32 * (NBP // 2))


def experts(nc, A, T, K):
    with Stage(nc, "exp") as S:
        HC = HID // P
        U = 4
        w1 = S.sb("w1", [P, U, 2, HID])
        w2 = S.sb("w2", [P, U, HC, D])
        b1 = S.sb("b1", [HC, U, P])
        b2 = S.sb("b2", [P, U, D])
        x = S.sb("x", [P, U, D])
        xT = S.sb("xT", [P, U, 2, P])
        b1T = S.sb("b1T", [P, U, HC])
        h1 = S.sb("h1", [P, U, HC, P])
        y = S.sb("y", [P, U, D])
        zero = S.sb("zero", [P, D])
        pX = [S.ps(f"pX{u}", [P, 4, P]) for u in range(2)]
        pH = [S.ps(f"pH{u}", [P, HC, P]) for u in range(2)]
        pY = [S.ps(f"pY{u}", [P, 512]) for u in range(2)]
        w_in, stored = S.sems_of("w_in", U), S.sems_of("stored", U)
        x_ps, xT_ready, h_ps, h_ready, y_ps, y_ready = (S.sem(k) for k in ("x_ps", "xT_ready", "h_ps", "h_ready", "y_ps", "y_ready"))
        turn, zeroed, dump = S.sem("turn"), S.sem("zeroed"), S.sem("dump")
        block = S.block()

        def need(eng, sem, i, u):
            at_least(eng, sem, snap(eng, i * U + (u + 1)))

        @block.sync
        def _(sp):
            sp.wait_ge(zeroed, 1)
            sp.dma_start(T["yslot"][SLOTS:SLOTS + P, :], zero[:, :]).then_inc(dump, 16)

            def load(i, u):
                e = sp.value_load(K["tiles"][0:1, bass.ds(i * U + u, 1)], min_val=0, max_val=EX - 1)
                need(sp, y_ready, i - 1, u)
                sp.sem_inc(turn, 1)
                sp.dma_start(x[:, u, :], rows(T["xslot"], snap(sp, (i * U + u) * P))).then_inc(w_in[u], 16)
                sp.dma_start(b1[:, u, :], A["L2_gnn_b1"][bass.ds(e, 1), :].rearrange("e (m p) -> (e m) p", p=P)).then_inc(w_in[u], 16)
                sp.dma_start(b2[:, u, :], A["L2_gnn_b2"][bass.ds(e, 1), :].to_broadcast([P, D])).then_inc(w_in[u], 16)
                sp.dma_start(w1[:, u, :, :], A["L2_gnn_w1"][bass.ds(e, 1), :, :].rearrange("e (c p) n -> p (e c) n", p=P)).then_inc(w_in[u], 16)
                sp.dma_start(w2[:, u, :, :], A["L2_gnn_w2"][bass.ds(e, 1), :, :].rearrange("e (c p) n -> p (e c) n", p=P)).then_inc(w_in[u], 16)

            for u in range(U):
                load(0, u)

            def step(i):
                for u in range(U):
                    r = snap(sp, (i * U + u) * P)
                    need(sp, y_ready, i, u)
                    sp.sem_inc(turn, 1)
                    sp.dma_start(rows(T["yslot"], r), y[:, u, :]).then_inc(stored[u], 16)
                    if not (isinstance(i, int) and i == NTILE // U - 1):
                        load(i + 1, u)

            step(0)
            with sp.Fori(1, NTILE // U - 1) as i:
                step(i)
            step(NTILE // U - 1)
            sp.wait_ge(dump, 16)
            for u in range(U):
                sp.wait_ge(stored[u], 16 * (NTILE // U))

        @block.gpsimd
        def _(pool):
            pool.memset(zero[:, :], 0.0).then_inc(zeroed, 1)

        @block.tensor
        def _(pe):
            def turn_rows(i, u):
                pe.wait_ge(w_in[u], snap(pe, (i + 1) * 80))
                need(pe, xT_ready, *((i, u - 2) if u >= 2 else (i - 1, u + U - 2)))
                for c in range(2):
                    pe.transpose(pX[u % 2][:, c, :], x[:, u, c * P:(c + 1) * P], K["ident"][:, :])
                pe.transpose(pX[u % 2][:, 2, 0:HC], b1[:, u, :], K["ident"][0:HC, 0:HC]).then_inc(x_ps, 1)

            def hidden(i, u):
                need(pe, xT_ready, i, u)
                need(pe, h_ready, *((i, u - 2) if u >= 2 else (i - 1, u + U - 2)))
                for m in range(HC):
                    for c in range(2):
                        last = pe.matmul(pH[u % 2][:, m, :], w1[:, u, c, m * P:(m + 1) * P], xT[:, u, c, :], start=(c == 0), stop=(c == 1))
                last.then_inc(h_ps, 1)

            def result(i, u):
                need(pe, h_ready, i, u)
                need(pe, y_ready, *((i, u - 2) if u >= 2 else (i - 1, u + U - 2)))
                for m in range(HC):
                    last = pe.matmul(pY[u % 2][:, 0:D], h1[:, u, m, :], w2[:, u, m, :], start=(m == 0), stop=(m == HC - 1))
                last.then_inc(y_ps, 1)

            def step(i):
                turn_rows(i, 0)
                for u in range(U):
                    if u + 1 < U:
                        turn_rows(i, u + 1)
                    hidden(i, u)
                    if u > 0:
                        result(i, u - 1)
                result(i, U - 1)

            repeat(pe, NTILE // U, step)

        @block.scalar
        def _(act):
            def step(i):
                for u in range(U):
                    need(act, h_ps, i, u)
                    need(act, xT_ready, i, u)
                    need(act, y_ps, i - 1, u)
                    for m in range(HC):
                        last = act.activation(h1[:, u, m, :], pH[u % 2][:, m, :], ACT.Gelu, bias=b1T[:, u, m:m + 1])
                    last.then_inc(h_ready, 1)

            repeat(act, NTILE // U, step)

        @block.vector
        def _(dve):
            def turned(i, u):
                need(dve, x_ps, i, u)
                need(dve, h_ready, i - 1, u)
                dve.tensor_copy(b1T[:, u, :], pX[u % 2][:, 2, 0:HC])
                dve.tensor_copy(xT[:, u, :, :], pX[u % 2][:, 0:2, :]).then_inc(xT_ready, 1)

            def result(i, u):
                at_least(dve, stored[u], snap(dve, i * 16))
                need(dve, y_ps, i, u)
                dve.tensor_tensor(y[:, u, :], pY[u % 2][:, 0:D], b2[:, u, :], ALU.add).then_inc(y_ready, 1)

            def step(i):
                turned(i, 0)
                for u in range(U):
                    if u + 1 < U:
                        turned(i, u + 1)
                    if u > 0:
                        result(i, u - 1)
                result(i, U - 1)

            repeat(dve, NTILE // U, step)


def combine(nc, A, T, K):
    with Stage(nc, "comb") as S:
        Y = S.sb("Y", [P, NBP * D])
        X2 = S.sb("X2", [P, NBP, D])
        SQ = S.sb("SQ", [P, NBP * D])
        x = S.sb("x", [P, 2, D])
        sl = S.sb("sl", [P, 2, 2], I32)
        gt = S.sb("gt", [P, 2, 2])
        ya = S.sb("ya", [P, 2, 2, D])
        tmp = S.sb("tmp", [P, 2, D])
        mk = S.sb("mk", [P, NBP, 2 * NT])
        va = S.sb("va", [P, NBP])
        gb = S.sb("gb", [P, 2, D])
        mean = S.sb("mean", [P, D])
        sd = S.sb("sd", [P, D])
        zero = S.sb("zero", [P, D])
        pM = S.ps("pM", [P, 512])
        two = lambda k: S.sems_of(k, 2)
        x_in, y_in, used = two("x_in"), two("y_in"), two("used")
        turn, c_in, m_ps, sq_ready, v_ps, v_ready, s_ready, out_ready, stored, y_all, zr = (
            S.sem(k) for k in ("turn", "c_in", "m_ps", "sq_ready", "v_ps", "v_ready", "s_ready", "out_ready", "stored", "y_all", "zr"))
        block = S.block()
        Y3 = Y[:, :].rearrange("p (b n) -> p b n", b=NBP)

        @block.sync
        def _(sp):
            for j, a in enumerate(("gamma", "beta")):
                sp.dma_start(gb[:, j, :], A[f"L2_gnn_{a}"].rearrange("(o n) -> o n", o=1).to_broadcast([P, D])).then_inc(c_in, 16)
            sp.dma_start(mk[:, :, :], T["tmask"].rearrange("(b p) c -> p b c", p=P)).then_inc(c_in, 16)
            sp.dma_start(X2[:, :, :], T["x2"].rearrange("(b p) c -> p b c", p=P)).then_inc(c_in, 16)

            def step(i):
                for u in range(2):
                    r = snap(sp, (2 * i + u) * P)
                    at_least(sp, used[u], i)
                    sp.sem_inc(turn, 1)
                    sp.dma_start(x[:, u, :], rows(T["xx"], r)).then_inc(x_in[u], 16)
                    sp.dma_start(sl[:, u, :], rows(T["slot"], r)).then_inc(x_in[u], 16)
                    sp.dma_start(gt[:, u, :], rows(T["gates"], r)).then_inc(x_in[u], 16)

            repeat(sp, NBP // 2, step)
            sp.wait_ge(out_ready, 1)
            sp.dma_start(T["x3"].rearrange("(b p) c -> p b c", p=P), X2[:, :, :]).then_inc(stored, 16)
            sp.wait_ge(stored, 16)

        @block.gpsimd
        def _(pool):
            pool.memset(zero[:, :], 0.0).then_inc(zr, 1)

            def step(i):
                n48 = snap(pool, (i + 1) * 48)
                for u in range(2):
                    pool.wait_ge(x_in[u], n48)
                    pool.sem_inc(turn, 1)
                    for k in range(2):
                        pool.indirect_dma_start(ya[:, u, k, :], None, T["yslot"][:, :], bass.IndirectOffsetOnAxis(ap=sl[:, u, k:k + 1], axis=0)).then_inc(y_in[u], 16)

            repeat(pool, NBP // 2, step)

        @block.vector
        def _(dve):
            def step(i):
                n32 = snap(dve, (i + 1) * 32)
                for u in range(2):
                    dve.wait_ge(y_in[u], n32)
                    dve.scalar_tensor_tensor(out=tmp[:, u, :], in0=ya[:, u, 0, :], scalar=gt[:, u, 0:1], in1=x[:, u, :], op0=ALU.mult, op1=ALU.add)
                    dve.drain()
                    dve.scalar_tensor_tensor(out=Y[:, bass.ds((2 * i + u) * D, D)], in0=ya[:, u, 1, :], scalar=gt[:, u, 1:2], in1=tmp[:, u, :], op0=ALU.mult, op1=ALU.add)
                    dve.drain().then_inc(used[u], 1)

            repeat(dve, NBP // 2, step)
            dve.wait_ge(c_in, 64)
            dve.tensor_reduce(va[:, :], mk[:, :, 0:NT], AX.X, ALU.add)
            dve.drain()
            valid = va[:, :].unsqueeze(2).to_broadcast([P, NBP, D])
            dve.tensor_tensor(Y3, Y3, valid, ALU.mult)
            dve.drain().then_inc(y_all, 1)
            dve.wait_ge(m_ps, 1)
            dve.tensor_scalar(mean[:, :], pM[:, 0:D], 1.0 / N, None, ALU.mult)
            dve.drain()
            dve.tensor_tensor(Y3, Y3, mean[:, :].unsqueeze(1).to_broadcast([P, NBP, D]), ALU.subtract)
            dve.drain()
            dve.tensor_tensor(Y3, Y3, valid, ALU.mult)
            dve.drain()
            dve.tensor_tensor(SQ[:, :], Y[:, :], Y[:, :], ALU.mult)
            dve.drain().then_inc(sq_ready, 1)
            dve.wait_ge(v_ps, 1)
            dve.tensor_scalar(sd[:, :], pM[:, 0:D], 1.0 / N, EPS, ALU.mult, ALU.add).then_inc(v_ready, 1)
            dve.wait_ge(s_ready, 1)
            dve.reciprocal(sd[:, :], sd[:, :])
            dve.drain()
            dve.tensor_tensor(sd[:, :], sd[:, :], gb[:, 0, :], ALU.mult)
            dve.drain()
            dve.tensor_tensor(Y3, Y3, sd[:, :].unsqueeze(1).to_broadcast([P, NBP, D]), ALU.mult)
            dve.tensor_tensor(X2[:, :, :], X2[:, :, :], gb[:, 1, :].unsqueeze(1).to_broadcast([P, NBP, D]), ALU.add)
            dve.drain()
            dve.tensor_tensor(X2[:, :, :], X2[:, :, :], Y3, ALU.add)
            dve.drain().then_inc(out_ready, 1)

        @block.tensor
        def _(pe):
            pe.wait_ge(zr, 1)
            for go, t, done in ((y_all, Y, m_ps), (sq_ready, SQ, v_ps)):
                pe.wait_ge(go, 1)
                pe.matmul(pM[:, 0:D], K["ones"][:, :], zero[:, :], start=True, stop=False)
                with pe.Fori(0, NBP) as b:
                    pe.matmul(pM[:, 0:D], K["ones"][:, :], t[:, bass.ds(b * D, D)], start=False, stop=False)
                pe.matmul(pM[:, 0:D], K["ones"][:, :], zero[:, :], start=False, stop=True).then_inc(done, 1)

        @block.scalar
        def _(act):
            act.wait_ge(v_ready, 1)
            act.activation(sd[:, :], sd[:, :], ACT.Sqrt).then_inc(s_ready, 1)


def layer3_nodes(nc, A, T, K):
    with Stage(nc, "l3n") as S:
        w = S.sb("w", [P, 2, 3, D])
        b = S.sb("b", [1, 3, D])
        qe = S.sb("qe", [P, D])
        rel = S.sb("rel", [R64, DK])
        relr = S.sb("relr", [R64, DK])
        rel3 = S.sb("rel3", [R64, 3, DK], BF16)
        q3 = S.sb("q3", [P, 2, 3, D], BF16)
        qr = S.sb("qr", [P, 2, D])
        x = S.sb("x", [P, 2, D])
        st = S.sb("st", [P, 2, 6])
        mv = S.sb("mv", [P, 2, 4])
        h = S.sb("h", [P, 2, D])
        en = S.sb("en", [P, 2, D])
        eT = S.sb("eT", [P, 2, 2, P])
        qs = S.sb("qs", [P, 2, D])
        kv = S.sb("kv", [P, 2, 2, D])
        pE = [S.ps(f"pE{u}", [P, 4, P]) for u in range(2)]
        pQ = [S.ps(f"pQ{u}", [P, 512]) for u in range(2)]
        pK = [S.ps(f"pK{u}", [P, 512]) for u in range(2)]
        two = lambda k: S.sems_of(k, 2)
        q_split = two("q_split")
        w_in, rel_in, rel_ready, rel_out, turn = (S.sem(k) for k in ("w_in", "rel_in", "rel_ready", "rel_out", "turn"))
        x_in, var_ready, root_ready, h_done, en_ready, e_ps, eT_ready, q_ps, kv_ready, stored = (
            two(k) for k in ("x_in", "var_ready", "root_ready", "h_done", "en_ready", "e_ps", "eT_ready", "q_ps", "kv_ready", "stored"))
        block = S.block()

        @block.sync
        def _(sp):
            for j, a in enumerate("qkv"):
                sp.dma_start(w[:, :, j, :], A[f"L3_gnn_W{a}"].rearrange("(c p) n -> p c n", p=P)).then_inc(w_in, 16)
                sp.dma_start(b[:, j, :], A[f"L3_gnn_b{a}"].rearrange("(o n) -> o n", o=1)).then_inc(w_in, 16)
            sp.dma_start(qe[:, :], A["L3_gnn_query_emb"].rearrange("(o n) -> o n", o=1).to_broadcast([P, D])).then_inc(w_in, 16)
            sp.dma_start(rel[:, :], A["L3_gnn_rel_w"][:, :]).then_inc(rel_in, 16)

            def load(i):
                for u in range(2):
                    r = snap(sp, (2 * i + u) * P)
                    at_least(sp, en_ready[u], i)
                    sp.sem_inc(turn, 1)
                    sp.dma_start(x[:, u, :], rows(T["x3"], r)).then_inc(x_in[u], 16)

            def step(i, more):
                n = snap(sp, i + 1)
                if more:
                    load(n)
                for u in range(2):
                    r = snap(sp, (2 * i + u) * P)
                    sp.wait_ge(kv_ready[u], n)
                    sp.sem_inc(turn, 1)
                    sp.wait_ge(q_split[u], n)
                    sp.sem_inc(turn, 1)
                    sp.dma_start(rows(T["q3"], r), q3[:, u, :, :].rearrange("p j n -> p (j n)")).then_inc(stored[u], 16)
                    sp.dma_start(rows(T["table3"], r), kv[:, u, :, :].rearrange("p k n -> p (k n)")).then_inc(stored[u], 16)
                    sp.dma_start(rows(T["h3"], r), h[:, u, :]).then_inc(stored[u], 16)

            load(0)
            run_ahead(sp, NBP // 2, step)
            sp.wait_ge(rel_ready, 1)
            sp.dma_start(T["rel"][:, :], rel3[:, :, :].rearrange("p j d -> p (j d)")).then_inc(rel_out, 16)
            sp.wait_ge(rel_out, 16)
            for u in range(2):
                sp.wait_ge(stored[u], 48 * (NBP // 2))

        @block.vector
        def _(dve):
            dve.wait_ge(w_in, 16 * 7)
            dve.tensor_scalar(qe[:, :], qe[:, :], 0.1, None, ALU.mult)
            dve.wait_ge(rel_in, 16)
            dve.tensor_scalar(rel[:, :], rel[:, :], 0.2, None, ALU.mult)
            dve.drain()
            split3(dve, [rel3[:, j, :] for j in range(3)], relr[:, :], rel[:, :])
            dve.drain().then_inc(rel_ready, 1)

            def step(i):
                n, n16 = snap(dve, i + 1), snap(dve, (i + 1) * 16)
                for u in range(2):
                    dve.wait_ge(x_in[u], n16)
                    dve.sem_inc(turn, 1)
                    at_least(dve, stored[u], snap(dve, i * 48))
                    normalise(nc, dve, x[:, u, :], st[:, u, :], mv[:, u, :], h[:, u, :], var_ready[u], root_ready[u], n)
                    dve.tensor_scalar(h[:, u, :], h[:, u, :], 0.0, None, ALU.max)
                    dve.drain()
                    dve.tensor_tensor(en[:, u, :], h[:, u, :], qe[:, :], ALU.add).then_inc(en_ready[u], 1)
                for u in range(2):
                    dve.wait_ge(kv_ready[u], n)
                    split3(dve, [q3[:, u, j, :] for j in range(3)], qr[:, u, :], qs[:, u, :])
                    dve.drain().then_inc(q_split[u], 1)

            repeat(dve, NBP // 2, step)

        @block.tensor
        def _(pe):
            pe.wait_ge(w_in, 16 * 7)

            def step(i):
                n = snap(pe, i + 1)
                for u in range(2):
                    pe.wait_ge(en_ready[u], n)
                    for c in range(2):
                        last = pe.transpose(pE[u][:, c, :], en[:, u, c * P:(c + 1) * P], K["ident"][:, :])
                    last.then_inc(e_ps[u], 1)
                for u in range(2):
                    pe.wait_ge(eT_ready[u], n)
                    for out, rhs, bias in ((pQ[u][:, 0:D], lambda c: w[:, c, 0, :], b[:, 0, :]),
                                           (pK[u][:, :], lambda c: w[:, c, 1:3, :].rearrange("p k n -> p (k n)"), b[:, 1:3, :].rearrange("p k n -> p (k n)"))):
                        for c in range(2):
                            pe.matmul(out, eT[:, u, c, :], rhs(c), start=(c == 0), stop=False)
                        last = pe.matmul(out, K["ones"][0:1, :], bias, start=False, stop=True)
                    last.then_inc(q_ps[u], 1)

            repeat(pe, NBP // 2, step)

        @block.scalar
        def _(act):
            def step(i):
                n = snap(act, i + 1)
                for u in range(2):
                    root(nc, act, mv[:, u, :], K["eps"], var_ready[u], root_ready[u], n)
                    act.wait_ge(e_ps[u], n)
                    act.activation(eT[:, u, :, :], pE[u][:, 0:2, :], ACT.Copy).then_inc(eT_ready[u], 1)
                for u in range(2):
                    at_least(act, stored[u], snap(act, i * 48))
                    act.wait_ge(q_ps[u], n)
                    act.activation(qs[:, u, :], pQ[u][:, 0:D], ACT.Copy, scale=DK ** -0.5)
                    act.activation(kv[:, u, :, :].rearrange("p k n -> p (k n)"), pK[u][:, :], ACT.Copy).then_inc(kv_ready[u], 1)

            repeat(act, NBP // 2, step)


def output(nc, A, T, K, out):
    with Stage(nc, "fin") as S:
        U = 4
        w = S.sb("w", [P, 2, D])
        bo = S.sb("bo", [1, D])
        gb = S.sb("gb", [P, 2, D])
        ag = S.sb("ag", [P, U, H, HV])
        v = S.sb("v", [P, U, D])
        h = S.sb("h", [P, U, D])
        x = S.sb("x", [P, U, D])
        rd = S.sb("rd", [P, U, 2, H])
        a = S.sb("a", [P, U, D])
        b = S.sb("b", [P, U, D])
        aT = S.sb("aT", [P, U, 2, P])
        xo = S.sb("xo", [P, U, D])
        st = S.sb("st", [P, U, 6])
        mv = S.sb("mv", [P, U, 4])
        y = S.sb("y", [P, U, D])
        pA = [S.ps(f"pA{u}", [P, 4, P]) for u in range(U)]
        pO = [S.ps(f"pO{u}", [P, 512]) for u in range(U)]
        of_slots = lambda k: S.sems_of(k, U)
        w_in, turn = S.sem("w_in"), S.sem("turn")
        x_in, a_ready, a_ps, aT_ready, o_ps, var_ready, root_ready, y_ready, stored = (
            of_slots(k) for k in ("x_in", "a_ready", "a_ps", "aT_ready", "o_ps", "var_ready", "root_ready", "y_ready", "stored"))
        FULL = N // P
        block = S.block()

        def over_blocks(eng, step):
            repeat(eng, FULL // U, lambda i: step(i, range(U)))
            step(FULL // U, range(1))

        @block.sync
        def _(sp):
            sp.dma_start(w[:, :, :], A["L3_gnn_Wo"].rearrange("(c p) n -> p c n", p=P)).then_inc(w_in, 16)
            sp.dma_start(bo[:, :], A["L3_gnn_bo"].rearrange("(o n) -> o n", o=1)).then_inc(w_in, 16)
            for j, g in enumerate(("gamma", "beta")):
                sp.dma_start(gb[:, j, :], A[f"L3_gnn_{g}"].rearrange("(o n) -> o n", o=1).to_broadcast([P, D])).then_inc(w_in, 16)

            def step(i, us):
                n = snap(sp, i + 1)
                for u in us:
                    r = snap(sp, (U * i + u) * P)
                    at_least(sp, y_ready[u], i)
                    sp.sem_inc(turn, 1)
                    sp.dma_start(ag[:, u, :, :].rearrange("p h c -> p (h c)"), rows(T["agg3"], r)).then_inc(x_in[u], 16)
                    sp.dma_start(v[:, u, :], T["table3"][bass.ds(r, P), D:2 * D]).then_inc(x_in[u], 16)
                    sp.dma_start(h[:, u, :], rows(T["h3"], r)).then_inc(x_in[u], 16)
                    sp.dma_start(x[:, u, :], rows(T["x3"], r)).then_inc(x_in[u], 16)
                for u in us:
                    r = snap(sp, (U * i + u) * P)
                    sp.wait_ge(y_ready[u], n)
                    sp.sem_inc(turn, 1)
                    m = N - FULL * P if isinstance(i, int) and i == FULL // U else P
                    sp.dma_start(out[bass.ds(r, m), :], y[0:m, u, :]).then_inc(stored[u], 16)

            over_blocks(sp, step)
            sp.wait_ge(stored[0], 16 * (FULL // U + 1))
            for u in range(1, U):
                sp.wait_ge(stored[u], 16 * (FULL // U))

        @block.vector
        def _(dve):
            dve.wait_ge(w_in, 64)

            def heads(t, u):
                return t[:, u, :].rearrange("p (h d) -> p h d", h=H)

            def step(i, us):
                n, n64 = snap(dve, i + 1), snap(dve, (i + 1) * 64)
                for u in us:
                    dve.wait_ge(x_in[u], n64)
                    dve.tensor_scalar(rd[:, u, 0, :], ag[:, u, :, DK], 1e-30, None, ALU.max)
                    dve.tensor_scalar(rd[:, u, 1, :], ag[:, u, :, DK], 0.0, None, ALU.is_equal)
                    dve.drain()
                    dve.reciprocal(rd[:, u, 0, :], rd[:, u, 0, :])
                    dve.tensor_tensor(heads(b, u), heads(v, u), rd[:, u, 1, :].unsqueeze(2).to_broadcast([P, H, DK]), ALU.mult)
                    dve.drain()
                    dve.tensor_tensor(heads(a, u), ag[:, u, :, 0:DK], rd[:, u, 0, :].unsqueeze(2).to_broadcast([P, H, DK]), ALU.mult)
                    dve.drain()
                    dve.tensor_tensor(a[:, u, :], a[:, u, :], b[:, u, :], ALU.add).then_inc(a_ready[u], 1)
                for u in us:
                    dve.wait_ge(o_ps[u], n)
                    dve.tensor_tensor(xo[:, u, :], h[:, u, :], pO[u][:, 0:D], ALU.add)
                    dve.drain()
                    normalise(nc, dve, xo[:, u, :], st[:, u, :], mv[:, u, :], xo[:, u, :], var_ready[u], root_ready[u], n)
                    dve.tensor_tensor(xo[:, u, :], xo[:, u, :], gb[:, 0, :], ALU.mult)
                    dve.tensor_tensor(x[:, u, :], x[:, u, :], gb[:, 1, :], ALU.add)
                    dve.drain()
                    at_least(dve, stored[u], snap(dve, i * 16))
                    dve.tensor_tensor(y[:, u, :], xo[:, u, :], x[:, u, :], ALU.add).then_inc(y_ready[u], 1)

            over_blocks(dve, step)

        @block.tensor
        def _(pe):
            pe.wait_ge(w_in, 64)

            def step(i, us):
                n = snap(pe, i + 1)
                for u in us:
                    pe.wait_ge(a_ready[u], n)
                    for c in range(2):
                        last = pe.transpose(pA[u][:, c, :], a[:, u, c * P:(c + 1) * P], K["ident"][:, :])
                    last.then_inc(a_ps[u], 1)
                for u in us:
                    pe.wait_ge(aT_ready[u], n)
                    for c in range(2):
                        pe.matmul(pO[u][:, 0:D], aT[:, u, c, :], w[:, c, :], start=(c == 0), stop=False)
                    pe.matmul(pO[u][:, 0:D], K["ones"][0:1, :], bo[:, :], start=False, stop=True).then_inc(o_ps[u], 1)

            over_blocks(pe, step)

        @block.scalar
        def _(act):
            def step(i, us):
                n = snap(act, i + 1)
                for u in us:
                    act.wait_ge(a_ps[u], n)
                    act.activation(aT[:, u, :, :], pA[u][:, 0:2, :], ACT.Copy).then_inc(aT_ready[u], 1)
                for u in us:
                    root(nc, act, mv[:, u, :], K["eps"], var_ready[u], root_ready[u], n)

            over_blocks(act, step)


SCRATCH = {"x0": ([NP, D], F32), "rec": ([EP, 4], I32), "tmask": ([NP, 2 * NT], F32), "itemf": ([NI, 4], F32), "rdego": ([NP, 1], F32),
           "q0": ([NP, 3 * D], BF16), "table0": ([NP * R8, 2 * D], F32), "agg0": ([NP, H * HV], F32),
           "x1": ([NP, D], F32), "table1": ([NP, D + 2 * H], F32), "tablel": ([NP, H], F32),
           "x2": ([NP, D], F32), "h2": ([NP, D], F32), "table2": ([NP, D], F32), "agg2": ([NP, D + 1], F32),
           "xx": ([NP, D], F32), "route": ([NP, 8], F32), "slot": ([NP, 2], I32), "gates": ([NP, 2], F32),
           "xslot": ([SLOTS + P, D], F32), "yslot": ([SLOTS + P, D], F32), "x3": ([NP, D], F32), "h3": ([NP, D], F32),
           "q3": ([NP, 3 * D], BF16), "table3": ([NP, 2 * D], F32), "rel": ([R64, 3 * DK], BF16), "agg3": ([NP, H * HV], F32)}
DEBUG = False


def build(nc, A, out):
    ctx = ExitStack()
    with ctx:
        T = {k: nc.dram_tensor(f"t_{k}", s, d, **({"kind": "ExternalOutput"} if DEBUG else {})).ap() for k, (s, d) in SCRATCH.items()}
        sb = lambda name, shape, dt=F32: ctx.enter_context(nc.sbuf_tensor(f"k_{name}", shape, dt))
        K = {"ident": sb("ident", [P, P]), "ones": sb("ones", [P, P]), "upper": sb("upper", [P, P]), "iota": sb("iota", [P, P]),
             "iotab": sb("iotab", [P, P], BF16), "identb": sb("identb", [P, P], BF16),
             "eps": sb("eps", [P, 1]), "items": sb("items", [1, 2, NI], I32),
             "count": sb("count", [EX, 1]), "tiles": sb("tiles", [1, NTILE], I32)}
        prepare(nc, A, T, K)
        layer0_nodes(nc, A, T, K)
        attention_items(nc, "l0e", T["table0"], 0, T["q0"], T["agg0"], T, K)
        layer1_nodes(nc, A, T, K)
        layer2_nodes(nc, A, T, K)
        sum_items(nc, "l2e", T["table2"], T["agg2"], T, K)
        gate(nc, A, T, K)
        slots(nc, A, T, K)
        dispatch(nc, A, T, K)
        experts(nc, A, T, K)
        combine(nc, A, T, K)
        layer3_nodes(nc, A, T, K)
        attention_items(nc, "l3e", T["table3"], 1, T["q3"], T["agg3"], T, K, rel=T["rel"])
        output(nc, A, T, K, out)


def kernel(**inputs):
    import numpy as _np
    import concourse.bacc as _bacc
    from concourse import mybir as _mybir
    from concourse.bass_utils import run_bass_kernel_spmd as _run

    nc = _bacc.Bacc("TRN2", target_bir_lowering=False, num_devices=1)
    arrays, args = {}, {}
    for name, a in inputs.items():
        a = _np.ascontiguousarray(a)
        arrays[f"in_{name}"] = a
        args[name] = nc.dram_tensor(f"in_{name}", a.shape, _mybir.dt.from_np(a.dtype), kind="ExternalInput").ap()
    out = nc.dram_tensor("out_x", (N, D), _mybir.dt.float32, kind="ExternalOutput").ap()
    build(nc, args, out)
    r = _run(nc, [arrays], core_ids=[0])
    return r.results[0]["out_x"]
```
